# Optimizing a Trainium2 kernel written in Bass

```python
import numpy as np
import jax
import jax.numpy as jnp

def _softmax(x, axis=-1):
    return jax.nn.softmax(x, axis=axis)

def _gelu(x):
    return jax.nn.gelu(x, approximate=True)

def _silu(x):
    return jax.nn.silu(x)

def _sigmoid(x):
    return jax.nn.sigmoid(x)

def _layernorm(x, axis=-1, eps=1e-05):
    m = jnp.mean(x, axis=axis, keepdims=True)
    v = jnp.var(x, axis=axis, keepdims=True)
    return (x - m) / jnp.sqrt(v + eps)

def _scatter_add(tgt, idx, src, axis=0):
    return tgt.at[idx].add(src)

def _segment_sum(src, seg, n):
    return jax.ops.segment_sum(src, seg, n)
kernel_name = 'mk_adaln_ffn_d2_seqx_r4_6e709a'

def setup_inputs(seed: int=0):
    np.random.seed(seed)
    _w = jnp.asarray

    def _rec_inputs():
        import jax
        import jax.numpy as jnp
        _rk = jax.random.key(seed)
        x = -0.000125 + 0.9999 * jax.random.normal(jax.random.fold_in(_rk, 1), (4, 512, 512), jnp.float32)
        _lenS = 512 - jax.random.randint(jax.random.fold_in(_rk, 7), (4,), 0, max(1, 512 // 4) + 1, jnp.int32)
        _lenS2 = 512 - jax.random.randint(jax.random.fold_in(_rk, 8), (4,), 0, max(1, 512 // 4) + 1, jnp.int32)
        fside_BxSxS_0 = -1.52775e-05 + 0.999936 * jax.random.normal(jax.random.fold_in(_rk, 11), (4, 512, 512), jnp.float32)
        cond_512 = -5.03954e-05 + 1.00559 * jax.random.normal(jax.random.fold_in(_rk, 12), (4, 128), jnp.float32)
        return (x, fside_BxSxS_0, cond_512)
    x, fside_BxSxS_0, cond_512 = _rec_inputs()

    def _L0_cond_setup():
        import jax, jax.numpy as jnp
        from jax import lax
        import numpy as np
        B, T, C, TD = (8, 512, 512, 128)

        def _bi_wkv(r, k, v, w, u, time_emb):
            tf = jax.nn.sigmoid(jnp.sum(time_emb, axis=-1))[:, None, None]
            decay = jnp.exp(-jnp.exp(w.astype(jnp.float32)))[None, :] * (0.5 + 0.5 * tf[:, :, 0])
            kf = k.astype(jnp.float32)
            vf = v.astype(jnp.float32)
            ek = jnp.exp(jnp.minimum(kf, 30.0))
            ekv = ek * vf

            def step(carry, x):
                a, b = carry
                ekv_t, ek_t = x
                a = a * decay + ekv_t
                b = b * decay + ek_t
                return ((a, b), (a, b))
            ekv_t = jnp.swapaxes(ekv, 0, 1)
            ek_t = jnp.swapaxes(ek, 0, 1)
            init = (jnp.zeros_like(decay), jnp.zeros_like(decay))
            _, (nf, df) = lax.scan(step, init, (ekv_t, ek_t))
            _, (nb, db) = lax.scan(step, init, (ekv_t, ek_t), reverse=True)
            nf = jnp.swapaxes(nf, 0, 1)
            df = jnp.swapaxes(df, 0, 1)
            nb = jnp.swapaxes(nb, 0, 1)
            db = jnp.swapaxes(db, 0, 1)
            euk = jnp.exp(jnp.minimum(u.astype(jnp.float32)[None, None, :] + kf, 30.0))
            num = nf + nb - ekv + euk * vf
            den = df + db - ek + euk
            base = jax.nn.sigmoid(r.astype(jnp.float32)) * (num / jnp.maximum(den, 1e-08))
            out = base * (0.8 + 0.2 * tf)
            return out.astype(r.dtype)
        key = jax.random.key(seed)
        ks = jax.random.split(key, 6)
        return {'r': jax.random.normal(ks[0], (B, T, C), dtype=jnp.float32), 'k': jax.random.normal(ks[1], (B, T, C), dtype=jnp.float32), 'v': jax.random.normal(ks[2], (B, T, C), dtype=jnp.float32), 'w': jax.random.normal(ks[3], (C,), dtype=jnp.float32), 'u': jax.random.normal(ks[4], (C,), dtype=jnp.float32), 'time_emb': jax.random.normal(ks[5], (B, TD), dtype=jnp.float32)}
    _L0_cond_all = _L0_cond_setup()
    _L0_cond_in = {k: v for k, v in _L0_cond_all.items() if k in ('w', 'u')}
    del _L0_cond_all

    def _L0_ffn_setup():
        import jax, jax.numpy as jnp
        import numpy as np
        SEQ, BS, D, F, E = (256, 2, 512, 512, 8)
        key = jax.random.key(seed)
        ks = jax.random.split(key, 8)
        s = 0.02
        return {'hidden_states': jax.random.normal(ks[0], (SEQ, BS, D), jnp.float32), 'router_w': jax.random.normal(ks[1], (D, E), jnp.float32) * s, 'gate_w': jax.random.normal(ks[2], (E, D, F), jnp.float32) * s, 'up_w': jax.random.normal(ks[3], (E, D, F), jnp.float32) * s, 'down_w': jax.random.normal(ks[4], (E, F, D), jnp.float32) * s, 'shared_gate_w': jax.random.normal(ks[5], (D, F), jnp.float32) * s, 'shared_up_w': jax.random.normal(ks[6], (D, F), jnp.float32) * s, 'shared_down_w': jax.random.normal(ks[7], (F, D), jnp.float32) * s}
    _L0_ffn_all = _L0_ffn_setup()
    _L0_ffn_in = {k: v for k, v in _L0_ffn_all.items() if k in ('router_w', 'gate_w', 'up_w', 'down_w', 'shared_gate_w', 'shared_up_w', 'shared_down_w')}
    del _L0_ffn_all

    def _L1_cond_setup():
        import jax, jax.numpy as jnp
        from jax import lax
        import numpy as np
        B, T, C, TD = (8, 512, 512, 128)

        def _bi_wkv(r, k, v, w, u, time_emb):
            tf = jax.nn.sigmoid(jnp.sum(time_emb, axis=-1))[:, None, None]
            decay = jnp.exp(-jnp.exp(w.astype(jnp.float32)))[None, :] * (0.5 + 0.5 * tf[:, :, 0])
            kf = k.astype(jnp.float32)
            vf = v.astype(jnp.float32)
            ek = jnp.exp(jnp.minimum(kf, 30.0))
            ekv = ek * vf

            def step(carry, x):
                a, b = carry
                ekv_t, ek_t = x
                a = a * decay + ekv_t
                b = b * decay + ek_t
                return ((a, b), (a, b))
            ekv_t = jnp.swapaxes(ekv, 0, 1)
            ek_t = jnp.swapaxes(ek, 0, 1)
            init = (jnp.zeros_like(decay), jnp.zeros_like(decay))
            _, (nf, df) = lax.scan(step, init, (ekv_t, ek_t))
            _, (nb, db) = lax.scan(step, init, (ekv_t, ek_t), reverse=True)
            nf = jnp.swapaxes(nf, 0, 1)
            df = jnp.swapaxes(df, 0, 1)
            nb = jnp.swapaxes(nb, 0, 1)
            db = jnp.swapaxes(db, 0, 1)
            euk = jnp.exp(jnp.minimum(u.astype(jnp.float32)[None, None, :] + kf, 30.0))
            num = nf + nb - ekv + euk * vf
            den = df + db - ek + euk
            base = jax.nn.sigmoid(r.astype(jnp.float32)) * (num / jnp.maximum(den, 1e-08))
            out = base * (0.8 + 0.2 * tf)
            return out.astype(r.dtype)
        key = jax.random.key(seed)
        ks = jax.random.split(key, 6)
        return {'r': jax.random.normal(ks[0], (B, T, C), dtype=jnp.float32), 'k': jax.random.normal(ks[1], (B, T, C), dtype=jnp.float32), 'v': jax.random.normal(ks[2], (B, T, C), dtype=jnp.float32), 'w': jax.random.normal(ks[3], (C,), dtype=jnp.float32), 'u': jax.random.normal(ks[4], (C,), dtype=jnp.float32), 'time_emb': jax.random.normal(ks[5], (B, TD), dtype=jnp.float32)}
    _L1_cond_all = _L1_cond_setup()
    _L1_cond_in = {k: v for k, v in _L1_cond_all.items() if k in ('w', 'u')}
    del _L1_cond_all

    def _L1_ffn_setup():
        import jax, jax.numpy as jnp
        import numpy as np
        EPS = 1e-05

        def _bitlinear(x, w):
            rms = jax.lax.rsqrt(jnp.maximum(jnp.mean(w * w), EPS))
            w_quant = jnp.clip(jnp.round(w * rms), -1.0, 1.0) / rms
            w_quant = jax.lax.stop_gradient(w_quant - w) + w
            scale = 127.0 / jnp.maximum(jnp.max(jnp.abs(x), axis=-1, keepdims=True), EPS)
            x_quant = jnp.clip(jnp.round(x * scale), -128.0, 127.0) / scale
            x_quant = jax.lax.stop_gradient(x_quant - x) + x
            return jnp.einsum('bsd,fd->bsf', x_quant, w_quant)
        key = jax.random.key(seed)
        k1, k2, k3 = jax.random.split(key, 3)
        n_embd, d_ff = (512, 2048)
        B, S = (4, 512)
        x = jax.random.normal(k1, (B, S, n_embd), dtype=jnp.float32)
        w1 = jax.random.normal(k2, (d_ff, n_embd), dtype=jnp.float32) * 0.02
        w2 = jax.random.normal(k3, (n_embd, d_ff), dtype=jnp.float32) * 0.02
        return {'x': x, 'w1': w1, 'w2': w2}
    _L1_ffn_all = _L1_ffn_setup()
    _L1_ffn_in = {k: v for k, v in _L1_ffn_all.items() if k in ('w1', 'w2')}
    del _L1_ffn_all
    return {'x': x, 'fside_BxSxS_0': fside_BxSxS_0, 'cond_512': cond_512, 'L0_cond_w': _L0_cond_in['w'], 'L0_cond_u': _L0_cond_in['u'], 'L0_ffn_router_w': _L0_ffn_in['router_w'], 'L0_ffn_gate_w': _L0_ffn_in['gate_w'], 'L0_ffn_up_w': _L0_ffn_in['up_w'], 'L0_ffn_down_w': _L0_ffn_in['down_w'], 'L0_ffn_shared_gate_w': _L0_ffn_in['shared_gate_w'], 'L0_ffn_shared_up_w': _L0_ffn_in['shared_up_w'], 'L0_ffn_shared_down_w': _L0_ffn_in['shared_down_w'], 'L1_cond_w': _L1_cond_in['w'], 'L1_cond_u': _L1_cond_in['u'], 'L1_ffn_w1': _L1_ffn_in['w1'], 'L1_ffn_w2': _L1_ffn_in['w2']}

def reference(x, fside_BxSxS_0, cond_512, L0_cond_w, L0_cond_u, L0_ffn_router_w, L0_ffn_gate_w, L0_ffn_up_w, L0_ffn_down_w, L0_ffn_shared_gate_w, L0_ffn_shared_up_w, L0_ffn_shared_down_w, L1_cond_w, L1_cond_u, L1_ffn_w1, L1_ffn_w2):
    import jax
    import jax.numpy as jnp

    def _L0_cond_ref(r, k, v, w, u, time_emb):
        import jax, jax.numpy as jnp
        from jax import lax
        import numpy as np
        B, T, C, TD = (8, 512, 512, 128)

        def _bi_wkv(r, k, v, w, u, time_emb):
            tf = jax.nn.sigmoid(jnp.sum(time_emb, axis=-1))[:, None, None]
            decay = jnp.exp(-jnp.exp(w.astype(jnp.float32)))[None, :] * (0.5 + 0.5 * tf[:, :, 0])
            kf = k.astype(jnp.float32)
            vf = v.astype(jnp.float32)
            ek = jnp.exp(jnp.minimum(kf, 30.0))
            ekv = ek * vf

            def step(carry, x):
                a, b = carry
                ekv_t, ek_t = x
                a = a * decay + ekv_t
                b = b * decay + ek_t
                return ((a, b), (a, b))
            ekv_t = jnp.swapaxes(ekv, 0, 1)
            ek_t = jnp.swapaxes(ek, 0, 1)
            init = (jnp.zeros_like(decay), jnp.zeros_like(decay))
            _, (nf, df) = lax.scan(step, init, (ekv_t, ek_t))
            _, (nb, db) = lax.scan(step, init, (ekv_t, ek_t), reverse=True)
            nf = jnp.swapaxes(nf, 0, 1)
            df = jnp.swapaxes(df, 0, 1)
            nb = jnp.swapaxes(nb, 0, 1)
            db = jnp.swapaxes(db, 0, 1)
            euk = jnp.exp(jnp.minimum(u.astype(jnp.float32)[None, None, :] + kf, 30.0))
            num = nf + nb - ekv + euk * vf
            den = df + db - ek + euk
            base = jax.nn.sigmoid(r.astype(jnp.float32)) * (num / jnp.maximum(den, 1e-08))
            out = base * (0.8 + 0.2 * tf)
            return out.astype(r.dtype)
        return _bi_wkv(r, k, v, w, u, time_emb)

    def _L0_ffn_ref(hidden_states, router_w, gate_w, up_w, down_w, shared_gate_w, shared_up_w, shared_down_w):
        import jax, jax.numpy as jnp
        import numpy as np
        SEQ, BS, D, F, E = (256, 2, 512, 512, 8)
        S, B, Dm = hidden_states.shape
        x = hidden_states.reshape(-1, Dm)
        logits = x @ router_w
        expert_idx = jnp.argmax(logits, axis=-1)
        score = jax.nn.sigmoid(jnp.max(logits, axis=-1))
        xs = x * score[:, None]
        n_experts = router_w.shape[1]
        out = jnp.zeros_like(x)
        for e in range(n_experts):
            m = (expert_idx == e)[:, None]
            xe = jnp.where(m, xs, 0.0)
            h = jax.nn.silu(xe @ gate_w[e]) * (xe @ up_w[e])
            out = out + jnp.where(m, h @ down_w[e], 0.0)
        shared = jax.nn.silu(x @ shared_gate_w) * (x @ shared_up_w) @ shared_down_w
        return (out + shared).reshape(S, B, Dm)

    def _L1_cond_ref(r, k, v, w, u, time_emb):
        import jax, jax.numpy as jnp
        from jax import lax
        import numpy as np
        B, T, C, TD = (8, 512, 512, 128)

        def _bi_wkv(r, k, v, w, u, time_emb):
            tf = jax.nn.sigmoid(jnp.sum(time_emb, axis=-1))[:, None, None]
            decay = jnp.exp(-jnp.exp(w.astype(jnp.float32)))[None, :] * (0.5 + 0.5 * tf[:, :, 0])
            kf = k.astype(jnp.float32)
            vf = v.astype(jnp.float32)
            ek = jnp.exp(jnp.minimum(kf, 30.0))
            ekv = ek * vf

            def step(carry, x):
                a, b = carry
                ekv_t, ek_t = x
                a = a * decay + ekv_t
                b = b * decay + ek_t
                return ((a, b), (a, b))
            ekv_t = jnp.swapaxes(ekv, 0, 1)
            ek_t = jnp.swapaxes(ek, 0, 1)
            init = (jnp.zeros_like(decay), jnp.zeros_like(decay))
            _, (nf, df) = lax.scan(step, init, (ekv_t, ek_t))
            _, (nb, db) = lax.scan(step, init, (ekv_t, ek_t), reverse=True)
            nf = jnp.swapaxes(nf, 0, 1)
            df = jnp.swapaxes(df, 0, 1)
            nb = jnp.swapaxes(nb, 0, 1)
            db = jnp.swapaxes(db, 0, 1)
            euk = jnp.exp(jnp.minimum(u.astype(jnp.float32)[None, None, :] + kf, 30.0))
            num = nf + nb - ekv + euk * vf
            den = df + db - ek + euk
            base = jax.nn.sigmoid(r.astype(jnp.float32)) * (num / jnp.maximum(den, 1e-08))
            out = base * (0.8 + 0.2 * tf)
            return out.astype(r.dtype)
        return _bi_wkv(r, k, v, w, u, time_emb)

    def _L1_ffn_ref(x, w1, w2):
        import jax, jax.numpy as jnp
        import numpy as np
        EPS = 1e-05

        def _bitlinear(x, w):
            rms = jax.lax.rsqrt(jnp.maximum(jnp.mean(w * w), EPS))
            w_quant = jnp.clip(jnp.round(w * rms), -1.0, 1.0) / rms
            w_quant = jax.lax.stop_gradient(w_quant - w) + w
            scale = 127.0 / jnp.maximum(jnp.max(jnp.abs(x), axis=-1, keepdims=True), EPS)
            x_quant = jnp.clip(jnp.round(x * scale), -128.0, 127.0) / scale
            x_quant = jax.lax.stop_gradient(x_quant - x) + x
            return jnp.einsum('bsd,fd->bsf', x_quant, w_quant)
        h = _bitlinear(x, w1)
        h = jax.nn.gelu(h, approximate=False)
        out = _bitlinear(h, w2)
        return out
    x = x + _L0_ffn_ref(_L0_cond_ref(x, fside_BxSxS_0, fside_BxSxS_0, L0_cond_w, L0_cond_u, cond_512), L0_ffn_router_w, L0_ffn_gate_w, L0_ffn_up_w, L0_ffn_down_w, L0_ffn_shared_gate_w, L0_ffn_shared_up_w, L0_ffn_shared_down_w)
    x = x + _L1_ffn_ref(_L1_cond_ref(x, fside_BxSxS_0, fside_BxSxS_0, L1_cond_w, L1_cond_u, cond_512), L1_ffn_w1, L1_ffn_w2)
    return x

_drawn_inputs = setup_inputs


def setup_inputs(seed=0):
    import zlib

    import numpy as np

    out = dict(_drawn_inputs(seed))
    spreads = {}
    factors = {'cond_512': 7.614,
     'L0_cond_w': 8.0,
     'L0_cond_u': 8.0,
     'L0_ffn_router_w': 8.0,
     'L0_ffn_gate_w': 8.0,
     'L0_ffn_up_w': 8.0,
     'L0_ffn_down_w': 8.0,
     'L0_ffn_shared_gate_w': 5.863,
     'L0_ffn_shared_up_w': 5.814,
     'L0_ffn_shared_down_w': 5.732,
     'L1_cond_u': 63.04,
     'L1_cond_w': 8.0,
     'L1_ffn_w1': 5.564,
     'L1_ffn_w2': 5.45}
    for name, (base, spread) in spreads.items():
        noise = np.random.default_rng([zlib.crc32(name.encode()), seed]).standard_normal(out[name].shape)
        drawn = base * np.exp(spread * noise) if base else spread * noise
        out[name] = jnp.asarray(drawn.astype(out[name].dtype))
    for name, factor in factors.items():
        out[name] = (out[name] * factor).astype(out[name].dtype)
    return out
```

```python
from contextlib import ExitStack

import concourse.bass as bass
from concourse import mybir

F32 = mybir.dt.float32
BF16 = mybir.dt.bfloat16
I32 = mybir.dt.int32
U32 = mybir.dt.uint32
ALU = mybir.AluOpType
ACT = mybir.ActivationFunctionType
AX = mybir.AxisListType

P = 128
EXP30 = 10686474581524.463
MAGIC = 12582912.0
EPS = 1e-5


class Steps:

    def __init__(self, eng, sem):
        self.eng, self.sem, self.base, self.n = eng, sem, 0, 0

    def mark(self, ins):
        self.n += 1
        ins.then_inc(self.sem, 1)

    def settle(self):
        self.eng.wait_ge(self.sem, self.base + self.n)

    def enter(self, i, per):
        self.start, self.per = self.base + self.n, per
        self.base, self.n = i * per + self.start, 0

    def leave(self, count):
        assert self.n == self.per, (self.n, self.per)
        self.base, self.n = self.start + count * self.per, 0


def build(nc, x, fside, cond, w0, u0, router_w, gate_w, up_w, down_w, sh_gate, sh_up, sh_down,
          w1c, u1c, w1, w2, out, slot_rows, slot_out):
    B, T, C = x.shape
    TD = cond.shape[1]
    E = router_w.shape[1]
    F = gate_w.shape[2]
    FF = w1.shape[0]
    KC = C // P
    KF = F // P
    KG = FF // P
    TQ = T // P
    NT = B * TQ
    NCH = B * KC
    NS = NT + E - 1
    SLOTS = 24
    FIRST_IN_LOOP = 20
    WE = 3 * KC * F
    assert C == F == T == 512 and TQ == 4 and KC == 4

    f_v = fside.rearrange("b (q p) c -> b p q c", p=P)
    x_v = x.rearrange("b (q p) c -> b p q c", p=P)
    out_v = out.rearrange("b (q p) c -> (b q) p c", p=P)
    rows_v = slot_rows.rearrange("(s p) c -> s p c", p=P)
    moe_v = slot_out.rearrange("(s p) c -> s p c", p=P)
    w1_v = w1.rearrange("(g p) c -> g p c", p=P)
    w2_v = w2.rearrange("(r p) f -> r p f", p=P)

    def chunk_at(z):
        return z if 0 <= z < NCH else z - 4 if z >= 20 else None

    def ytok_tiles(z):
        b, c = (z - 4) // 4, z % 4
        if b == B - 1:
            return range(4 * b, 4 * b + 4) if c == 0 else ()
        return [4 * b + q for q in ((), (0,), (1, 2), (3,))[c]]

    with ExitStack() as ctx:
        def sb(name, shape, dt=F32):
            return ctx.enter_context(nc.sbuf_tensor(name, shape, dt))

        def sem(name):
            return ctx.enter_context(nc.semaphore(name))

        resid = sb("resid", [P, NT * C])
        ytok = sb("ytok", [P, NT * C])
        r1tok = ytok
        region = sb("region", [P, 2 * KC * T * 2])
        y0T = region[:, 0:2 * KC * T].rearrange("p (a k t) -> p a k t", a=2, k=KC)
        shT = region[:, 2 * KC * T:4 * KC * T].rearrange("p (a k t) -> p a k t", a=2, k=KF)
        w1flat = region[:, 0:2 * KC * T].bitcast(BF16)
        w2flat = region[:, 2 * KC * T:4 * KC * T].bitcast(BF16)
        w1T = w1flat.rearrange("p (k f) -> p k f", k=KC)
        w2T = w2flat.rearrange("p (g c) -> p g c", g=KG)
        wexp = sb("wexp", [P, 2 * WE])
        wsh = wexp[:, WE:2 * WE].rearrange("p (m k f) -> p m k f", m=3, k=KC)

        fk = sb("fk", [P, 2, TQ, P])
        xk = sb("xk", [P, 2, TQ, P])
        ksb = sb("ksb", [P, 2, T])
        ek = sb("ek", [P, 2, T])
        euk = sb("euk", [P, 2, T])
        ekv = sb("ekv", [P, T])
        fwd_n = sb("fwd_n", [P, T])
        fwd_d = sb("fwd_d", [P, T])
        bwd_n = sb("bwd_n", [P, T + 1])
        bwd_d = sb("bwd_d", [P, T + 1])
        num = sb("num", [P, 2, T])
        den = sb("den", [P, 2, T])
        tx = sb("tx", [P, 2, T])
        wraw_f = fk[:, :, :, :].rearrange("p a q t -> p a (q t)")
        txflat = tx[:, :, :].rearrange("p a t -> p (a t)").bitcast(BF16)
        above = txflat[:, 0:512]
        below = txflat[:, 512:1024]
        wtern = txflat[:, 1024:2048].rearrange("p (a t) -> p a t", a=2)

        work = sb("work", [P, 9, 512])
        wstat_in = work[:, 0:2, :]
        gtanh = work[:, 2, :]
        gt1 = work[:, 3, :]
        junk = work[:, 4, :]
        dn_sb = work[:, 5, :]
        zero = work[:, 6, :]
        xe = work[:, 0:2, :]
        xeT = work[:, 4:6, :].rearrange("p a (k t) -> p a k t", k=KC)
        hE = work[:, 6:8, :]
        heT = work[:, 8, :].rearrange("p (k t) -> p k t", k=KF)
        oE = xk[:, :, :, :].rearrange("p a q t -> p a (q t)")

        ident = sb("ident", [P, P])
        identb = sb("identb", [P, P], BF16)
        ones = sb("ones", [P, P])
        upper = work[:, 8, 0:P]
        iota_e = sb("iota_e", [P, E])
        iota_j = sb("iota_j", [P, NT])
        iota_s = sb("iota_s", [P, 24])
        sign_e = sb("sign_e", [P, E])
        par = sb("par", [P, 4, KC])
        cnd = den[:, 0, :].rearrange("p (b t) -> p b t", b=B)
        tf = sb("tf", [P, B])
        dhalf = sb("dhalf", [P, B])
        osh = sb("osh", [P, B])
        ew = sb("ew", [P, 2, KC])
        dec = sb("dec", [P, 2, KC, B])
        rw = sb("rw", [P, KC, E])
        lgT = work[0:E, 7, :]
        lg = sb("lg", [P, NT, E])
        score = sb("score", [P, NT])
        rt = num[:, :, :].rearrange("p a (k t) -> p (a k) t", t=NT * E)
        rs = den[:, 0, 0:240].rearrange("p (k s) -> p k s", k=10)
        tabf = den[0:1, 1, 384:480].rearrange("p (a s) -> p a s", a=3)
        cmp3 = den[0:1, 1, 0:384].rearrange("p (a s e) -> p a s e", a=2, e=8)
        tabi = sb("tabi", [1, 3, 32], I32)
        pos = sb("pos", [P, NT], U32)
        wstat = sb("wstat", [P, 2, 16])
        wsum = sb("wsum", [P, 2])
        magic = sb("magic", [P, 1])
        posn = sb("posn", [P, 2], U32)
        wq = sb("wq", [P, 2, 8])
        sc = sb("sc", [P, 2, 16])

        bank = [ctx.enter_context(nc.psum_tensor(f"bank{i}", [P, 512], F32)) for i in range(8)]
        KPS, XPS, GPS, UPS, DPS, YPS, LPS, MPS = bank

        s_const = sem("s_const")
        s_par = sem("s_par")
        s_tf = sem("s_tf")
        s_f = [sem("s_f0"), sem("s_f1")]
        s_x = [sem("s_xin0"), sem("s_xin1")]
        s_ws = [sem("s_ws0"), sem("s_ws1")]
        s_wsh = sem("s_wsh")
        s_resid = sem("s_resid")
        s_zero = sem("s_zero")
        s_ktr = sem("s_ktr")
        s_xtr = sem("s_xtr")
        s_kexp = sem("s_kexp")
        s_tx = sem("s_tx")
        s_ukc = sem("s_ukc")
        s_ek = sem("s_ek")
        s_euk = sem("s_euk")
        s_comb = sem("s_comb")
        s_nd = sem("s_nd")
        s_y = sem("s_y")
        s_rtr = sem("s_rtr")
        s_rev = sem("s_rev")
        s_lgmm = sem("s_lgmm")
        s_lgT = sem("s_lgT")
        s_lgtr = sem("s_lgtr")
        s_lg = sem("s_lg")
        s_ytr = sem("s_ytr")
        s_ytok = sem("s_ytok")
        s_g = sem("s_g")
        s_u = sem("s_u")
        s_tanh = sem("s_tanh")
        s_h = sem("s_h")
        s_down = sem("s_down")
        s_dn = sem("s_dn")
        s_res = sem("s_res")
        s_stat = sem("s_stat")
        s_oh = sem("s_oh")
        s_cum = sem("s_cum")
        s_pos = sem("s_pos")
        s_score = sem("s_score")
        s_scaled = sem("s_scaled")
        s_scat = sem("s_scat")
        s_tab = sem("s_tab")
        s_wsum = sem("s_wsum")
        s_wtot = sem("s_wtot")
        s_sq = sem("s_sq")
        s_rms = sem("s_rms")
        s_wl = sem("s_wl")
        s_xe = [sem("s_xe0"), sem("s_xe1")]
        s_xetr = sem("s_xetr")
        s_xeT = sem("s_xeT")
        s_eg = sem("s_eg")
        s_eu = sem("s_eu")
        s_et = sem("s_et")
        s_eh = sem("s_eh")
        s_ehtr = sem("s_ehtr")
        s_ehT = sem("s_ehT")
        s_eo = sem("s_eo")
        s_oe = sem("s_oe")
        s_ost = [sem("s_ost0"), sem("s_ost1")]
        s_wr = [sem("s_wr0"), sem("s_wr1")]
        s_tern = sem("s_tern")
        s_wtr = sem("s_wtr")
        s_wT = sem("s_wT")
        s_alone = sem("s_alone")
        s_posn = sem("s_posn")
        s_mo = [sem("s_mo0"), sem("s_mo1")]
        s_x1 = sem("s_x1")
        s_t1 = sem("s_t1")
        s_q1 = sem("s_q1")
        s_q1tr = sem("s_q1tr")
        s_q1T = sem("s_q1T")
        s_hh = sem("s_hh")
        s_gelu = sem("s_gelu")
        s_sc1 = sem("s_sc1")
        s_rnd = sem("s_rnd")
        s_q2 = sem("s_q2")
        s_q2tr = sem("s_q2tr")
        s_q2Ta = sem("s_q2Ta")
        s_q2Tv = sem("s_q2Tv")
        s_out = sem("s_out")
        s_fin = sem("s_fin")
        s_store = [sem("s_store0"), sem("s_store1")]
        s_vstep = sem("s_vstep")
        s_gstep = sem("s_gstep")
        s_astep = sem("s_astep")
        N_CONST = 13

        def late(a, n):
            return wexp[:, a * 512:(a + n) * 512]
        mo = late(0, 2).rearrange("p (a c) -> p a c", a=2)
        t1 = late(2, 1)
        y1 = late(3, 1)
        q1 = late(4, 1).bitcast(BF16)[:, 0:512]
        q1T = late(5, 1).bitcast(BF16).rearrange("p (a k t) -> p a k t", a=2, k=KC)
        gel = late(6, 8).rearrange("p (a f) -> p a f", a=2)
        q2 = late(14, 2).bitcast(BF16)
        q2T = late(16, 2).bitcast(BF16).rearrange("p (g t) -> p g t", g=KG)
        fin = late(18, 2).rearrange("p (a c) -> p a c", a=2)
        HPS = bank[0:4]
        QPS = bank[4][:, :].bitcast(BF16)
        TPS = [bank[5][:, :].bitcast(BF16), bank[6][:, :].bitcast(BF16)]
        OPS = bank[7]

        WPS = [YPS[:, :].bitcast(BF16), MPS[:, :].bitcast(BF16)]
        egt1 = gt1

        def route_1(dve, st, v_):
            def one(ins):
                st.mark(ins)
                st.settle()
            t_e = [P, NT, E]
            f = lambda k: rt[:, k, :].rearrange("p (t e) -> p t e", e=E)
            dve.wait_ge(s_lg, B)
            v_.tensor_reduce(score[:], lg[:, :, :], AX.X, ALU.max).then_inc(s_score, 1)
            dve.wait_ge(s_score, 1)
            st.mark(v_.tensor_tensor(out=f(0), in0=lg[:, :, :], in1=score[:].unsqueeze(2).to_broadcast(t_e),
                                     op=ALU.is_equal))
            st.settle()
            one(v_.tensor_tensor(out=f(1), in0=f(0), in1=iota_e[:].unsqueeze(1).to_broadcast(t_e),
                                 op=ALU.mult))
            one(v_.tensor_reduce(rs[:, 0, 0:NT], f(1), AX.X, ALU.min))
            v_.tensor_tensor(out=f(5), in0=iota_e[:].unsqueeze(1).to_broadcast(t_e),
                             in1=rs[:, 0, 0:NT].unsqueeze(2).to_broadcast(t_e),
                             op=ALU.is_equal).then_inc(s_oh, 1)

        def route_2(dve, st, v_):
            def one(ins):
                st.mark(ins)
                st.settle()
            e_t = [P, E, NT]
            g = lambda k: rt[:, k, :].rearrange("p (e t) -> p e t", e=E)
            f = lambda k: rt[:, k, :].rearrange("p (t e) -> p t e", e=E)
            r = lambda k, n=E: rs[:, k, 0:n]
            dve.wait_ge(s_cum, 1)
            one(v_.tensor_copy(g(0), MPS[:, 256:384].rearrange("p (t e) -> p e t", e=E)))
            one(v_.tensor_tensor_scan(rt[:, 1, :], ones[:], rt[:, 0, :], 0.0, ALU.mult, ALU.add))
            one(v_.tensor_tensor(out=rt[:, 2, :], in0=rt[:, 1, :], in1=rt[:, 0, :], op=ALU.subtract))
            one(v_.tensor_reduce(r(0), g(0), AX.X, ALU.add))
            one(v_.tensor_tensor(out=g(3), in0=r(0).unsqueeze(2).to_broadcast(e_t),
                                 in1=iota_j[:].unsqueeze(1).to_broadcast(e_t), op=ALU.is_gt))
            one(v_.tensor_reduce(r(1), g(3), AX.X, ALU.add))
            one(v_.tensor_tensor_scan(r(2), ones[:, 0:E], r(1), 0.0, ALU.mult, ALU.add))
            one(v_.tensor_tensor(out=r(3), in0=r(2), in1=r(1), op=ALU.subtract))
            one(v_.scalar_tensor_tensor(out=r(4), in0=r(3), scalar=float(P), in1=g(2)[:, :, 0],
                                        op0=ALU.mult, op1=ALU.subtract))
            one(v_.tensor_tensor(out=g(4), in0=g(2), in1=r(4).unsqueeze(2).to_broadcast(e_t), op=ALU.add))
            one(v_.tensor_tensor(out=f(1), in0=rt[:, 4, :].rearrange("p (e t) -> p t e", e=E),
                                 in1=MPS[:, 128:256].rearrange("p (t e) -> p t e", e=E), op=ALU.add))
            one(v_.tensor_tensor(out=f(3), in0=f(1), in1=f(5), op=ALU.mult))
            one(v_.tensor_reduce(r(5, NT), f(3), AX.X, ALU.add))
            v_.tensor_copy(pos[:], r(5, NT)).then_inc(s_pos, 1)
            ends = rs[0:1, 2, 0:E - 1].unsqueeze(1).to_broadcast([1, 24, E - 1])
            one(v_.tensor_tensor(out=cmp3[:, 0, :, 0:E - 1],
                                 in0=iota_s[0:1, :].unsqueeze(2).to_broadcast([1, 24, E - 1]),
                                 in1=ends, op=ALU.is_ge))
            one(v_.tensor_tensor(out=cmp3[:, 1, :, 0:E - 1], in0=cmp3[:, 0, :, 0:E - 1],
                                 in1=sign_e[0:1, 0:E - 1].unsqueeze(1).to_broadcast([1, 24, E - 1]),
                                 op=ALU.mult))
            one(v_.tensor_reduce(tabf[:, 0:2, 0:24], cmp3[:, :, :, 0:E - 1], AX.X, ALU.add))
            st.mark(v_.tensor_scalar(tabi[:, 0, 0:24], tabf[:, 0, 0:24], 48.0, 48.0, ALU.mult, ALU.add))
            st.mark(v_.tensor_scalar(tabi[:, 1, 0:24], tabf[:, 1, 0:24], float(WE), None, ALU.mult))
            st.mark(v_.tensor_scalar(tabi[:, 2, 0:E], rs[0:1, 2, 0:E], 1.0, None, ALU.add))
            st.settle()
            dve.sem_inc(s_tab, 1)

        block = ctx.enter_context(nc.Block())

        @block.sync
        def _(sp):
            sp.dma_start(fk[:, 0], f_v[0, :, :, 0:P]).then_inc(s_f[0], 16)
            sp.dma_start(xk[:, 0], x_v[0, :, :, 0:P]).then_inc(s_x[0], 16)
            with nc.allow_non_contiguous_dma(reason="vectors of 512 channels"):
                for j, v in enumerate((w0, u0, w1c, u1c)):
                    sp.dma_start(par[:, j, :], v.rearrange("(k p) -> p k", p=P)).then_inc(s_par, 16)
                sp.dma_start(cnd, cond.unsqueeze(0).to_broadcast([P, B, TD])).then_inc(s_par, 16)
                sp.dma_start(rw[:, :, :], router_w.rearrange("(k p) e -> p k e", p=P)).then_inc(s_par, 16)
            for n in range(NCH):
                if n + 1 < NCH:
                    m = n + 1
                    b, c = m // KC, m % KC
                    if m >= 2:
                        sp.wait_ge(s_ktr, m - 1)
                        sp.wait_ge(s_xtr, m - 1)
                    sp.dma_start(fk[:, m % 2], f_v[b, :, :, c * P:(c + 1) * P]).then_inc(s_f[m % 2], 16)
                    sp.dma_start(xk[:, m % 2], x_v[b, :, :, c * P:(c + 1) * P]).then_inc(s_x[m % 2], 16)
                for j, src in enumerate((w1_v[n], w2_v[n // 4, :, (n % 4) * 512:(n % 4 + 1) * 512])):
                    if n >= 1:
                        sp.wait_ge(s_stat, 2 * (n - 1) + j + 1)
                    sp.dma_start(wstat_in[:, j], src).then_inc(s_ws[j], 16)
                if n == 0:
                    for j, src in enumerate((sh_gate, sh_up, sh_down)):
                        sp.dma_start(wsh[:, j], src.rearrange("(k p) f -> p k f", p=P)).then_inc(s_wsh, 16)
                if n == 2:
                    for b in range(B):
                        sp.dma_start(resid[:, b * TQ * C:(b + 1) * TQ * C].rearrange("p (q c) -> p q c", q=TQ),
                                     x_v[b]).then_inc(s_resid, 16)
                if n == 3:
                    sp.wait_ge(s_const, N_CONST)
                if n >= 3 and n < 3 + 12:
                    for s in range(2 * (n - 3), 2 * (n - 3) + 2):
                        sp.dma_start(rows_v[s], zero).then_inc(s_zero, 16)
            for e in range(E):
                dst = wexp[:, (e % 2) * WE:(e % 2 + 1) * WE].rearrange("p (m k f) -> p m k f", m=3, k=KC)
                if e == 1:
                    for m in range(NCH, FIRST_IN_LOOP):
                        sp.wait_ge(s_ktr, m - 1)
                        sp.dma_start(fk[:, m % 2], f_v[0, :, :, m % KC * P:(m % KC + 1) * P]
                                     ).then_inc(s_f[m % 2], 16)
                    sp.wait_ge(s_down, NT)
                if e == 2:
                    sp.wait_ge(s_tab, 1)
                if e >= 2:
                    tiles = sp.value_load(tabi[0:1, 2, e - 2:e - 1], min_val=1, max_val=NS + 1)
                    sp.wait_ge(s_eo, tiles)
                for j, src in enumerate((gate_w, up_w, down_w)):
                    sp.dma_start(dst[:, j], src[e].rearrange("(k p) f -> p k f", p=P)).then_inc(s_wl, 16)
                sp.wait_ge(s_wl, 48 * (e + 1))
            with sp.Fori(0, NT // 2) as i:
                for a in range(2):
                    sp.wait_ge(s_fin, i * 2 + (a + 2))
                    sp.dma_start(out_v[bass.ds(i * 2 + a, 1)].rearrange("o p c -> (o p) c"),
                                 fin[:, a]).then_inc(s_store[a], 16)
            for a in range(2):
                sp.wait_ge(s_store[a], 16 * (NT // 2 + 1))

        @block.gpsimd
        def _(pool):
            st = Steps(pool, s_gstep)
            g = nc.gpsimd
            g.memset(ident[:], 0.0).then_inc(s_const, 1)
            g.memset(ones[:], 1.0).then_inc(s_const, 1)
            g.memset(bwd_n[:, T:T + 1], 0.0).then_inc(s_const, 1)
            g.memset(bwd_d[:, T:T + 1], 0.0).then_inc(s_const, 1)
            g.memset(zero, 0.0).then_inc(s_const, 1)
            pool.wait_ge(s_const, 5)
            g.affine_select(out=ident[:], in_=ident[:], compare_op=ALU.not_equal, fill=1.0, base=0,
                            pattern=[[-1, P]], channel_multiplier=1).then_inc(s_const, 1)
            g.affine_select(out=upper, in_=ones[:], compare_op=ALU.is_gt, fill=0.0, base=0,
                            pattern=[[1, P]], channel_multiplier=-1).then_inc(s_const, 1)
            g.iota(iota_e[:], pattern=[[1, E]], base=-E, channel_multiplier=0,
                   allow_small_or_imprecise_dtypes=True).then_inc(s_const, 1)
            g.iota(iota_j[:], pattern=[[P, NT]], base=0, channel_multiplier=0,
                   allow_small_or_imprecise_dtypes=True).then_inc(s_const, 1)
            g.iota(iota_s[:], pattern=[[1, 24]], base=0, channel_multiplier=0,
                   allow_small_or_imprecise_dtypes=True).then_inc(s_const, 1)
            g.iota(sign_e[:], pattern=[[0, E // 2], [-2, 2]], base=1, channel_multiplier=0,
                   allow_small_or_imprecise_dtypes=True).then_inc(s_const, 1)
            g.memset(magic[:], MAGIC).then_inc(s_const, 1)
            pool.wait_ge(s_const, 6)
            g.tensor_copy(identb[:], ident[:]).then_inc(s_const, 1)

            def alone():
                pool.sem_inc(s_alone, 1)

            def first(n, p, l, c):
                pool.wait_ge(s_kexp, n + 1)
                if not isinstance(n, int) or n >= 2:
                    pool.wait_ge(s_nd, n - 1)
                alone()
                g.tensor_scalar(euk[:, p], ksb[:, p], par[:, 2 * l + 1, c:c + 1], 30.0,
                                ALU.add, ALU.min).then_inc(s_ukc, 1)
                g.tensor_scalar(ek[:, p], ek[:, p], EXP30, None, ALU.min).then_inc(s_ek, 1)

            def second(n, p):
                pool.wait_ge(s_euk, n + 1)
                pool.wait_ge(s_comb, n + 1)
                st.mark(g.tensor_tensor(out=ksb[:, p], in0=euk[:, p], in1=ksb[:, p], op=ALU.mult))
                st.mark(g.tensor_tensor(out=den[:, p], in0=den[:, p], in1=euk[:, p], op=ALU.add))
                st.settle()
                st.mark(g.tensor_tensor(out=num[:, p], in0=num[:, p], in1=ksb[:, p], op=ALU.add))
                g.tensor_scalar(den[:, p], den[:, p], 1e-8, None, ALU.max).then_inc(s_nd, 1)

            pool.wait_ge(s_par, 96)
            for z in range(SLOTS):
                n = chunk_at(z)
                if n is not None:
                    first(n, n % 2, n // NCH, n % KC)
                    second(n, n % 2)
                if z == 17:
                    pool.wait_ge(s_zero, 16 * (NS + 1))
                    pool.wait_ge(s_pos, 1)
                    for t in range(NT):
                        pool.wait_ge(s_scaled, t + 1)
                        g.indirect_dma_start(slot_rows[:, :],
                                             bass.IndirectOffsetOnAxis(ap=pos[:, t:t + 1], axis=0),
                                             ytok[:, t * C:(t + 1) * C], None).then_inc(s_scat, 16)
                if z >= 8:
                    m = z - 8
                    pool.wait_ge(s_dn, m + 1)
                    pool.wait_ge(s_resid, 16 * B)
                    g.tensor_tensor(out=resid[:, m * C:(m + 1) * C], in0=resid[:, m * C:(m + 1) * C],
                                    in1=dn_sb, op=ALU.add).then_inc(s_res, 1)

            with pool.Fori(0, 3) as i:
                st.enter(i, 4 * 3)
                for c in range(KC):
                    n = i * KC + (c + FIRST_IN_LOOP)
                    first(n, c % 2, 1, c)
                    second(n, c % 2)
                st.leave(3)

            pool.wait_ge(s_rms, 1)
            pool.wait_ge(s_y, NCH)
            with pool.Fori(0, 4) as i:
                st.enter(i, 8 * 2)
                for v in range(8):
                    j, a = v // 4, v % 2
                    u = i * 8 + v
                    pool.wait_ge(s_wr[a], i * 64 + 16 * (v // 2 + 1))
                    pool.wait_ge(s_tern, u + 2)
                    alone()
                    st.mark(g.tensor_scalar(above, wraw_f[:, a], wq[:, j, 4:5], 0.5, ALU.mult, ALU.is_gt))
                    st.mark(g.tensor_scalar(below, wraw_f[:, a], wq[:, j, 4:5], -0.5, ALU.mult, ALU.is_lt))
                    st.settle()
                    pool.wait_ge(s_wtr, u + 1)
                    g.tensor_tensor(out=wtern[:, a], in0=above, in1=below, op=ALU.subtract).then_inc(s_tern, 1)
                st.leave(4)

            for a in range(2):
                pool.wait_ge(s_ost[a], 16 * ((NS + 1 - a) // 2 + 1))
            pool.wait_ge(s_eo, NS + 1)

            def gather(t, a):
                pool.wait_ge(s_x1, t + 1)
                g.tensor_copy(posn[:, a:a + 1], pos[:, bass.ds(t, 1)]).then_inc(s_posn, 1)
                pool.wait_ge(s_posn, t + 1)
                alone()
                g.indirect_dma_start(mo[:, a], None, slot_out[:, :],
                                     bass.IndirectOffsetOnAxis(ap=posn[:, a:a + 1], axis=0)
                                     ).then_inc(s_mo[a], 16)

            def round_2(t, a):
                pool.wait_ge(s_rnd, t + 1)
                pool.wait_ge(s_q2tr, t + 1)
                alone()
                g.tensor_scalar(q2, gel[:, a], MAGIC, 127.0, ALU.subtract, ALU.min).then_inc(s_q2, 1)

            gather(0, 0)
            with pool.Fori(0, 7) as i:
                for a in range(2):
                    gather(i * 2 + (a + 1), 1 - a)
                    round_2(i * 2 + a, a)
            gather(15, 1)
            round_2(14, 0)
            round_2(15, 1)

        @block.scalar
        def _(act):
            st = Steps(act, s_astep)
            a_ = nc.scalar.activation
            act.wait_ge(s_par, 96)
            act.wait_ge(s_tf, 1)
            a_(tf[:], dhalf[:], ACT.Sigmoid).then_inc(s_tf, 1)
            for l in range(2):
                st.mark(a_(ew[:, l], par[:, 2 * l], ACT.Exp))
            st.settle()
            a_(ew[:, :, :], ew[:, :, :], ACT.Exp, scale=-1.0).then_inc(s_tf, 1)

            def k_in(n, p):
                act.wait_ge(s_ktr, n + 1)
                if not isinstance(n, int) or n >= 2:
                    act.wait_ge(s_nd, n - 1)
                st.mark(a_(ksb[:, p], KPS[:, :], ACT.Copy))
                a_(ek[:, p], KPS[:, :], ACT.Exp).then_inc(s_kexp, 1)

            def euk_of(n, p):
                act.wait_ge(s_ukc, n + 1)
                a_(euk[:, p], euk[:, p], ACT.Exp).then_inc(s_euk, 1)

            def r_out(n, b, c):
                act.wait_ge(s_rtr, n - (NCH - 1))
                act.wait_ge(s_scat, 16 * NT)
                a_(r1tok[:, bass.ds(b * (TQ * C), TQ * C)].rearrange("p (q c) -> p q c", q=TQ)
                   [:, :, c * P:(c + 1) * P], YPS[:, :].rearrange("p (q c) -> p q c", q=TQ),
                   ACT.Copy).then_inc(s_rev, 1)

            for z in range(SLOTS):
                n = chunk_at(z)
                if n is not None:
                    k_in(n, n % 2)
                if n is not None and n < NCH:
                    act.wait_ge(s_xtr, n + 1)
                    if n >= 2:
                        act.wait_ge(s_y, n - 1)
                    a_(tx[:, n % 2], XPS[:, :], ACT.Tanh, scale=0.5).then_inc(s_tx, 1)
                if n is not None:
                    euk_of(n, n % 2)
                if n is not None and n < NCH:
                    for j in range(2):
                        act.wait_ge(s_ws[j], 16 * (n + 1))
                        if n or j:
                            act.wait_ge(s_stat, 2 * n + j)
                        a_(junk, wstat_in[:, j], ACT.Square,
                           accum_out=wstat[:, j, n:n + 1]).then_inc(s_stat, 1)
                if n is not None and n >= NCH + 2:
                    r_out(n - 2, 0, (n - 2) % KC)
                if z >= 8:
                    m = z - 8
                    act.wait_ge(s_down, m + 1)
                    if m:
                        act.wait_ge(s_res, m)
                    a_(dn_sb, DPS[:, :], ACT.Copy).then_inc(s_dn, 1)
                if 4 <= z < 20:
                    b, c = (z - 4) // 4, z % 4
                    if c == 0:
                        act.wait_ge(s_lgmm, b + 1)
                        if b:
                            act.wait_ge(s_lgtr, b)
                        a_(lgT, LPS[0:E, :], ACT.Copy).then_inc(s_lgT, 1)
                    act.wait_ge(s_g, z - 3)
                    if z > 4:
                        act.wait_ge(s_h, z - 4)
                    a_(gtanh, GPS[:, :], ACT.Tanh, scale=0.5).then_inc(s_tanh, 1)
                    for q in ytok_tiles(z):
                        act.wait_ge(s_ytr, q + 1)
                        a_(ytok[:, q * C:(q + 1) * C], YPS[:, :], ACT.Copy).then_inc(s_ytok, 1)
                if z == 16:
                    act.wait_ge(s_oh, 1)
                    a_(score[:], score[:], ACT.Sigmoid).then_inc(s_score, 1)
                    act.wait_ge(s_score, 2)
                    act.wait_ge(s_ytok, NT)
                    for t in range(NT):
                        a_(ytok[:, t * C:(t + 1) * C], ytok[:, t * C:(t + 1) * C], ACT.Copy,
                           scale=score[:, t:t + 1]).then_inc(s_scaled, 1)
                if z == 19:
                    act.wait_ge(s_sq, 1)
                    a_(wq[:, :, 1:2], wq[:, :, 0:1], ACT.Sqrt).then_inc(s_sq, 1)

            def xe_load(s, p):
                act.wait_ge(s_xetr, s + 1)
                act.dma_start(xe[:, p], rows_v[bass.ds(s, 1)].rearrange("o p c -> (o p) c")
                              ).then_inc(s_xe[p], 16)

            def xe_copy(s, p):
                act.wait_ge(s_xetr, s + 3)
                act.wait_ge(s_eu, s + 1)
                a_(xeT[:, p].rearrange("p k t -> p (k t)"), XPS[:, :], ACT.Copy).then_inc(s_xeT, 1)

            def e_tanh(s):
                act.wait_ge(s_eg, s + 1)
                act.wait_ge(s_eh, s + 1)
                a_(gtanh, GPS[:, :], ACT.Tanh, scale=0.5).then_inc(s_et, 1)

            def he_copy(s):
                act.wait_ge(s_ehtr, s + 2)
                act.wait_ge(s_eo, s + 1)
                a_(heT.rearrange("p k t -> p (k t)"), LPS[:, :], ACT.Copy).then_inc(s_ehT, 1)

            def o_copy(s, p, k):
                act.wait_ge(s_eo, s + 2)
                act.wait_ge(s_ost[p], k * 16 + 16)
                a_(oE[:, p], DPS[:, :], ACT.Copy).then_inc(s_oe, 1)
                act.wait_ge(s_oe, s + 2)
                act.dma_start(moe_v[bass.ds(s, 1)].rearrange("o p c -> (o p) c"), oE[:, p]
                              ).then_inc(s_ost[p], 16)

            act.wait_ge(s_scat, 16 * NT)
            act.wait_ge(s_res, NT)
            act.sem_inc(s_oe, 1)
            act.sem_inc(s_ehT, 1)
            for p in range(2):
                act.sem_inc(s_ost[p], 16)
            for p in range(2):
                xe_load(p, p)
            for p in range(2):
                xe_copy(p, p)
            e_tanh(0)
            with act.Fori(0, 3) as i:
                st.enter(i, 4)
                for c in range(KC):
                    s = i * KC + c
                    n = i * KC + (c + FIRST_IN_LOOP)
                    p = c % 2
                    act.wait_ge(s_ktr, n - 1)
                    act.dma_start(fk[:, p], f_v[bass.ds(i + 1, 1), :, :, c * P:(c + 1) * P
                                                ].rearrange("o p q c -> (o p) q c")).then_inc(s_f[p], 16)
                    xe_load(i * KC + (c + 2), p)
                    r_out(i * KC + (c + FIRST_IN_LOOP - 2), i + (c + 2) // KC, (c + 2) % KC)
                    e_tanh(i * KC + (c + 1))
                    k_in(n, p)
                    euk_of(n, p)
                    he_copy(s)
                    xe_copy(i * KC + (c + 2), p)
                    o_copy(s, p, i * 2 + c // 2)
                st.leave(3)
            for n in (2 * NCH - 2, 2 * NCH - 1):
                r_out(n, B - 1, n % KC)
            act.wait_ge(s_ktr, 2 * NCH)
            with act.Fori(0, 4) as i:
                for a in range(2):
                    s = i * 2 + (a + 12)
                    xe_load(i * 2 + (a + 14), a)
                    for v in range(4 * a, 4 * a + 4):
                        act.wait_ge(s_tern, i * 8 + (v + 1))
                        src = (w1_v[bass.ds(i * 4 + v, 1)].rearrange("o p c -> (o p) c") if v < 4 else
                               w2_v[bass.ds(i, 1), :, (v - 4) * 512:(v - 3) * 512].rearrange("o p c -> (o p) c"))
                        act.dma_start(wraw_f[:, v % 2], src).then_inc(s_wr[v % 2], 16)
                        if v % 4 == 1:
                            e_tanh(i * 2 + (a + 13))
                    he_copy(s)
                    xe_copy(i * 2 + (a + 14), a)
                    o_copy(s, a, i + 6)
            for s in (20, 21):
                if s == 20:
                    xe_load(22, 0)
                e_tanh(s + 1)
                he_copy(s)
                if s == 20:
                    xe_copy(22, 0)
                o_copy(s, s % 2, s // 2)
            he_copy(22)
            o_copy(22, 0, 11)

            def layer1_in(t, a):
                act.wait_ge(s_x1, t + 3)
                act.wait_ge(s_q1, t + 1)
                a_(t1, resid[:, bass.ds(t * C, C)], ACT.Tanh, scale=0.5).then_inc(s_t1, 1)
                act.wait_ge(s_q1tr, t + 2)
                act.wait_ge(s_hh, t * 4 + 4)
                a_(q1T[:, a].rearrange("p k t -> p (k t)"), QPS[:, 0:512], ACT.Copy).then_inc(s_q1T, 1)
                act.wait_ge(s_q2, t + 1)
                for j in range(4):
                    act.wait_ge(s_hh, t * 4 + (j + 9))
                    a_(gel[:, a, j * 512:(j + 1) * 512], HPS[j][:, :], ACT.Gelu,
                       scale=sc[:, a, 4:5]).then_inc(s_gelu, 1)

            def q2T_half(t):
                act.wait_ge(s_q2tr, t + 2)
                act.wait_ge(s_out, t + 1)
                a_(q2T[:, 0:8].rearrange("p g t -> p (g t)"), TPS[0], ACT.Copy).then_inc(s_q2Ta, 1)

            layer1_in(0, 0)
            with act.Fori(0, 7) as i:
                for a in range(2):
                    layer1_in(i * 2 + (a + 1), 1 - a)
                    q2T_half(i * 2 + a)
            layer1_in(15, 1)
            q2T_half(14)
            q2T_half(15)

        @block.tensor
        def _(pe):
            pe.sem_inc(s_xetr, 2)
            pe.sem_inc(s_eu, 2)
            pe.sem_inc(s_eh, 1)
            pe.sem_inc(s_ehtr, 1)
            pe.sem_inc(s_eo, 1)
            pe.sem_inc(s_wtr, 2)
            pe.sem_inc(s_tern, 2)
            pe.sem_inc(s_wT, 2)
            pe.wait_ge(s_const, N_CONST)
            mm, tr = nc.tensor.matmul, nc.tensor.transpose

            def four(out, src, idt, done):
                for q in range(4):
                    last = tr(out[:, q * P:(q + 1) * P], src(q), idt)
                last.then_inc(done, 1)

            def k_tr(n, p, count):
                pe.wait_ge(s_f[p], count)
                if not isinstance(n, int) or n >= 1:
                    pe.wait_ge(s_kexp, n)
                four(KPS, lambda q: fk[:, p, q, :], ident[:], s_ktr)

            def r_tr(n, p):
                pe.wait_ge(s_y, n + 1)
                if not isinstance(n, int):
                    pe.wait_ge(s_rev, n - NCH)
                elif n > NCH:
                    pe.wait_ge(s_rev, n - NCH)
                four(YPS, lambda q: num[:, p, q * P:(q + 1) * P], ident[:], s_rtr)

            for z in range(SLOTS):
                n = chunk_at(z)
                if n is not None:
                    k_tr(n, n % 2, 16 * (n // 2 + 1))
                if n is not None and n < NCH:
                    pe.wait_ge(s_x[n % 2], 16 * (n // 2 + 1))
                    if n:
                        pe.wait_ge(s_tx, n)
                    four(XPS, lambda q: xk[:, n % 2, q, :], ident[:], s_xtr)
                if n is not None and n >= NCH + 2:
                    r_tr(n - 2, n % 2)
                if z >= 8:
                    m = z - 8
                    pe.wait_ge(s_h, 4 * (m // 4 + 1))
                    if m:
                        pe.wait_ge(s_dn, m)
                    for j in range(KF):
                        last = mm(DPS[:, :], shT[:, m // 4 % 2, j, m % 4 * P:(m % 4 + 1) * P], wsh[:, 2, j, :],
                                  start=j == 0, stop=j == KF - 1)
                    last.then_inc(s_down, 1)
                if 4 <= z < 20:
                    b, c = (z - 4) // 4, z % 4
                    yb = y0T[:, b % 2]
                    if c == 0:
                        pe.wait_ge(s_y, 4 * (b + 1))
                        pe.wait_ge(s_par, 96)
                        if b:
                            pe.wait_ge(s_lgT, b)
                        for k in range(KC):
                            last = mm(LPS[0:E, :], rw[:, k, :], yb[:, k, :], start=k == 0, stop=k == KC - 1)
                        last.then_inc(s_lgmm, 1)
                    pe.wait_ge(s_wsh, 48)
                    if z > 4:
                        pe.wait_ge(s_h, z - 4)
                    for m_, ps, done in ((0, GPS, s_g), (1, UPS, s_u)):
                        for k in range(KC):
                            last = mm(ps[:, :], wsh[:, m_, k, c * P:(c + 1) * P], yb[:, k, :],
                                      start=k == 0, stop=k == KC - 1)
                        last.then_inc(done, 1)
                    if c == 0:
                        pe.wait_ge(s_lgT, b + 1)
                        if b:
                            pe.wait_ge(s_lg, b)
                        for q in range(4):
                            last = tr(MPS[:, q * E:(q + 1) * E], lgT[:, q * P:(q + 1) * P], ident[0:E, 0:E])
                        last.then_inc(s_lgtr, 1)
                    for t in ytok_tiles(z):
                        if t:
                            pe.wait_ge(s_ytok, t)
                        four(YPS, lambda k: yb[:, k, t % 4 * P:(t % 4 + 1) * P], ident[:], s_ytr)
                if z == 16:
                    pe.wait_ge(s_oh, 1)
                    mm(MPS[:, 128:256], upper, rt[:, 5, :], start=True, stop=True)
                    mm(MPS[:, 256:384], ones[:], rt[:, 5, :], start=True, stop=True).then_inc(s_cum, 1)
                if z == 18:
                    pe.wait_ge(s_wsum, 1)
                    mm(MPS[:, 384:386], ones[:], wsum[:], start=True, stop=True).then_inc(s_wtot, 1)

            def e_in(s, p, k):
                pe.wait_ge(s_xe[p], k * 16 + 16)
                if not isinstance(s, int) or s >= 1:
                    pe.wait_ge(s_xeT, s)
                four(XPS, lambda q: xe[:, p, q * P:(q + 1) * P], ident[:], s_xetr)

            def e_gate_up(s, p):
                loads = pe.value_load(tabi[0:1, 0, bass.ds(s, 1)], min_val=48, max_val=48 * E)
                at = pe.value_load(tabi[0:1, 1, bass.ds(s, 1)], min_val=0, max_val=WE)
                pe.wait_ge(s_wl, loads)
                pe.wait_ge(s_xeT, s + 1)
                pe.wait_ge(s_eh, s + 1)
                for m_, ps, done in ((0, GPS, s_eg), (1, UPS, s_eu)):
                    for k in range(KC):
                        last = mm(ps[:, :], xeT[:, p, k, :], wexp[:, bass.ds(at + (m_ * KC + k) * F, F)],
                                  start=k == 0, stop=k == KC - 1)
                    last.then_inc(done, 1)

            def e_h(s, p):
                pe.wait_ge(s_eh, s + 2)
                pe.wait_ge(s_ehT, s + 1)
                four(LPS, lambda q: hE[:, p, q * P:(q + 1) * P], ident[:], s_ehtr)

            def e_down(s):
                at = pe.value_load(tabi[0:1, 1, bass.ds(s, 1)], min_val=0, max_val=WE)
                pe.wait_ge(s_ehT, s + 2)
                pe.wait_ge(s_oe, s + 1)
                for j in range(KF):
                    last = mm(DPS[:, :], heT[:, j, :], wexp[:, bass.ds(at + (2 * KC + j) * F, F)],
                              start=j == 0, stop=j == KF - 1)
                last.then_inc(s_eo, 1)

            def w_tr(u, v):
                a = v % 2
                pe.wait_ge(s_tern, u + 3)
                pe.wait_ge(s_wT, u + 1)
                four(WPS[a], lambda q: wtern[:, a, q * P:(q + 1) * P], identb[:], s_wtr)

            pe.wait_ge(s_tab, 1)
            e_in(0, 0, 0)
            e_in(1, 1, 0)
            e_gate_up(0, 0)
            with pe.Fori(0, 3) as i:
                for c in range(KC):
                    s = i * KC + c
                    p = c % 2
                    r_tr(i * KC + (c + FIRST_IN_LOOP - 2), p)
                    e_gate_up(i * KC + (c + 1), 1 - p)
                    k_tr(i * KC + (c + FIRST_IN_LOOP), p, i * 32 + 16 * ((c + FIRST_IN_LOOP) // 2 + 1))
                    e_h(s, p)
                    e_in(i * KC + (c + 2), p, i * 2 + (c + 2) // 2)
                    e_down(s)
            for n in (2 * NCH - 2, 2 * NCH - 1):
                r_tr(n, n % 2)
            pe.wait_ge(s_rev, NCH)
            with pe.Fori(0, 4) as i:
                for a in range(2):
                    s = i * 2 + (a + 12)
                    e_gate_up(i * 2 + (a + 13), 1 - a)
                    for v in range(4 * a, 4 * a + 2):
                        w_tr(i * 8 + v, v)
                    e_h(s, a)
                    e_in(i * 2 + (a + 14), a, i + 7)
                    e_down(s)
                    for v in range(4 * a + 2, 4 * a + 4):
                        w_tr(i * 8 + v, v)
            for s in (20, 21):
                e_gate_up(s + 1, 1 - s % 2)
                e_h(s, s % 2)
                if s == 20:
                    e_in(22, 0, 11)
                e_down(s)
            e_h(22, 0)
            e_down(22)

            def layer1_h(t, a):
                pe.wait_ge(s_q1, t + 2)
                pe.wait_ge(s_q1T, t + 1)
                four(QPS, lambda q: q1[:, q * P:(q + 1) * P], identb[:], s_q1tr)
                pe.wait_ge(s_q1T, t + 2)
                for j in range(4):
                    pe.wait_ge(s_gelu, t * 4 + (j + 1))
                    for k in range(KC):
                        last = mm(HPS[j][:, :], q1T[:, a, k, :], w1T[:, k, j * 512:(j + 1) * 512],
                                  start=k == 0, stop=k == KC - 1)
                    last.then_inc(s_hh, 1)

            def layer1_out(t):
                pe.wait_ge(s_q2, t + 3)
                pe.wait_ge(s_q2Ta, t + 1)
                pe.wait_ge(s_q2Tv, t + 1)
                for g in range(KG):
                    last = tr(TPS[g // 8][:, g % 8 * P:(g % 8 + 1) * P], q2[:, g * P:(g + 1) * P], identb[:])
                last.then_inc(s_q2tr, 1)
                pe.wait_ge(s_q2Ta, t + 2)
                pe.wait_ge(s_q2Tv, t + 2)
                pe.wait_ge(s_fin, t + 1)
                for g in range(KG):
                    last = mm(OPS[:, :], q2T[:, g, :], w2T[:, g, :], start=g == 0, stop=g == KG - 1)
                last.then_inc(s_out, 1)

            layer1_h(0, 0)
            with pe.Fori(0, 7) as i:
                for a in range(2):
                    layer1_h(i * 2 + (a + 1), 1 - a)
                    layer1_out(i * 2 + a)
            layer1_h(15, 1)
            layer1_out(14)
            layer1_out(15)

        @block.vector
        def _(dve):
            st = Steps(dve, s_vstep)
            v_ = nc.vector
            for s_, k in ((s_x1, 2), (s_q1, 1), (s_q1tr, 1), (s_q1T, 1), (s_hh, 8), (s_gelu, 4), (s_q2, 2),
                          (s_q2tr, 1), (s_q2Ta, 1), (s_q2Tv, 1), (s_out, 1), (s_fin, 1),
                          (s_store[0], 16), (s_store[1], 16)):
                dve.sem_inc(s_, k)
            dve.wait_ge(s_par, 96)
            v_.tensor_reduce(dhalf[:], cnd, AX.X, ALU.add).then_inc(s_tf, 1)
            dve.wait_ge(s_tf, 3)
            st.mark(v_.tensor_scalar(dhalf[:], tf[:], 0.5, 0.5, ALU.mult, ALU.add))
            st.mark(v_.tensor_scalar(osh[:], tf[:], 0.1, 0.4, ALU.mult, ALU.add))
            st.settle()
            for l in range(2):
                for c in range(KC):
                    st.mark(v_.tensor_scalar(dec[:, l, c, :], dhalf[:], ew[:, l, c:c + 1], None, ALU.mult))
            st.settle()
            dve.wait_ge(s_const, N_CONST)

            def scans(n, p, l, c, b):
                dve.wait_ge(s_ek, n + 1)
                if not isinstance(n, int) or n >= 1:
                    dve.wait_ge(s_comb, n)
                if not isinstance(n, int) or n >= 2:
                    dve.wait_ge(s_y, n - 1)
                if not isinstance(n, int) or n >= NCH + 2:
                    dve.wait_ge(s_rtr, n - (NCH + 1))
                d1 = dec[:, l, c, bass.ds(b, 1)]
                d = d1.to_broadcast([P, T])
                st.mark(v_.tensor_tensor(out=ekv[:, :], in0=ek[:, p], in1=ksb[:, p], op=ALU.mult))
                st.mark(v_.tensor_tensor_scan(fwd_d[:, :], d, ek[:, p], 0.0, ALU.mult, ALU.add))
                st.mark(v_.tensor_tensor_scan(bwd_d[:, 0:T][:, ::-1], d, ek[:, p][:, ::-1], 0.0,
                                              ALU.mult, ALU.add))
                st.settle()
                st.mark(v_.tensor_tensor_scan(fwd_n[:, :], d, ekv[:, :], 0.0, ALU.mult, ALU.add))
                st.mark(v_.tensor_tensor_scan(bwd_n[:, 0:T][:, ::-1], d, ekv[:, ::-1], 0.0,
                                              ALU.mult, ALU.add))
                st.mark(v_.scalar_tensor_tensor(out=den[:, p], in0=bwd_d[:, 1:T + 1], scalar=d1,
                                                in1=fwd_d[:, :], op0=ALU.mult, op1=ALU.add))
                st.settle()
                v_.scalar_tensor_tensor(out=num[:, p], in0=bwd_n[:, 1:T + 1], scalar=d1,
                                        in1=fwd_n[:, :], op0=ALU.mult, op1=ALU.add).then_inc(s_comb, 1)

            def ratio(n, p, l, b):
                dve.wait_ge(s_nd, n + 1)
                st.mark(v_.reciprocal(den[:, p], den[:, p]))
                st.settle()
                o = osh[:, bass.ds(b, 1)]
                ins = v_.scalar_tensor_tensor(out=num[:, p], in0=num[:, p], scalar=o, in1=den[:, p],
                                              op0=ALU.mult, op1=ALU.mult)
                if l:
                    ins.then_inc(s_y, 1)
                    return
                st.mark(ins)
                st.settle()
                dve.wait_ge(s_tx, n + 1)
                if b >= 2:
                    dve.wait_ge(s_ytr, 4 * (b - 1))
                v_.scalar_tensor_tensor(out=y0T[:, b % 2, n % KC, :], in0=tx[:, p], scalar=1.0, in1=num[:, p],
                                        op0=ALU.add, op1=ALU.mult).then_inc(s_y, 1)

            for z in range(SLOTS):
                n = chunk_at(z)
                m = chunk_at(z - 1)
                if m is not None:
                    ratio(m, m % 2, m // NCH, m % NCH // KC)
                if n is not None:
                    scans(n, n % 2, n // NCH, n % KC, n % NCH // KC)
                if 4 <= z < 20:
                    b, c = (z - 4) // 4, z % 4
                    dve.wait_ge(s_tanh, z - 3)
                    if z > 4:
                        dve.wait_ge(s_h, z - 4)
                    st.mark(v_.scalar_tensor_tensor(out=gt1, in0=gtanh, scalar=1.0, in1=GPS[:, :],
                                                    op0=ALU.add, op1=ALU.mult))
                    st.settle()
                    dve.wait_ge(s_u, z - 3)
                    if b >= 2:
                        dve.wait_ge(s_down, 4 * (b - 1))
                    v_.scalar_tensor_tensor(out=shT[:, b % 2, c, :], in0=gt1, scalar=0.5, in1=UPS[:, :],
                                            op0=ALU.mult, op1=ALU.mult).then_inc(s_h, 1)
                    if c == 0:
                        dve.wait_ge(s_lgtr, b + 1)
                        v_.tensor_copy(lg[:, 4 * b:4 * b + 4, :].rearrange("p t e -> p (t e)"),
                                       MPS[:, 0:4 * E]).then_inc(s_lg, 1)
                if z == 16:
                    route_1(dve, st, v_)
                if z == 16:
                    route_2(dve, st, v_)
                if z == 17:
                    v_.tensor_reduce(wsum[:], wstat[:, :, :], AX.X, ALU.add).then_inc(s_wsum, 1)
                if z == 18:
                    dve.wait_ge(s_wtot, 1)
                    v_.tensor_scalar(wq[:, :, 0:1], MPS[:, 384:386].rearrange("p (j o) -> p j o", o=1),
                                     1.0 / (FF * C), EPS, ALU.mult, ALU.max).then_inc(s_sq, 1)
                if z == 20:
                    w = lambda k: wq[:, :, k:k + 1]
                    def one(ins):
                        st.mark(ins)
                        st.settle()
                    dve.wait_ge(s_sq, 2)
                    one(v_.reciprocal(w(2), w(1)))
                    one(v_.tensor_tensor(out=w(3), in0=w(2), in1=w(2), op=ALU.mult))
                    one(v_.tensor_tensor(out=w(3), in0=w(3), in1=w(0), op=ALU.mult))
                    one(v_.tensor_scalar(w(3), w(3), -0.5, 1.5, ALU.mult, ALU.add))
                    one(v_.tensor_tensor(out=w(4), in0=w(3), in1=w(2), op=ALU.mult))
                    one(v_.reciprocal(w(5), w(4)))
                    v_.tensor_scalar(w(6), w(5), 1.0 / 127.0, None, ALU.mult).then_inc(s_rms, 1)

            def e_silu(s, p):
                dve.wait_ge(s_et, s + 1)
                st.mark(v_.scalar_tensor_tensor(out=egt1, in0=gtanh, scalar=1.0, in1=GPS[:, :],
                                                op0=ALU.add, op1=ALU.mult))
                st.settle()
                dve.wait_ge(s_eu, s + 3)
                dve.wait_ge(s_ehtr, s) if not isinstance(s, int) or s >= 1 else None
                v_.scalar_tensor_tensor(out=hE[:, p], in0=egt1, scalar=0.5, in1=UPS[:, :],
                                        op0=ALU.mult, op1=ALU.mult).then_inc(s_eh, 1)

            e_silu(0, 0)
            with dve.Fori(0, 3) as i:
                st.enter(i, 4 * 8)
                for c in range(KC):
                    n = i * KC + (c + FIRST_IN_LOOP)
                    p = c % 2
                    ratio(i * KC + (c + FIRST_IN_LOOP - 1), 1 - p, 1, i + (c + KC - 1) // KC)
                    e_silu(i * KC + (c + 1), 1 - p)
                    scans(n, p, 1, c, i + 1)
                st.leave(3)
            ratio(2 * NCH - 1, 1, 1, B - 1)

            def w_out(u, i, v):
                dve.wait_ge(s_wtr, u + 3)
                src = WPS[v % 2][:, 0:512].rearrange("p (k t) -> p k t", k=4)
                if v < 4:
                    dst = w1flat.rearrange("p (k f) -> p k f", k=KC)[:, :, bass.ds(i * 512 + v * P, P)]
                else:
                    dst = w2T[:, (v - 4) * 4:(v - 3) * 4, bass.ds(i * P, P)]
                v_.tensor_copy(dst, src).then_inc(s_wT, 1)

            with dve.Fori(0, 4) as i:
                st.enter(i, 2)
                for a in range(2):
                    e_silu(i * 2 + (a + 13), 1 - a)
                    for v in range(4 * a, 4 * a + 4):
                        w_out(i * 8 + v, i, v)
                st.leave(4)
            e_silu(21, 1)
            e_silu(22, 0)

            def small(ins):
                st.mark(ins)
                st.settle()

            def layer1_x(t, a, k):
                dve.wait_ge(s_mo[a], k * 16 + 16)
                xt = resid[:, bass.ds(t * C, C)]
                v_.tensor_tensor(out=xt, in0=xt, in1=mo[:, a], op=ALU.add).then_inc(s_x1, 1)
                dve.wait_ge(s_t1, t + 1)
                dve.wait_ge(s_q1, t + 1)
                small(v_.scalar_tensor_tensor(out=y1, in0=t1, scalar=1.0, in1=r1tok[:, bass.ds(t * C, C)],
                                              op0=ALU.add, op1=ALU.mult))
                S = lambda j: sc[:, a, j:j + 1]
                small(v_.tensor_reduce(S(0), y1, AX.X, ALU.max, apply_absolute_value=True))
                small(v_.tensor_scalar(S(0), S(0), EPS, None, ALU.max))
                small(v_.reciprocal(S(1), S(0)))
                dve.wait_ge(s_gelu, t * 4)
                st.mark(v_.tensor_scalar(S(4), S(0), wq[:, 0, 6:7], None, ALU.mult))
                small(v_.tensor_scalar(S(2), S(1), 127.0, None, ALU.mult))
                small(v_.tensor_scalar(y1, y1, S(2), MAGIC, ALU.mult, ALU.add))
                dve.wait_ge(s_q1tr, t + 1)
                v_.tensor_scalar(q1, y1, MAGIC, 127.0, ALU.subtract, ALU.min).then_inc(s_q1, 1)

            def layer1_round(t, a, k):
                S = lambda j: sc[:, a, j:j + 1]
                for j in range(4):
                    dve.wait_ge(s_gelu, t * 4 + (j + 5))
                    st.mark(v_.tensor_reduce(S(8 + j), gel[:, a, j * 512:(j + 1) * 512], AX.X, ALU.max,
                                             apply_absolute_value=True))
                st.settle()
                small(v_.tensor_reduce(S(5), sc[:, a, 8:12], AX.X, ALU.max))
                small(v_.tensor_scalar(S(5), S(5), EPS, None, ALU.max))
                small(v_.reciprocal(S(6), S(5)))
                st.mark(v_.tensor_scalar(S(12), S(5), wq[:, 1, 6:7], None, ALU.mult))
                small(v_.tensor_scalar(S(7), S(6), 127.0, None, ALU.mult))
                v_.tensor_scalar(gel[:, a], gel[:, a], S(7), MAGIC, ALU.mult, ALU.add).then_inc(s_rnd, 1)
                dve.wait_ge(s_q2tr, t + 2)
                dve.wait_ge(s_out, t + 1)
                v_.tensor_copy(q2T[:, 8:16].rearrange("p g t -> p (g t)"), TPS[1]).then_inc(s_q2Tv, 1)
                dve.wait_ge(s_out, t + 2)
                dve.wait_ge(s_store[a], k * 16 + 16)
                v_.scalar_tensor_tensor(out=fin[:, a], in0=OPS[:, :], scalar=S(12),
                                        in1=resid[:, bass.ds(t * C, C)], op0=ALU.mult, op1=ALU.add
                                        ).then_inc(s_fin, 1)

            PER = 7 + 9
            layer1_x(0, 0, 0)
            with dve.Fori(0, 7) as i:
                st.enter(i, 2 * PER)
                for a in range(2):
                    layer1_x(i * 2 + (a + 1), 1 - a, i + a)
                    layer1_round(i * 2 + a, a, i)
                st.leave(7)
            layer1_x(15, 1, 7)
            layer1_round(14, 0, 7)
            layer1_round(15, 1, 7)


_INS = ['x', 'fside_BxSxS_0', 'cond_512', 'L0_cond_w', 'L0_cond_u', 'L0_ffn_router_w', 'L0_ffn_gate_w',
        'L0_ffn_up_w', 'L0_ffn_down_w', 'L0_ffn_shared_gate_w', 'L0_ffn_shared_up_w', 'L0_ffn_shared_down_w',
        'L1_cond_w', 'L1_cond_u', 'L1_ffn_w1', 'L1_ffn_w2']


def kernel(**inputs):
    import numpy as _np
    import concourse.bacc as _bacc
    from concourse import mybir as _mybir
    from concourse.bass_utils import run_bass_kernel_spmd as _run

    nc = _bacc.Bacc("TRN2", target_bir_lowering=False, num_devices=1)
    arrays, args = {}, []
    for name in _INS:
        a = _np.ascontiguousarray(inputs[name])
        arrays[f"in_{name}_dram"] = a
        args.append(nc.dram_tensor(f"in_{name}_dram", a.shape, _mybir.dt.from_np(a.dtype), kind="ExternalInput").ap())
    f32 = _mybir.dt.float32
    args.append(nc.dram_tensor("out_0_dram", inputs["x"].shape, f32, kind="ExternalOutput").ap())
    tokens, channels = inputs["x"].shape[0] * inputs["x"].shape[1], inputs["x"].shape[2]
    slots = tokens + 128 * inputs["L0_ffn_router_w"].shape[1]
    args.append(nc.dram_tensor("slot_rows", (slots, channels), f32, kind="Internal").ap())
    args.append(nc.dram_tensor("slot_out", (slots - 128, channels), f32, kind="Internal").ap())
    build(nc, *args)
    r = _run(nc, [arrays], core_ids=[0])
    return r.results[0]["out_0_dram"]
```

```python
from contextlib import ExitStack

import concourse.bass as bass
from concourse import mybir

F32 = mybir.dt.float32
BF16 = mybir.dt.bfloat16
I32 = mybir.dt.int32
U32 = mybir.dt.uint32
ALU = mybir.AluOpType
ACT = mybir.ActivationFunctionType
AX = mybir.AxisListType

P = 128
EXP30 = 10686474581524.463
MAGIC = 12582912.0
EPS = 1e-5


class Steps:

    def __init__(self, eng, sem):
        self.eng, self.sem, self.base, self.n = eng, sem, 0, 0

    def mark(self, ins):
        self.n += 1
        ins.then_inc(self.sem, 1)

    def settle(self):
        self.eng.wait_ge(self.sem, self.base + self.n)

    def enter(self, i, per, first=0):
        self.start, self.per = self.base + self.n, per
        self.base, self.n = i * per + (self.start - first * per), 0

    def leave(self, count):
        assert self.n == self.per, (self.n, self.per)
        self.base, self.n = self.start + count * self.per, 0


def build(nc, x, fside, cond, w0, u0, router_w, gate_w, up_w, down_w, sh_gate, sh_up, sh_down,
          w1c, u1c, w1, w2, out, slot_rows, slot_out):
    B, T, C = x.shape
    TD = cond.shape[1]
    E = router_w.shape[1]
    F = gate_w.shape[2]
    FF = w1.shape[0]
    KC = C // P
    KF = F // P
    KG = FF // P
    TQ = T // P
    NT = B * TQ
    NCH = B * KC
    NS = NT + E - 1
    STEPS_A = 25
    NU = 2 * NT
    WE = 3 * KC * F
    assert C == F == T == 512 and TQ == 4 and KC == 4

    f_v = fside.rearrange("b (q p) c -> b p q c", p=P)
    x_v = x.rearrange("b (q p) c -> b p q c", p=P)
    out_v = out.rearrange("b (q p) c -> (b q) p c", p=P)
    rows_v = slot_rows.rearrange("(s p) c -> s p c", p=P)
    moe_v = slot_out.rearrange("(s p) c -> s p c", p=P)
    w1_v = w1.rearrange("(g p) c -> g p c", p=P)
    w2_v = w2.rearrange("(r p) f -> r p f", p=P)

    def ytok_tiles(z):
        b, c = (z - 5) // 4, (z - 5) % 4
        if b == B - 1:
            return range(4 * b, 4 * b + 4) if c == 0 else ()
        return [4 * b + q for q in ((), (0,), (1, 2), (3,))[c]]

    def units_in_a(z):
        return range(2 * (z - 21), 2 * (z - 21) + 2) if z >= 21 else ()

    def units_at(s):
        return range(8 + 4 * (s - NT), 12 + 4 * (s - NT)) if NT <= s < NT + 6 else ()

    with ExitStack() as ctx:
        def sb(name, shape, dt=F32):
            return ctx.enter_context(nc.sbuf_tensor(name, shape, dt))

        def sem(name):
            return ctx.enter_context(nc.semaphore(name))

        resid = sb("resid", [P, NT * C])
        ytok = sb("ytok", [P, NT * C])
        r1tok = ytok
        region = sb("region", [P, 2 * KC * T * 2])
        y0T = region[:, 0:2 * KC * T].rearrange("p (a k t) -> p a k t", a=2, k=KC)
        shT = region[:, 2 * KC * T:4 * KC * T].rearrange("p (a k t) -> p a k t", a=2, k=KF)
        w1flat = region[:, 0:2 * KC * T].bitcast(BF16)
        w2flat = region[:, 2 * KC * T:4 * KC * T].bitcast(BF16)
        w1T = w1flat.rearrange("p (k f) -> p k f", k=KC)
        w2T = w2flat.rearrange("p (g c) -> p g c", g=KG)
        wexp = sb("wexp", [P, 2 * WE])
        wsh = wexp[:, WE:2 * WE].rearrange("p (m k f) -> p m k f", m=3, k=KC)

        fk = sb("fk", [P, 2, TQ, P])
        xk = sb("xk", [P, 2, TQ, P])
        ksb = sb("ksb", [P, 2, T])
        kk = sb("kk", [P, 2, 2, T])
        ekv = sb("ekv", [P, 2, T])
        bwd_n = sb("bwd_n", [P, T + 1])
        bwd_d = sb("bwd_d", [P, T + 1])
        num = sb("num", [P, 2, T])
        den = sb("den", [P, 2, T])
        tx = sb("tx", [P, 2, T])
        wraw_a = xk[:, :, :, :].rearrange("p a q t -> p a (q t)")
        wraw_e = fk[:, :, :, :].rearrange("p a q t -> p a (q t)")
        txflat = tx[:, :, :].rearrange("p a t -> p (a t)").bitcast(BF16)
        above = txflat[:, 0:512]
        below = txflat[:, 512:1024]
        wtern = txflat[:, 1024:2048].rearrange("p (a t) -> p a t", a=2)

        work = sb("work", [P, 9, 512])
        wstat_in = work[:, 0:2, :]
        gtanh = work[:, 2, :]
        gt1 = work[:, 3, :]
        junk = work[:, 4, :]
        dn_sb = work[:, 5, :]
        zero = work[:, 6, :]
        xe = work[:, 0:2, :]
        xeT = work[:, 7:9, :].rearrange("p a (k t) -> p a k t", k=KC)
        hE = [junk, zero]
        heT = sb("heT", [P, KF, P])
        oE = xk[:, :, :, :].rearrange("p a q t -> p a (q t)")

        ident = sb("ident", [P, P])
        identb = sb("identb", [P, P], BF16)
        ones = sb("ones", [P, P])
        upper = work[:, 8, 0:P]
        iota_e = sb("iota_e", [P, E])
        iota_j = sb("iota_j", [P, NT])
        iota_s = sb("iota_s", [P, 24])
        sign_e = sb("sign_e", [P, E])
        par = sb("par", [P, 4, KC])
        cnd = den[:, 0, :].rearrange("p (b t) -> p b t", b=B)
        tf = sb("tf", [P, B])
        dhalf = sb("dhalf", [P, B])
        osh = sb("osh", [P, B])
        ew = sb("ew", [P, 2, KC])
        dec = sb("dec", [P, 2, KC, B])
        rw = sb("rw", [P, KC, E])
        lgT = work[0:E, 7, :]
        lg = sb("lg", [P, NT, E])
        score = sb("score", [P, NT])
        rt = num[:, :, :].rearrange("p a (k t) -> p (a k) t", t=NT * E)
        rs = den[:, 0, 0:240].rearrange("p (k s) -> p k s", k=10)
        tabf = den[0:1, 1, 384:480].rearrange("p (a s) -> p a s", a=3)
        cmp3 = den[0:1, 1, 0:384].rearrange("p (a s e) -> p a s e", a=2, e=8)
        tabi = sb("tabi", [1, 3, 32], I32)
        pos = sb("pos", [P, NT], U32)
        wstat = sb("wstat", [P, 2, 16])
        wsum = sb("wsum", [P, 2])
        magic = sb("magic", [P, 1])
        posn = sb("posn", [P, 2], U32)
        wq = sb("wq", [P, 2, 8])
        sc = sb("sc", [P, 2, 16])

        bank = [ctx.enter_context(nc.psum_tensor(f"bank{i}", [P, 512], F32)) for i in range(8)]
        KPS, XPS, GPS, UPS, DPS, YPS, LPS, MPS = bank

        s_const = sem("s_const")
        s_par = sem("s_par")
        s_tf = sem("s_tf")
        s_f = [sem("s_f0"), sem("s_f1")]
        s_x = [sem("s_xin0"), sem("s_xin1")]
        s_ws = [sem("s_ws0"), sem("s_ws1")]
        s_wsh = sem("s_wsh")
        s_resid = sem("s_resid")
        s_zero = sem("s_zero")
        s_ktr = sem("s_ktr")
        s_xtr = sem("s_xtr")
        s_kexp = sem("s_kexp")
        s_kcopy = sem("s_kcopy")
        s_tx = sem("s_tx")
        s_ukc = sem("s_ukc")
        s_pre = sem("s_pre")
        s_comb = sem("s_comb")
        s_nd = sem("s_nd")
        s_y = sem("s_y")
        s_rtr = sem("s_rtr")
        s_rev = sem("s_rev")
        s_lgmm = sem("s_lgmm")
        s_lgT = sem("s_lgT")
        s_lgtr = sem("s_lgtr")
        s_lg = sem("s_lg")
        s_ytr = sem("s_ytr")
        s_ytok = sem("s_ytok")
        s_g = sem("s_g")
        s_u = sem("s_u")
        s_tanh = sem("s_tanh")
        s_h = sem("s_h")
        s_down = sem("s_down")
        s_dn = sem("s_dn")
        s_res = sem("s_res")
        s_stat = sem("s_stat")
        s_oh = sem("s_oh")
        s_cum = sem("s_cum")
        s_pos = sem("s_pos")
        s_score = sem("s_score")
        s_scaled = sem("s_scaled")
        s_scat = sem("s_scat")
        s_tab = sem("s_tab")
        s_wsum = sem("s_wsum")
        s_wtot = sem("s_wtot")
        s_sq = sem("s_sq")
        s_rms = sem("s_rms")
        s_wl = sem("s_wl")
        s_xe = [sem("s_xe0"), sem("s_xe1")]
        s_xetr = sem("s_xetr")
        s_xeT = sem("s_xeT")
        s_eg = sem("s_eg")
        s_eu = sem("s_eu")
        s_et = sem("s_et")
        s_eh = sem("s_eh")
        s_ehtr = sem("s_ehtr")
        s_ehT = sem("s_ehT")
        s_eo = sem("s_eo")
        s_oe = sem("s_oe")
        s_ost = [sem("s_ost0"), sem("s_ost1")]
        s_wr = [sem("s_wr0"), sem("s_wr1")]
        s_tern = sem("s_tern")
        s_wtr = sem("s_wtr")
        s_wT = sem("s_wT")
        s_alone = sem("s_alone")
        s_mo = [sem(f"s_mo{j}") for j in range(4)]
        s_x1 = sem("s_x1")
        s_t1 = sem("s_t1")
        s_q1 = sem("s_q1")
        s_q1tr = sem("s_q1tr")
        s_q1T = sem("s_q1T")
        s_hh = sem("s_hh")
        s_gelu = sem("s_gelu")
        s_sc1 = sem("s_sc1")
        s_y1 = sem("s_y1")
        s_amax = sem("s_amax")
        s_rnd = sem("s_rnd")
        s_q2 = sem("s_q2")
        s_q2tr = sem("s_q2tr")
        s_q2Ta = sem("s_q2Ta")
        s_q2Tv = sem("s_q2Tv")
        s_out = sem("s_out")
        s_fin = sem("s_fin")
        s_store = [sem("s_store0"), sem("s_store1")]
        s_vstep = sem("s_vstep")
        s_gstep = sem("s_gstep")
        s_astep = sem("s_astep")
        N_CONST = 13

        def late(a, n):
            return wexp[:, a * 512:(a + n) * 512]
        gel = late(0, 8).rearrange("p (a f) -> p a f", a=2)
        t1 = late(8, 2).rearrange("p (a c) -> p a c", a=2)
        y1 = late(10, 1)
        q1 = late(11, 1).bitcast(BF16).rearrange("p (a c) -> p a c", a=2)
        q1T = late(12, 1).bitcast(BF16).rearrange("p (a k t) -> p a k t", a=2, k=KC)
        q2 = late(13, 2).bitcast(BF16)
        q2T = late(15, 2).bitcast(BF16).rearrange("p (g t) -> p g t", g=KG)
        fin = late(17, 2).rearrange("p (a c) -> p a c", a=2)
        HPS = bank[0:4]
        QPS = bank[4][:, :].bitcast(BF16)
        TPS = [bank[5][:, :].bitcast(BF16), bank[6][:, :].bitcast(BF16)]
        OPS = bank[7]

        WPS = [KPS[:, :].bitcast(BF16), MPS[:, :].bitcast(BF16)]

        def route_1(dve, st, v_):
            def one(ins):
                st.mark(ins)
                st.settle()
            t_e = [P, NT, E]
            f = lambda k: rt[:, k, :].rearrange("p (t e) -> p t e", e=E)
            dve.wait_ge(s_lg, B)
            v_.tensor_reduce(score[:], lg[:, :, :], AX.X, ALU.max).then_inc(s_score, 1)
            dve.wait_ge(s_score, 1)
            st.mark(v_.tensor_tensor(out=f(0), in0=lg[:, :, :], in1=score[:].unsqueeze(2).to_broadcast(t_e),
                                     op=ALU.is_equal))
            st.settle()
            one(v_.tensor_tensor(out=f(1), in0=f(0), in1=iota_e[:].unsqueeze(1).to_broadcast(t_e),
                                 op=ALU.mult))
            one(v_.tensor_reduce(rs[:, 0, 0:NT], f(1), AX.X, ALU.min))
            v_.tensor_tensor(out=f(5), in0=iota_e[:].unsqueeze(1).to_broadcast(t_e),
                             in1=rs[:, 0, 0:NT].unsqueeze(2).to_broadcast(t_e),
                             op=ALU.is_equal).then_inc(s_oh, 1)

        def route_2(dve, st, v_):
            def one(ins):
                st.mark(ins)
                st.settle()
            e_t = [P, E, NT]
            g = lambda k: rt[:, k, :].rearrange("p (e t) -> p e t", e=E)
            f = lambda k: rt[:, k, :].rearrange("p (t e) -> p t e", e=E)
            r = lambda k, n=E: rs[:, k, 0:n]
            dve.wait_ge(s_cum, 1)
            one(v_.tensor_copy(g(0), MPS[:, 256:384].rearrange("p (t e) -> p e t", e=E)))
            one(v_.tensor_tensor_scan(rt[:, 1, :], ones[:], rt[:, 0, :], 0.0, ALU.mult, ALU.add))
            one(v_.tensor_tensor(out=rt[:, 2, :], in0=rt[:, 1, :], in1=rt[:, 0, :], op=ALU.subtract))
            one(v_.tensor_reduce(r(0), g(0), AX.X, ALU.add))
            one(v_.tensor_tensor(out=g(3), in0=r(0).unsqueeze(2).to_broadcast(e_t),
                                 in1=iota_j[:].unsqueeze(1).to_broadcast(e_t), op=ALU.is_gt))
            one(v_.tensor_reduce(r(1), g(3), AX.X, ALU.add))
            one(v_.tensor_tensor_scan(r(2), ones[:, 0:E], r(1), 0.0, ALU.mult, ALU.add))
            one(v_.tensor_tensor(out=r(3), in0=r(2), in1=r(1), op=ALU.subtract))
            one(v_.scalar_tensor_tensor(out=r(4), in0=r(3), scalar=float(P), in1=g(2)[:, :, 0],
                                        op0=ALU.mult, op1=ALU.subtract))
            one(v_.tensor_tensor(out=g(4), in0=g(2), in1=r(4).unsqueeze(2).to_broadcast(e_t), op=ALU.add))
            one(v_.tensor_tensor(out=f(1), in0=rt[:, 4, :].rearrange("p (e t) -> p t e", e=E),
                                 in1=MPS[:, 128:256].rearrange("p (t e) -> p t e", e=E), op=ALU.add))
            one(v_.tensor_tensor(out=f(3), in0=f(1), in1=f(5), op=ALU.mult))
            one(v_.tensor_reduce(r(5, NT), f(3), AX.X, ALU.add))
            v_.tensor_copy(pos[:], r(5, NT)).then_inc(s_pos, 1)
            ends = rs[0:1, 2, 0:E - 1].unsqueeze(1).to_broadcast([1, 24, E - 1])
            one(v_.tensor_tensor(out=cmp3[:, 0, :, 0:E - 1],
                                 in0=iota_s[0:1, :].unsqueeze(2).to_broadcast([1, 24, E - 1]),
                                 in1=ends, op=ALU.is_ge))
            one(v_.tensor_tensor(out=cmp3[:, 1, :, 0:E - 1], in0=cmp3[:, 0, :, 0:E - 1],
                                 in1=sign_e[0:1, 0:E - 1].unsqueeze(1).to_broadcast([1, 24, E - 1]),
                                 op=ALU.mult))
            one(v_.tensor_reduce(tabf[:, 0:2, 0:24], cmp3[:, :, :, 0:E - 1], AX.X, ALU.add))
            st.mark(v_.tensor_scalar(tabi[:, 0, 0:24], tabf[:, 0, 0:24], 48.0, 48.0, ALU.mult, ALU.add))
            st.mark(v_.tensor_scalar(tabi[:, 1, 0:24], tabf[:, 1, 0:24], float(WE), None, ALU.mult))
            st.mark(v_.tensor_scalar(tabi[:, 2, 0:E], rs[0:1, 2, 0:E], 1.0, None, ALU.add))
            st.settle()
            dve.sem_inc(s_tab, 1)

        block = ctx.enter_context(nc.Block())

        @block.sync
        def _(sp):
            sp.dma_start(fk[:, 0], f_v[0, :, :, 0:P]).then_inc(s_f[0], 16)
            sp.dma_start(xk[:, 0], x_v[0, :, :, 0:P]).then_inc(s_x[0], 16)
            with nc.allow_non_contiguous_dma(reason="vectors of 512 channels"):
                for j, v in enumerate((w0, u0, w1c, u1c)):
                    sp.dma_start(par[:, j, :], v.rearrange("(k p) -> p k", p=P)).then_inc(s_par, 16)
                sp.dma_start(cnd, cond.unsqueeze(0).to_broadcast([P, B, TD])).then_inc(s_par, 16)
                sp.dma_start(rw[:, :, :], router_w.rearrange("(k p) e -> p k e", p=P)).then_inc(s_par, 16)
            for n in range(NCH):
                if n + 1 < NCH:
                    m = n + 1
                    b, c = m // KC, m % KC
                    if m >= 2:
                        sp.wait_ge(s_ktr, m - 1)
                        sp.wait_ge(s_xtr, m - 1)
                    sp.dma_start(fk[:, m % 2], f_v[b, :, :, c * P:(c + 1) * P]).then_inc(s_f[m % 2], 16)
                    sp.dma_start(xk[:, m % 2], x_v[b, :, :, c * P:(c + 1) * P]).then_inc(s_x[m % 2], 16)
                for j, src in enumerate((w1_v[n], w2_v[n // 4, :, (n % 4) * 512:(n % 4 + 1) * 512])):
                    if n >= 1:
                        sp.wait_ge(s_stat, 2 * (n - 1) + j + 1)
                    sp.dma_start(wstat_in[:, j], src).then_inc(s_ws[j], 16)
                if n == 0:
                    for j, src in enumerate((sh_gate, sh_up, sh_down)):
                        sp.dma_start(wsh[:, j], src.rearrange("(k p) f -> p k f", p=P)).then_inc(s_wsh, 16)
                if n == 2:
                    for b in range(B):
                        sp.dma_start(resid[:, b * TQ * C:(b + 1) * TQ * C].rearrange("p (q c) -> p q c", q=TQ),
                                     x_v[b]).then_inc(s_resid, 16)
                if n == 3:
                    sp.wait_ge(s_const, N_CONST)
                if n >= 3 and n < 3 + 12:
                    for s in range(2 * (n - 3), 2 * (n - 3) + 2):
                        sp.dma_start(rows_v[s], zero).then_inc(s_zero, 16)
            for e in range(E):
                dst = wexp[:, (e % 2) * WE:(e % 2 + 1) * WE].rearrange("p (m k f) -> p m k f", m=3, k=KC)
                if e == 1:
                    for m in (NCH, NCH + 1):
                        sp.wait_ge(s_ktr, m - 1)
                        sp.dma_start(fk[:, m % 2], f_v[0, :, :, m % KC * P:(m % KC + 1) * P]
                                     ).then_inc(s_f[m % 2], 16)
                    sp.wait_ge(s_xtr, NCH)
                    for u in range(8):
                        if u >= 2:
                            sp.wait_ge(s_tern, u - 1)
                        sp.dma_start(wraw_a[:, u % 2], w1_v[u]).then_inc(s_wr[u % 2], 16)
                    sp.wait_ge(s_down, NT)
                if e == 2:
                    sp.wait_ge(s_tab, 1)
                if e >= 2:
                    tiles = sp.value_load(tabi[0:1, 2, e - 2:e - 1], min_val=1, max_val=NS + 1)
                    sp.wait_ge(s_eo, tiles)
                for j, src in enumerate((gate_w, up_w, down_w)):
                    sp.dma_start(dst[:, j], src[e].rearrange("(k p) f -> p k f", p=P)).then_inc(s_wl, 16)
                sp.wait_ge(s_wl, 48 * (e + 1))
            with sp.Fori(0, NT // 2) as i:
                for a in range(2):
                    sp.wait_ge(s_fin, i * 2 + (a + 2))
                    sp.dma_start(out_v[bass.ds(i * 2 + a, 1)].rearrange("o p c -> (o p) c"),
                                 fin[:, a]).then_inc(s_store[a], 16)
            for a in range(2):
                sp.wait_ge(s_store[a], 16 * (NT // 2 + 1))

        @block.gpsimd
        def _(pool):
            st = Steps(pool, s_gstep)
            g = nc.gpsimd
            g.memset(ident[:], 0.0).then_inc(s_const, 1)
            g.memset(ones[:], 1.0).then_inc(s_const, 1)
            g.memset(bwd_n[:, T:T + 1], 0.0).then_inc(s_const, 1)
            g.memset(bwd_d[:, T:T + 1], 0.0).then_inc(s_const, 1)
            g.memset(zero, 0.0).then_inc(s_const, 1)
            pool.wait_ge(s_const, 5)
            g.affine_select(out=ident[:], in_=ident[:], compare_op=ALU.not_equal, fill=1.0, base=0,
                            pattern=[[-1, P]], channel_multiplier=1).then_inc(s_const, 1)
            g.affine_select(out=upper, in_=ones[:], compare_op=ALU.is_gt, fill=0.0, base=0,
                            pattern=[[1, P]], channel_multiplier=-1).then_inc(s_const, 1)
            g.iota(iota_e[:], pattern=[[1, E]], base=-E, channel_multiplier=0,
                   allow_small_or_imprecise_dtypes=True).then_inc(s_const, 1)
            g.iota(iota_j[:], pattern=[[P, NT]], base=0, channel_multiplier=0,
                   allow_small_or_imprecise_dtypes=True).then_inc(s_const, 1)
            g.iota(iota_s[:], pattern=[[1, 24]], base=0, channel_multiplier=0,
                   allow_small_or_imprecise_dtypes=True).then_inc(s_const, 1)
            g.iota(sign_e[:], pattern=[[0, E // 2], [-2, 2]], base=1, channel_multiplier=0,
                   allow_small_or_imprecise_dtypes=True).then_inc(s_const, 1)
            g.memset(magic[:], MAGIC).then_inc(s_const, 1)
            pool.wait_ge(s_const, 6)
            g.tensor_copy(identb[:], ident[:]).then_inc(s_const, 1)

            def alone():
                pool.sem_inc(s_alone, 1)

            def products(n, p):
                pool.wait_ge(s_kexp, n + 1)
                g.tensor_tensor(out=ekv[:, p], in0=kk[:, p, 0], in1=ksb[:, p], op=ALU.mult).then_inc(s_pre, 1)
                pool.wait_ge(s_pre, n + 1)
                st.mark(g.tensor_tensor(out=ksb[:, p], in0=kk[:, p, 1], in1=ksb[:, p], op=ALU.mult))

            def sums(n, p):
                pool.wait_ge(s_comb, n + 1)
                st.settle()
                st.mark(g.tensor_tensor(out=den[:, p], in0=den[:, p], in1=kk[:, p, 1], op=ALU.add))
                st.settle()
                g.tensor_tensor(out=num[:, p], in0=num[:, p], in1=ksb[:, p], op=ALU.add).then_inc(s_nd, 1)

            for z in range(STEPS_A):
                if z < NCH:
                    products(z, z % 2)
                if 1 <= z <= NCH:
                    sums(z - 1, (z - 1) % 2)
                if z == 18:
                    pool.wait_ge(s_zero, 16 * (NS + 1))
                    pool.wait_ge(s_pos, 1)
                    for t in range(NT):
                        pool.wait_ge(s_scaled, t + 1)
                        g.indirect_dma_start(slot_rows[:, :],
                                             bass.IndirectOffsetOnAxis(ap=pos[:, t:t + 1], axis=0),
                                             ytok[:, t * C:(t + 1) * C], None).then_inc(s_scat, 16)
                if z >= 9:
                    m = z - 9
                    pool.wait_ge(s_dn, m + 1)
                    pool.wait_ge(s_resid, 16 * B)
                    g.tensor_tensor(out=resid[:, m * C:(m + 1) * C], in0=resid[:, m * C:(m + 1) * C],
                                    in1=dn_sb, op=ALU.add).then_inc(s_res, 1)

            for s in range(4):
                if s >= 1:
                    sums(NCH + s - 1, (s - 1) % 2)
                products(NCH + s, s % 2)
            with pool.Fori(1, 4) as i:
                st.enter(i, 4 * 2, 1)
                for c in range(KC):
                    sums(i * KC + (NCH + c - 1), (c + 1) % 2)
                    products(i * KC + (NCH + c), c % 2)
                st.leave(3)
            sums(2 * NCH - 1, 1)

            for a in range(2):
                pool.wait_ge(s_ost[a], 16 * ((NS + 1 - a) // 2 + 1))
            for t in range(NT + 3):
                if t < NT:
                    g.indirect_dma_start(resid[:, t * C:(t + 1) * C], None, slot_out[:, :],
                                         bass.IndirectOffsetOnAxis(ap=pos[:, t:t + 1], axis=0),
                                         compute_op=ALU.add).then_inc(s_mo[t % 4], 16)
                if t >= 3:
                    pool.wait_ge(s_mo[(t - 3) % 4], 16 * ((t - 3) // 4 + 1))
                    pool.sem_inc(s_x1, 1)

            with pool.Fori(0, NT // 2) as i:
                st.enter(i, 2)
                for a in range(2):
                    t = i * 2 + a
                    r = r1tok[:, bass.ds(t * C, C)]
                    pool.wait_ge(s_t1, t + 1)
                    alone()
                    st.mark(g.tensor_tensor(out=t1[:, a], in0=t1[:, a], in1=r, op=ALU.mult))
                    st.settle()
                    alone()
                    g.tensor_tensor(out=r, in0=r, in1=t1[:, a], op=ALU.add).then_inc(s_y1, 1)
                st.leave(NT // 2)

        @block.scalar
        def _(act):
            st = Steps(act, s_astep)
            a_ = nc.scalar.activation
            act.wait_ge(s_par, 96)
            act.wait_ge(s_tf, 1)
            a_(tf[:], dhalf[:], ACT.Sigmoid).then_inc(s_tf, 1)
            for l in range(2):
                st.mark(a_(ew[:, l], par[:, 2 * l], ACT.Exp))
            st.settle()
            a_(ew[:, :, :], ew[:, :, :], ACT.Exp, scale=-1.0).then_inc(s_tf, 1)

            def k_in(n, p):
                act.wait_ge(s_ktr, n + 1)
                if not isinstance(n, int) or n >= 2:
                    act.wait_ge(s_nd, n - 1)
                a_(ksb[:, p], KPS[:, :], ACT.Copy).then_inc(s_kcopy, 1)
                act.wait_ge(s_ukc, n + 1)
                a_(kk[:, p], kk[:, p], ACT.Exp).then_inc(s_kexp, 1)

            def r_out(n, b, c):
                act.wait_ge(s_rtr, n - (NCH - 1))
                act.wait_ge(s_scat, 16 * NT)
                a_(r1tok[:, bass.ds(b * (TQ * C), TQ * C)].rearrange("p (q c) -> p q c", q=TQ)
                   [:, :, c * P:(c + 1) * P], YPS[:, :].rearrange("p (q c) -> p q c", q=TQ),
                   ACT.Copy).then_inc(s_rev, 1)

            def x_tanh(n):
                act.wait_ge(s_xtr, n + 1)
                if n >= 2:
                    act.wait_ge(s_y, n - 1)
                a_(tx[:, n % 2], XPS[:, :], ACT.Tanh, scale=0.5).then_inc(s_tx, 1)

            for z in range(STEPS_A):
                if z < NCH:
                    n = z
                    k_in(n, n % 2)
                    x_tanh(n)
                    for j in range(2):
                        act.wait_ge(s_ws[j], 16 * (n + 1))
                        if n or j:
                            act.wait_ge(s_stat, 2 * n + j)
                        a_(junk, wstat_in[:, j], ACT.Square,
                           accum_out=wstat[:, j, n:n + 1]).then_inc(s_stat, 1)
                if z >= 9:
                    m = z - 9
                    act.wait_ge(s_down, m + 1)
                    if m:
                        act.wait_ge(s_res, m)
                    a_(dn_sb, DPS[:, :], ACT.Copy).then_inc(s_dn, 1)
                if 5 <= z < 21:
                    k = z - 5
                    if k % 4 == 0:
                        act.wait_ge(s_lgmm, k // 4 + 1)
                        if k:
                            act.wait_ge(s_lgtr, k // 4)
                        a_(lgT, LPS[0:E, :], ACT.Copy).then_inc(s_lgT, 1)
                    act.wait_ge(s_g, k + 1)
                    if k:
                        act.wait_ge(s_h, k)
                    a_(gtanh, GPS[:, :], ACT.Tanh, scale=0.5).then_inc(s_tanh, 1)
                    for q in ytok_tiles(z):
                        act.wait_ge(s_ytr, q + 1)
                        a_(ytok[:, q * C:(q + 1) * C], YPS[:, :], ACT.Copy).then_inc(s_ytok, 1)
                if z == 17:
                    act.wait_ge(s_oh, 1)
                    a_(score[:], score[:], ACT.Sigmoid).then_inc(s_score, 1)
                    act.wait_ge(s_score, 2)
                    act.wait_ge(s_ytok, NT)
                    for t in range(NT):
                        a_(ytok[:, t * C:(t + 1) * C], ytok[:, t * C:(t + 1) * C], ACT.Copy,
                           scale=score[:, t:t + 1]).then_inc(s_scaled, 1)
                if z == 19:
                    act.wait_ge(s_sq, 1)
                    a_(wq[:, :, 1:2], wq[:, :, 0:1], ACT.Sqrt).then_inc(s_sq, 1)

            def xe_load(s, p):
                act.wait_ge(s_xetr, s + 1)
                act.dma_start(xe[:, p], rows_v[bass.ds(s, 1)].rearrange("o p c -> (o p) c")
                              ).then_inc(s_xe[p], 16)

            def xe_copy(s, p):
                act.wait_ge(s_xetr, s + 3)
                act.wait_ge(s_eu, s + 1)
                a_(xeT[:, p].rearrange("p k t -> p (k t)"), XPS[:, :], ACT.Copy).then_inc(s_xeT, 1)

            def e_tanh(s):
                act.wait_ge(s_eg, s + 1)
                act.wait_ge(s_eh, s + 1)
                a_(gtanh, GPS[:, :], ACT.Tanh, scale=0.5).then_inc(s_et, 1)

            def he_copy(s):
                act.wait_ge(s_ehtr, s + 2)
                act.wait_ge(s_eo, s + 1)
                a_(heT.rearrange("p k t -> p (k t)"), LPS[:, :], ACT.Copy).then_inc(s_ehT, 1)

            def o_copy(s, p, k):
                act.wait_ge(s_eo, s + 2)
                act.wait_ge(s_ost[p], k * 16 + 16)
                a_(oE[:, p], DPS[:, :], ACT.Copy).then_inc(s_oe, 1)
                act.wait_ge(s_oe, s + 2)
                act.dma_start(moe_v[bass.ds(s, 1)].rearrange("o p c -> (o p) c"), oE[:, p]
                              ).then_inc(s_ost[p], 16)

            act.wait_ge(s_scat, 16 * NT)
            act.sem_inc(s_oe, 1)
            act.sem_inc(s_ehT, 1)
            for p in range(2):
                act.sem_inc(s_ost[p], 16)
            for p in range(2):
                xe_load(p, p)
            for p in range(2):
                xe_copy(p, p)
            e_tanh(0)

            def e_step(s, p, k, chunk=None, ratio=None, fetch=True, last=False, units=()):
                if chunk:
                    n, b, c = chunk
                    if not isinstance(n, int) or n >= NCH + 2:
                        act.wait_ge(s_ktr, n - 1)
                        act.dma_start(fk[:, p], f_v[bass.ds(b, 1), :, :, c * P:(c + 1) * P
                                                    ].rearrange("o p q c -> (o p) q c")).then_inc(s_f[p], 16)
                if fetch:
                    xe_load(s + 2, p)
                if ratio:
                    r_out(*ratio)
                for u in units[0:2]:
                    unit_load(u)
                if not last:
                    e_tanh(s + 1)
                if chunk:
                    k_in(n, p)
                he_copy(s)
                if fetch:
                    xe_copy(s + 2, p)
                for u in units[2:4]:
                    unit_load(u)
                o_copy(s, p, k)

            def unit_load(u):
                act.wait_ge(s_tern, u - 1)
                src = w1_v[u] if u < NT else w2_v[(u - NT) // 4, :, (u - NT) % 4 * 512:((u - NT) % 4 + 1) * 512]
                act.dma_start(wraw_e[:, u % 2], src).then_inc(s_wr[u % 2], 16)

            for s in range(4):
                e_step(s, s % 2, s // 2, (NCH + s, 0, s), (NCH, 0, 0) if s == 3 else None)
            with act.Fori(1, 4) as i:
                for c in range(KC):
                    e_step(i * KC + c, c % 2, i * 2 + c // 2, (i * KC + (NCH + c), i, c),
                           (i * KC + (NCH + c - 3), i + (c + 1) // KC - 1, (c + 1) % KC))
            act.wait_ge(s_ktr, 2 * NCH)
            for s in range(NT, NS):
                n = NCH + s - 3
                e_step(s, s % 2, s // 2, None, (n, B - 1, n % KC) if n < 2 * NCH else None,
                       s + 2 < NS, s == NS - 1, units_at(s))

            def tanh_1(t, a):
                act.wait_ge(s_x1, t + 1)
                if not isinstance(t, int) or t >= 2:
                    act.wait_ge(s_y1, t - 1)
                a_(t1[:, a], resid[:, bass.ds(t * C, C)], ACT.Tanh, scale=0.5).then_inc(s_t1, 1)

            def q1T_copy(t, a):
                act.wait_ge(s_q1tr, t + 2)
                act.wait_ge(s_hh, t * 4 + 4)
                a_(q1T[:, a].rearrange("p k t -> p (k t)"), QPS[:, 0:512], ACT.Copy).then_inc(s_q1T, 1)

            def gelu(t, a, j):
                act.wait_ge(s_q2, t * 2 + 1)
                act.wait_ge(s_hh, t * 4 + (j + 9))
                a_(gel[:, a, j * 512:(j + 1) * 512], HPS[j][:, :], ACT.Gelu,
                   scale=sc[:, a, 4:5]).then_inc(s_gelu, 1)

            def scale_2(t, a):
                act.wait_ge(s_amax, t + 1)
                for h in range(2):
                    a_(gel[:, a, h * 1024:(h + 1) * 1024], gel[:, a, h * 1024:(h + 1) * 1024], ACT.Identity,
                       scale=sc[:, a, 6:7], bias=magic[:, 0:1]).then_inc(s_rnd, 1)

            def q2T_half(t):
                act.wait_ge(s_q2tr, t + 2)
                act.wait_ge(s_out, t + 1)
                a_(q2T[:, 0:8].rearrange("p g t -> p (g t)"), TPS[0], ACT.Copy).then_inc(s_q2Ta, 1)

            tanh_1(0, 0)
            tanh_1(1, 1)
            q1T_copy(0, 0)
            for j in range(4):
                gelu(0, 0, j)
            scale_2(0, 0)

            def step_1(t, a, more, most):
                if more:
                    q1T_copy(t + 1, 1 - a)
                    gelu(t + 1, 1 - a, 0)
                    gelu(t + 1, 1 - a, 1)
                q2T_half(t)
                if more:
                    gelu(t + 1, 1 - a, 2)
                    gelu(t + 1, 1 - a, 3)
                if most:
                    tanh_1(t + 2, a)
                if more:
                    scale_2(t + 1, 1 - a)

            with act.Fori(0, 7) as i:
                for a in range(2):
                    step_1(i * 2 + a, a, True, True)
            step_1(14, 0, True, False)
            step_1(15, 1, False, False)

        @block.tensor
        def _(pe):
            pe.sem_inc(s_xetr, 2)
            pe.sem_inc(s_eu, 2)
            pe.sem_inc(s_eh, 1)
            pe.sem_inc(s_ehtr, 1)
            pe.sem_inc(s_eo, 1)
            pe.wait_ge(s_const, N_CONST)
            mm, tr = nc.tensor.matmul, nc.tensor.transpose

            def four(out, src, idt, done):
                for q in range(4):
                    last = tr(out[:, q * P:(q + 1) * P], src(q), idt)
                last.then_inc(done, 1)

            def k_tr(n, p, count):
                pe.wait_ge(s_f[p], count)
                if not isinstance(n, int) or n >= 1:
                    pe.wait_ge(s_kcopy, n)
                four(KPS, lambda q: fk[:, p, q, :], ident[:], s_ktr)

            def r_tr(n, p):
                pe.wait_ge(s_y, n + 1)
                if not isinstance(n, int):
                    pe.wait_ge(s_rev, n - NCH)
                elif n > NCH:
                    pe.wait_ge(s_rev, n - NCH)
                four(YPS, lambda q: num[:, p, q * P:(q + 1) * P], ident[:], s_rtr)

            def w_tr(u):
                pe.wait_ge(s_tern, u + 1)
                if u >= 2:
                    pe.wait_ge(s_wT, u - 1)
                four(WPS[u % 2], lambda q: wtern[:, u % 2, q * P:(q + 1) * P], identb[:], s_wtr)

            for z in range(STEPS_A):
                if z < NCH:
                    n = z
                    k_tr(n, n % 2, 16 * (n // 2 + 1))
                    pe.wait_ge(s_x[n % 2], 16 * (n // 2 + 1))
                    if n:
                        pe.wait_ge(s_tx, n)
                    four(XPS, lambda q: xk[:, n % 2, q, :], ident[:], s_xtr)
                if z >= 9:
                    m = z - 9
                    pe.wait_ge(s_h, 4 * (m // 4 + 1))
                    if m:
                        pe.wait_ge(s_dn, m)
                    for j in range(KF):
                        last = mm(DPS[:, :], shT[:, m // 4 % 2, j, m % 4 * P:(m % 4 + 1) * P], wsh[:, 2, j, :],
                                  start=j == 0, stop=j == KF - 1)
                    last.then_inc(s_down, 1)
                if 5 <= z < 21:
                    b, c = (z - 5) // 4, (z - 5) % 4
                    yb = y0T[:, b % 2]
                    if c == 0:
                        pe.wait_ge(s_y, 4 * (b + 1))
                        pe.wait_ge(s_par, 96)
                        if b:
                            pe.wait_ge(s_lgT, b)
                        for k in range(KC):
                            last = mm(LPS[0:E, :], rw[:, k, :], yb[:, k, :], start=k == 0, stop=k == KC - 1)
                        last.then_inc(s_lgmm, 1)
                    pe.wait_ge(s_wsh, 48)
                    if z > 5:
                        pe.wait_ge(s_h, z - 5)
                    for m_, ps, done in ((0, GPS, s_g), (1, UPS, s_u)):
                        for k in range(KC):
                            last = mm(ps[:, :], wsh[:, m_, k, c * P:(c + 1) * P], yb[:, k, :],
                                      start=k == 0, stop=k == KC - 1)
                        last.then_inc(done, 1)
                    if c == 0:
                        pe.wait_ge(s_lgT, b + 1)
                        if b:
                            pe.wait_ge(s_lg, b)
                        for q in range(4):
                            last = tr(MPS[:, q * E:(q + 1) * E], lgT[:, q * P:(q + 1) * P], ident[0:E, 0:E])
                        last.then_inc(s_lgtr, 1)
                    for t in ytok_tiles(z):
                        if t:
                            pe.wait_ge(s_ytok, t)
                        four(YPS, lambda k: yb[:, k, t % 4 * P:(t % 4 + 1) * P], ident[:], s_ytr)
                if z == 17:
                    pe.wait_ge(s_oh, 1)
                    mm(MPS[:, 128:256], upper, rt[:, 5, :], start=True, stop=True)
                    mm(MPS[:, 256:384], ones[:], rt[:, 5, :], start=True, stop=True).then_inc(s_cum, 1)
                if z == 18:
                    pe.wait_ge(s_wsum, 1)
                    mm(MPS[:, 384:386], ones[:], wsum[:], start=True, stop=True).then_inc(s_wtot, 1)
                for u in units_in_a(z):
                    w_tr(u)

            def e_in(s, p, k):
                pe.wait_ge(s_xe[p], k * 16 + 16)
                if not isinstance(s, int) or s >= 1:
                    pe.wait_ge(s_xeT, s)
                four(XPS, lambda q: xe[:, p, q * P:(q + 1) * P], ident[:], s_xetr)

            def e_gate_up(s, p):
                loads = pe.value_load(tabi[0:1, 0, bass.ds(s, 1)], min_val=48, max_val=48 * E)
                at = pe.value_load(tabi[0:1, 1, bass.ds(s, 1)], min_val=0, max_val=WE)
                pe.wait_ge(s_wl, loads)
                pe.wait_ge(s_xeT, s + 1)
                pe.wait_ge(s_eh, s + 1)
                for m_, ps, done in ((0, GPS, s_eg), (1, UPS, s_eu)):
                    for k in range(KC):
                        last = mm(ps[:, :], xeT[:, p, k, :], wexp[:, bass.ds(at + (m_ * KC + k) * F, F)],
                                  start=k == 0, stop=k == KC - 1)
                    last.then_inc(done, 1)

            def e_h(s, p):
                pe.wait_ge(s_eh, s + 2)
                pe.wait_ge(s_ehT, s + 1)
                four(LPS, lambda q: hE[p][:, q * P:(q + 1) * P], ident[:], s_ehtr)

            def e_down(s):
                at = pe.value_load(tabi[0:1, 1, bass.ds(s, 1)], min_val=0, max_val=WE)
                pe.wait_ge(s_ehT, s + 2)
                pe.wait_ge(s_oe, s + 1)
                for j in range(KF):
                    last = mm(DPS[:, :], heT[:, j, :], wexp[:, bass.ds(at + (2 * KC + j) * F, F)],
                              start=j == 0, stop=j == KF - 1)
                last.then_inc(s_eo, 1)

            pe.wait_ge(s_tab, 1)
            e_in(0, 0, 0)
            e_in(1, 1, 0)
            e_gate_up(0, 0)
            pe.wait_ge(s_wT, 8)

            def e_step(s, p, k, chunk=None, ratio=None, fetch=True, last=False, units=()):
                if ratio is not None:
                    r_tr(*ratio)
                if not last:
                    e_gate_up(s + 1, 1 - p)
                if chunk:
                    k_tr(*chunk)
                for u in units[0:2]:
                    w_tr(u)
                e_h(s, p)
                if fetch:
                    e_in(s + 2, p, k + 1)
                e_down(s)
                for u in units[2:4]:
                    w_tr(u)

            for s in range(4):
                e_step(s, s % 2, s // 2, (NCH + s, s % 2, 16 * ((NCH + s) // 2 + 1)),
                       (NCH, 0) if s == 3 else None)
            with pe.Fori(1, 4) as i:
                for c in range(KC):
                    e_step(i * KC + c, c % 2, i * 2 + c // 2,
                           (i * KC + (NCH + c), c % 2, i * 32 + 16 * ((NCH + c) // 2 + 1)),
                           (i * KC + (NCH + c - 3), (c + 1) % 2))
            for s in range(NT, NS):
                n = NCH + s - 3
                e_step(s, s % 2, s // 2, None, (n, n % 2) if n < 2 * NCH else None,
                       s + 2 < NS, s == NS - 1, units_at(s))

            def q1_tr(t, a):
                pe.wait_ge(s_q1, t + 1)
                pe.wait_ge(s_q1T, t + 1)
                four(QPS, lambda q: q1[:, a, q * P:(q + 1) * P], identb[:], s_q1tr)
                pe.wait_ge(s_q1T, t + 2)

            def hidden(t, a, j):
                pe.wait_ge(s_gelu, t * 4 + (j + 1))
                for k in range(KC):
                    last = mm(HPS[j][:, :], q1T[:, a, k, :], w1T[:, k, j * 512:(j + 1) * 512],
                              start=k == 0, stop=k == KC - 1)
                last.then_inc(s_hh, 1)

            def q2_tr(t):
                pe.wait_ge(s_q2, t * 2 + 6)
                pe.wait_ge(s_q2Ta, t + 1)
                pe.wait_ge(s_q2Tv, t + 1)
                for g in range(KG):
                    last = tr(TPS[g // 8][:, g % 8 * P:(g % 8 + 1) * P], q2[:, g * P:(g + 1) * P], identb[:])
                last.then_inc(s_q2tr, 1)

            def result(t):
                pe.wait_ge(s_q2Ta, t + 2)
                pe.wait_ge(s_q2Tv, t + 2)
                pe.wait_ge(s_fin, t + 1)
                for g in range(KG):
                    last = mm(OPS[:, :], q2T[:, g, :], w2T[:, g, :], start=g == 0, stop=g == KG - 1)
                last.then_inc(s_out, 1)

            pe.wait_ge(s_wT, NU)
            q1_tr(0, 0)
            for j in range(4):
                hidden(0, 0, j)

            def step_1(t, a, more):
                if more:
                    q1_tr(t + 1, 1 - a)
                    hidden(t + 1, 1 - a, 0)
                    hidden(t + 1, 1 - a, 1)
                q2_tr(t)
                if more:
                    hidden(t + 1, 1 - a, 2)
                    hidden(t + 1, 1 - a, 3)
                result(t)

            with pe.Fori(0, 7) as i:
                for a in range(2):
                    step_1(i * 2 + a, a, True)
            step_1(14, 0, True)
            step_1(15, 1, False)

        @block.vector
        def _(dve):
            st = Steps(dve, s_vstep)
            v_ = nc.vector
            for s_, k in ((s_q1tr, 1), (s_q1T, 1), (s_hh, 8), (s_gelu, 4), (s_q2, 4),
                          (s_q2tr, 1), (s_q2Ta, 1), (s_q2Tv, 1), (s_out, 1), (s_fin, 1),
                          (s_store[0], 16), (s_store[1], 16)):
                dve.sem_inc(s_, k)
            dve.wait_ge(s_par, 96)
            v_.tensor_reduce(dhalf[:], cnd, AX.X, ALU.add).then_inc(s_tf, 1)
            dve.wait_ge(s_tf, 3)
            st.mark(v_.tensor_scalar(dhalf[:], tf[:], 0.5, 0.5, ALU.mult, ALU.add))
            st.mark(v_.tensor_scalar(osh[:], tf[:], 0.1, 0.4, ALU.mult, ALU.add))
            st.settle()
            for l in range(2):
                for c in range(KC):
                    st.mark(v_.tensor_scalar(dec[:, l, c, :], dhalf[:], ew[:, l, c:c + 1], None, ALU.mult))
            st.settle()
            dve.wait_ge(s_const, N_CONST)

            def guards(n, p, l, c):
                dve.wait_ge(s_kcopy, n + 1)
                st.mark(v_.tensor_scalar(kk[:, p, 0], ksb[:, p], 30.0, None, ALU.min))
                v_.tensor_scalar(kk[:, p, 1], ksb[:, p], par[:, 2 * l + 1, c:c + 1], 30.0,
                                 ALU.add, ALU.min).then_inc(s_ukc, 1)

            def scans(n, p, l, c, b):
                dve.wait_ge(s_pre, n + 1)
                if not isinstance(n, int) or n >= 1:
                    dve.wait_ge(s_comb, n)
                if not isinstance(n, int) or n >= 2:
                    dve.wait_ge(s_y, n - 1)
                if not isinstance(n, int) or n >= NCH + 2:
                    dve.wait_ge(s_rtr, n - (NCH + 1))
                d1 = dec[:, l, c, bass.ds(b, 1)]
                d = d1.to_broadcast([P, T])
                for sums_, bwd, src in ((den, bwd_d, kk[:, p, 0]), (num, bwd_n, ekv[:, p])):
                    st.mark(v_.tensor_tensor_scan(sums_[:, p], d, src, 0.0, ALU.mult, ALU.add))
                    st.mark(v_.tensor_tensor_scan(bwd[:, 0:T][:, ::-1], d, src[:, ::-1], 0.0,
                                                  ALU.mult, ALU.add))
                st.settle()
                st.mark(v_.scalar_tensor_tensor(out=den[:, p], in0=bwd_d[:, 1:T + 1], scalar=d1,
                                                in1=den[:, p], op0=ALU.mult, op1=ALU.add))
                st.settle()
                v_.scalar_tensor_tensor(out=num[:, p], in0=bwd_n[:, 1:T + 1], scalar=d1,
                                        in1=num[:, p], op0=ALU.mult, op1=ALU.add).then_inc(s_comb, 1)

            def ratio(n, p, l, b):
                dve.wait_ge(s_nd, n + 1)
                st.mark(v_.tensor_scalar(den[:, p], den[:, p], 1e-8, None, ALU.max))
                st.settle()
                st.mark(v_.reciprocal(den[:, p], den[:, p]))
                st.settle()
                o = osh[:, bass.ds(b, 1)]
                ins = v_.scalar_tensor_tensor(out=num[:, p], in0=num[:, p], scalar=o, in1=den[:, p],
                                              op0=ALU.mult, op1=ALU.mult)
                if l:
                    ins.then_inc(s_y, 1)
                    return
                st.mark(ins)
                st.settle()
                dve.wait_ge(s_tx, n + 1)
                if b >= 2:
                    dve.wait_ge(s_ytr, 4 * (b - 1))
                v_.scalar_tensor_tensor(out=y0T[:, b % 2, n % KC, :], in0=tx[:, p], scalar=1.0, in1=num[:, p],
                                        op0=ALU.add, op1=ALU.mult).then_inc(s_y, 1)

            def tern(u, raw):
                j, a = u // NT, u % 2
                dve.wait_ge(s_wr[a], 16 * (u // 2 + 1))
                if u:
                    dve.wait_ge(s_tern, u)
                st.mark(v_.tensor_scalar(above, raw[:, a], wq[:, j, 4:5], 0.5, ALU.mult, ALU.is_gt))
                st.mark(v_.tensor_scalar(below, raw[:, a], wq[:, j, 4:5], -0.5, ALU.mult, ALU.is_lt))
                st.settle()
                if u >= 2:
                    dve.wait_ge(s_wtr, u - 1)
                v_.tensor_tensor(out=wtern[:, a], in0=above, in1=below, op=ALU.subtract).then_inc(s_tern, 1)

            def w_out(u):
                dve.wait_ge(s_wtr, u + 1)
                src = WPS[u % 2][:, 0:512].rearrange("p (k t) -> p k t", k=4)
                if u < NT:
                    dst = w1T[:, :, u * P:(u + 1) * P]
                else:
                    r, v = (u - NT) // 4, (u - NT) % 4
                    dst = w2T[:, v * 4:(v + 1) * 4, r * P:(r + 1) * P]
                v_.tensor_copy(dst, src).then_inc(s_wT, 1)

            for z in range(STEPS_A):
                if z < NCH:
                    guards(z, z % 2, 0, z % KC)
                if 1 <= z <= NCH:
                    scans(z - 1, (z - 1) % 2, 0, (z - 1) % KC, (z - 1) // KC)
                if 5 <= z < 21:
                    b, c = (z - 5) // 4, (z - 5) % 4
                    dve.wait_ge(s_tanh, z - 4)
                    if z > 5:
                        dve.wait_ge(s_h, z - 5)
                    st.mark(v_.scalar_tensor_tensor(out=gt1, in0=gtanh, scalar=1.0, in1=GPS[:, :],
                                                    op0=ALU.add, op1=ALU.mult))
                    st.settle()
                    dve.wait_ge(s_u, z - 4)
                    if b >= 2:
                        dve.wait_ge(s_down, 4 * (b - 1))
                    v_.scalar_tensor_tensor(out=shT[:, b % 2, c, :], in0=gt1, scalar=0.5, in1=UPS[:, :],
                                            op0=ALU.mult, op1=ALU.mult).then_inc(s_h, 1)
                    if c == 0:
                        dve.wait_ge(s_lgtr, b + 1)
                        v_.tensor_copy(lg[:, 4 * b:4 * b + 4, :].rearrange("p t e -> p (t e)"),
                                       MPS[:, 0:4 * E]).then_inc(s_lg, 1)
                if 1 <= z <= NCH:
                    ratio(z - 1, (z - 1) % 2, 0, (z - 1) // KC)
                if z == 17:
                    route_1(dve, st, v_)
                    route_2(dve, st, v_)
                if z == 17:
                    v_.tensor_reduce(wsum[:], wstat[:, :, :], AX.X, ALU.add).then_inc(s_wsum, 1)
                if z == 18:
                    dve.wait_ge(s_wtot, 1)
                    v_.tensor_scalar(wq[:, :, 0:1], MPS[:, 384:386].rearrange("p (j o) -> p j o", o=1),
                                     1.0 / (FF * C), EPS, ALU.mult, ALU.max).then_inc(s_sq, 1)
                if z == 20:
                    w = lambda k: wq[:, :, k:k + 1]
                    def one(ins):
                        st.mark(ins)
                        st.settle()
                    dve.wait_ge(s_sq, 2)
                    one(v_.reciprocal(w(2), w(1)))
                    one(v_.tensor_tensor(out=w(3), in0=w(2), in1=w(2), op=ALU.mult))
                    one(v_.tensor_tensor(out=w(3), in0=w(3), in1=w(0), op=ALU.mult))
                    one(v_.tensor_scalar(w(3), w(3), -0.5, 1.5, ALU.mult, ALU.add))
                    one(v_.tensor_tensor(out=w(4), in0=w(3), in1=w(2), op=ALU.mult))
                    one(v_.reciprocal(w(5), w(4)))
                    v_.tensor_scalar(w(6), w(5), 1.0 / 127.0, None, ALU.mult).then_inc(s_rms, 1)
                us = list(units_in_a(z))
                for u in us:
                    tern(u, wraw_a)
                for u in us:
                    w_out(u)

            def e_silu(s, p):
                dve.wait_ge(s_et, s + 1)
                st.mark(v_.scalar_tensor_tensor(out=gt1, in0=gtanh, scalar=1.0, in1=GPS[:, :],
                                                op0=ALU.add, op1=ALU.mult))
                st.settle()
                dve.wait_ge(s_eu, s + 3)
                if not isinstance(s, int) or s >= 1:
                    dve.wait_ge(s_ehtr, s)
                v_.scalar_tensor_tensor(out=hE[p], in0=gt1, scalar=0.5, in1=UPS[:, :],
                                        op0=ALU.mult, op1=ALU.mult).then_inc(s_eh, 1)

            dve.wait_ge(s_zero, 16 * (NS + 1))
            e_silu(0, 0)

            def e_step(s, p, chunk=None, scan=None, done=None, last=False, units=()):
                if done:
                    ratio(*done)
                if scan:
                    scans(*scan)
                for u in units[0:2]:
                    tern(u, wraw_e)
                if not last:
                    e_silu(s + 1, 1 - p)
                for u in units[0:2]:
                    w_out(u)
                if chunk:
                    guards(*chunk)
                for u in units[2:4]:
                    tern(u, wraw_e)
                for u in units[2:4]:
                    w_out(u)

            for s in range(4):
                n = NCH + s
                e_step(s, s % 2, (n, s % 2, 1, s), (n - 1, (s - 1) % 2, 1, s - 1, 0) if s >= 1 else None,
                       (n - 2, s % 2, 1, 0) if s >= 2 else None)
            with dve.Fori(1, 4) as i:
                st.enter(i, 4 * (2 + 5 + 1 + 1), 1)
                for c in range(KC):
                    n = i * KC + (NCH + c)
                    e_step(i * KC + c, c % 2, (n, c % 2, 1, c),
                           (i * KC + (NCH + c - 1), (c + 1) % 2, 1, (c + 3) % KC, i + (c + 3) // KC - 1),
                           (i * KC + (NCH + c - 2), c % 2, 1, i + (c + 2) // KC - 1))
                st.leave(3)
            for s in range(NT, NS):
                e_step(s, s % 2, None, (2 * NCH - 1, 1, 1, KC - 1, B - 1) if s == NT else None,
                       (NCH + s - 2, s % 2, 1, B - 1) if s <= NT + 1 else None, s == NS - 1, units_at(s))

            def small(ins):
                st.mark(ins)
                st.settle()

            S = lambda a, j: sc[:, a, j:j + 1]

            def round_1(t, a):
                y = r1tok[:, bass.ds(t * C, C)]
                dve.wait_ge(s_y1, t + 1)
                small(v_.tensor_reduce(S(a, 0), y, AX.X, ALU.max, apply_absolute_value=True))
                small(v_.tensor_scalar(S(a, 0), S(a, 0), EPS, 1.0 / 127.0, ALU.max, ALU.mult))
                small(v_.reciprocal(S(a, 1), S(a, 0)))
                dve.wait_ge(s_gelu, t * 4)
                st.mark(v_.tensor_scalar(S(a, 4), S(a, 0), wq[:, 0, 5:6], None, ALU.mult))
                small(v_.tensor_scalar(y1, y, S(a, 1), MAGIC, ALU.mult, ALU.add))
                if not isinstance(t, int) or t >= 2:
                    dve.wait_ge(s_q1tr, t)
                v_.tensor_scalar(q1[:, a], y1, MAGIC, 127.0, ALU.subtract, ALU.min).then_inc(s_q1, 1)

            def largest(t, a):
                for h in range(2):
                    dve.wait_ge(s_gelu, t * 4 + (2 * h + 6))
                    st.mark(v_.tensor_reduce(S(a, 8 + h), gel[:, a, h * 1024:(h + 1) * 1024], AX.X, ALU.max,
                                             apply_absolute_value=True))
                st.settle()
                small(v_.tensor_tensor(out=S(a, 5), in0=S(a, 8), in1=S(a, 9), op=ALU.max))
                small(v_.tensor_scalar(S(a, 5), S(a, 5), EPS, 1.0 / 127.0, ALU.max, ALU.mult))
                dve.wait_ge(s_fin, t) if not isinstance(t, int) or t >= 1 else None
                st.mark(v_.tensor_scalar(S(a, 12), S(a, 5), wq[:, 1, 5:6], None, ALU.mult))
                v_.reciprocal(S(a, 6), S(a, 5)).then_inc(s_amax, 1)

            def round_2(t, a):
                for h in range(2):
                    dve.wait_ge(s_rnd, t * 2 + (h + 1))
                    dve.wait_ge(s_q2tr, t + 1)
                    v_.tensor_scalar(q2[:, h * 1024:(h + 1) * 1024], gel[:, a, h * 1024:(h + 1) * 1024],
                                     MAGIC, 127.0, ALU.subtract, ALU.min).then_inc(s_q2, 1)

            def finish(t, a, k):
                dve.wait_ge(s_out, t + 2)
                dve.wait_ge(s_store[a], k * 16 + 16)
                v_.scalar_tensor_tensor(out=fin[:, a], in0=OPS[:, :], scalar=S(a, 12),
                                        in1=resid[:, bass.ds(t * C, C)], op0=ALU.mult, op1=ALU.add
                                        ).then_inc(s_fin, 1)

            def q2T_half(t):
                dve.wait_ge(s_q2tr, t + 2)
                dve.wait_ge(s_out, t + 1)
                v_.tensor_copy(q2T[:, 8:16].rearrange("p g t -> p (g t)"), TPS[1]).then_inc(s_q2Tv, 1)

            dve.wait_ge(s_eo, NS + 1)
            round_1(0, 0)
            round_1(1, 1)
            largest(0, 0)

            def step_1(t, a, k, more, most):
                round_2(t, a)
                q2T_half(t)
                if most:
                    round_1(t + 2, a)
                if more:
                    largest(t + 1, 1 - a)
                finish(t, a, k)

            with dve.Fori(0, 7) as i:
                st.enter(i, 2 * (5 + 5))
                for a in range(2):
                    step_1(i * 2 + a, a, i, True, True)
                st.leave(7)
            step_1(14, 0, 7, True, False)
            step_1(15, 1, 7, False, False)


_INS = ['x', 'fside_BxSxS_0', 'cond_512', 'L0_cond_w', 'L0_cond_u', 'L0_ffn_router_w', 'L0_ffn_gate_w',
        'L0_ffn_up_w', 'L0_ffn_down_w', 'L0_ffn_shared_gate_w', 'L0_ffn_shared_up_w', 'L0_ffn_shared_down_w',
        'L1_cond_w', 'L1_cond_u', 'L1_ffn_w1', 'L1_ffn_w2']


def kernel(**inputs):
    import numpy as _np
    import concourse.bacc as _bacc
    from concourse import mybir as _mybir
    from concourse.bass_utils import run_bass_kernel_spmd as _run

    nc = _bacc.Bacc("TRN2", target_bir_lowering=False, num_devices=1)
    arrays, args = {}, []
    for name in _INS:
        a = _np.ascontiguousarray(inputs[name])
        arrays[f"in_{name}_dram"] = a
        args.append(nc.dram_tensor(f"in_{name}_dram", a.shape, _mybir.dt.from_np(a.dtype), kind="ExternalInput").ap())
    f32 = _mybir.dt.float32
    args.append(nc.dram_tensor("out_0_dram", inputs["x"].shape, f32, kind="ExternalOutput").ap())
    tokens, channels = inputs["x"].shape[0] * inputs["x"].shape[1], inputs["x"].shape[2]
    slots = tokens + 128 * inputs["L0_ffn_router_w"].shape[1]
    args.append(nc.dram_tensor("slot_rows", (slots, channels), f32, kind="Internal").ap())
    args.append(nc.dram_tensor("slot_out", (slots - 128, channels), f32, kind="Internal").ap())
    build(nc, *args)
    r = _run(nc, [arrays], core_ids=[0])
    return r.results[0]["out_0_dram"]
```

```python
from contextlib import ExitStack

import concourse.bass as bass
from concourse import mybir

F32 = mybir.dt.float32
BF16 = mybir.dt.bfloat16
I32 = mybir.dt.int32
U32 = mybir.dt.uint32
ALU = mybir.AluOpType
ACT = mybir.ActivationFunctionType
AX = mybir.AxisListType

P = 128
MAGIC = 12582912.0
EPS = 1e-5


class Steps:

    def __init__(self, eng, sem):
        self.eng, self.sem, self.base, self.n = eng, sem, 0, 0

    def mark(self, ins):
        self.n += 1
        ins.then_inc(self.sem, 1)

    def settle(self):
        self.eng.wait_ge(self.sem, self.base + self.n)

    def enter(self, i, per, first=0):
        self.start, self.per = self.base + self.n, per
        self.base, self.n = i * per + (self.start - first * per), 0

    def leave(self, count):
        assert self.n == self.per, (self.n, self.per)
        self.base, self.n = self.start + count * self.per, 0




def build(nc, x, fside, cond, w0, u0, router_w, gate_w, up_w, down_w, sh_gate, sh_up, sh_down,
          w1c, u1c, w1, w2, out, slot_rows, slot_out, side_rows):
    B, T, C = x.shape
    TD = cond.shape[1]
    E = router_w.shape[1]
    F = gate_w.shape[2]
    FF = w1.shape[0]
    KC = C // P
    KF = F // P
    KG = FF // P
    TQ = T // P
    NT = B * TQ
    NCH = B * KC
    NS = NT + E - 1
    STEPS_A = 26
    NU = 2 * NT
    WE = 3 * KC * F
    assert C == F == T == 512 and TQ == 4 and KC == 4

    f_v = fside.rearrange("b (q p) c -> b p q c", p=P)
    x_v = x.rearrange("b (q p) c -> b p q c", p=P)
    out_v = out.rearrange("b (q p) c -> (b q) p c", p=P)
    rows_v = slot_rows.rearrange("(s p) c -> s p c", p=P)
    moe_v = slot_out.rearrange("(s p) c -> s p c", p=P)
    side_v = side_rows.rearrange("b (c p) t -> (b c) p t", p=P)
    w1_v = w1.rearrange("(g p) c -> g p c", p=P)
    w2_v = w2.rearrange("(r p) f -> r p f", p=P)

    def ytok_tiles(z):
        b, c = (z - 6) // 4, (z - 6) % 4
        if b == B - 1:
            return range(4 * b, 4 * b + 4) if c == 0 else ()
        return [4 * b + q for q in ((), (0,), (1, 2), (3,))[c]]

    def w1_unit(u, v):
        return (u, u % 2, 16 * (u // 2 + 1), 0, v, 0)

    def w2_unit(i, c):
        if c < 0:
            i, c = i - 1, c + 4
        return (i * 4 + (NU // 4 + c), c % 2, i * 32 + 16 * (NU // 8 + c // 2 + 1), 1, i, c)

    def units_in_a(z):
        return [w1_unit(u, u) for u in (2 * (z - 22), 2 * (z - 22) + 1)] if 22 <= z < 26 else []

    def units_late(s):
        k = 2 * (s - NT)
        return [w1_unit(3 * NU // 4 + k + h, NU // 4 + k + h) for h in range(2)] if s < NT + 4 else []

    def unit_rows(unit):
        u, a, loads, j, r, c = unit
        return w2_v[bass.ds(r, 1), :, c * 512:(c + 1) * 512].rearrange("o p f -> (o p) f") if j else w1_v[r]

    with ExitStack() as ctx:
        def sb(name, shape, dt=F32):
            return ctx.enter_context(nc.sbuf_tensor(name, shape, dt))

        def sem(name):
            return ctx.enter_context(nc.semaphore(name))

        resid = sb("resid", [P, NT * C])
        ytok = sb("ytok", [P, NT * C])
        r1tok = ytok
        region = sb("region", [P, 2 * KC * T * 2])
        y0T = region[:, 0:2 * KC * T].rearrange("p (a k t) -> p a k t", a=2, k=KC)
        shT = region[:, 2 * KC * T:4 * KC * T].rearrange("p (a k t) -> p a k t", a=2, k=KF)
        w1flat = region[:, 0:2 * KC * T].bitcast(BF16)
        w2flat = region[:, 2 * KC * T:4 * KC * T].bitcast(BF16)
        w1T = w1flat.rearrange("p (k f) -> p k f", k=KC)
        w2T = w2flat.rearrange("p (g c) -> p g c", g=KG)
        wexp = sb("wexp", [P, 2 * WE])
        wsh = wexp[:, WE:2 * WE].rearrange("p (m k f) -> p m k f", m=3, k=KC)

        fk = sb("fk", [P, 2, TQ, P])
        xk = sb("xk", [P, 2, TQ, P])
        ksb = sb("ksb", [P, 2, T])
        fT = fk[:, :, :, :].rearrange("p a q t -> p a (q t)")
        kk = sb("kk", [P, 2, 2, T])
        ekv = sb("ekv", [P, 2, T])
        bwd_n = sb("bwd_n", [P, T + 1])
        bwd_d = sb("bwd_d", [P, T + 1])
        num = sb("num", [P, 2, T])
        den = sb("den", [P, 2, T])
        tx = sb("tx", [P, 2, T])
        wraw = tx

        work = sb("work", [P, 9, 512])
        wstat_in = work[:, 0:2, :]
        gtanh = work[:, 2, :]
        gt1 = work[:, 3, :]
        junk = work[:, 4, :]
        dn_sb = work[:, 5, :]
        zero = work[:, 6, :]
        wtern_a = xk[:, 0, :, :].rearrange("p q t -> p (q t)").bitcast(BF16)
        wtern_b = dn_sb.bitcast(BF16)
        xe = work[:, 0:2, :]
        xeT = work[:, 7:9, :].rearrange("p a (k t) -> p a k t", k=KC)
        hE = [junk, zero]
        heT = sb("heT", [P, KF, P])
        oE = xk[:, :, :, :].rearrange("p a q t -> p a (q t)")

        ident = sb("ident", [P, P])
        identb = sb("identb", [P, P], BF16)
        ones = sb("ones", [P, P])
        upper = work[:, 8, 0:P]
        iota_e = sb("iota_e", [P, E])
        iota_j = sb("iota_j", [P, NT])
        iota_s = sb("iota_s", [P, 24])
        sign_e = sb("sign_e", [P, E])
        par = sb("par", [P, 4, KC])
        cnd = den[:, 0, :].rearrange("p (b t) -> p b t", b=B)
        tf = sb("tf", [P, B])
        dhalf = sb("dhalf", [P, B])
        osh = sb("osh", [P, B])
        ew = sb("ew", [P, 2, KC])
        dec = sb("dec", [P, 2, KC, B])
        rw = sb("rw", [P, KC, E])
        lgT = work[0:E, 7, :]
        lg = sb("lg", [P, NT, E])
        score = sb("score", [P, NT])
        rt = num[:, :, :].rearrange("p a (k t) -> p (a k) t", t=NT * E)
        rs = den[:, 0, 0:240].rearrange("p (k s) -> p k s", k=10)
        tabf = den[0:1, 1, 384:480].rearrange("p (a s) -> p a s", a=3)
        cmp3 = den[0:1, 1, 0:384].rearrange("p (a s e) -> p a s e", a=2, e=8)
        tabi = sb("tabi", [1, 3, 32], I32)
        pos = sb("pos", [P, NT], U32)
        wstat = sb("wstat", [P, 2, 16])
        wsum = sb("wsum", [P, 2])
        magic = sb("magic", [P, 1])
        wq = sb("wq", [P, 2, 8])
        sc = sb("sc", [P, 2, 16])
        rsc = sb("rsc", [P, NT])

        bank = [ctx.enter_context(nc.psum_tensor(f"bank{i}", [P, 512], F32)) for i in range(8)]
        KPS, XPS, GPS, UPS, DPS, YPS, LPS, MPS = bank

        s_const = sem("s_const")
        s_par = [sem(f"s_par{j}") for j in range(4)]
        s_rw = sem("s_rw")
        s_cnd = sem("s_cnd")
        s_tf = sem("s_tf")
        s_f = [sem("s_f0"), sem("s_f1")]
        s_x = [sem("s_xin0"), sem("s_xin1")]
        s_ws = [sem("s_ws0"), sem("s_ws1")]
        s_wsh = sem("s_wsh")
        s_resid = sem("s_resid")
        s_zero = sem("s_zero")
        s_ktr = sem("s_ktr")
        s_xtr = sem("s_xtr")
        s_kexp = sem("s_kexp")
        s_kcopy = sem("s_kcopy")
        s_kst = [sem("s_kst0"), sem("s_kst1")]
        s_tx = sem("s_tx")
        s_ukc = sem("s_ukc")
        s_pre = sem("s_pre")
        s_comb = sem("s_comb")
        s_dd = sem("s_dd")
        s_nd = sem("s_nd")
        s_y = sem("s_y")
        s_rtr = sem("s_rtr")
        s_rev = sem("s_rev")
        s_lgmm = sem("s_lgmm")
        s_lgT = sem("s_lgT")
        s_lgtr = sem("s_lgtr")
        s_lg = sem("s_lg")
        s_ytr = sem("s_ytr")
        s_ytok = sem("s_ytok")
        s_g = sem("s_g")
        s_u = sem("s_u")
        s_tanh = sem("s_tanh")
        s_h = sem("s_h")
        s_gt = sem("s_gt")
        s_down = sem("s_down")
        s_dn = sem("s_dn")
        s_res = sem("s_res")
        s_stat = sem("s_stat")
        s_oh = sem("s_oh")
        s_cum = sem("s_cum")
        s_pos = sem("s_pos")
        s_score = sem("s_score")
        s_scaled = sem("s_scaled")
        s_scat = sem("s_scat")
        s_tab = sem("s_tab")
        s_wsum = sem("s_wsum")
        s_wtot = sem("s_wtot")
        s_sq = sem("s_sq")
        s_rms = sem("s_rms")
        s_wl = sem("s_wl")
        s_xe = [sem("s_xe0"), sem("s_xe1")]
        s_xetr = sem("s_xetr")
        s_xeT = sem("s_xeT")
        s_eg = sem("s_eg")
        s_eu = sem("s_eu")
        s_et = sem("s_et")
        s_eh = sem("s_eh")
        s_ehtr = sem("s_ehtr")
        s_ehT = sem("s_ehT")
        s_eo = sem("s_eo")
        s_oe = sem("s_oe")
        s_ost = [sem("s_ost0"), sem("s_ost1")]
        s_wr = [sem("s_wr0"), sem("s_wr1")]
        s_wrnd = sem("s_wrnd")
        s_tern = sem("s_tern")
        s_wtr = sem("s_wtr")
        s_wT = sem("s_wT")
        s_mo = [sem(f"s_mo{j}") for j in range(4)]
        s_x1 = sem("s_x1")
        s_t1 = sem("s_t1")
        s_q1 = sem("s_q1")
        s_q1tr = sem("s_q1tr")
        s_q1T = sem("s_q1T")
        s_hh = sem("s_hh")
        s_gelu = sem("s_gelu")
        s_y1 = sem("s_y1")
        s_amax = sem("s_amax")
        s_rnd = sem("s_rnd")
        s_q2 = sem("s_q2")
        s_q2tr = sem("s_q2tr")
        s_q2Ta = sem("s_q2Ta")
        s_q2Tv = sem("s_q2Tv")
        s_out = sem("s_out")
        s_fin = sem("s_fin")
        s_store = [sem("s_store0"), sem("s_store1")]
        s_vstep = sem("s_vstep")
        s_gstep = sem("s_gstep")
        s_astep = sem("s_astep")
        N_CONST = 13

        def late(a, n):
            return wexp[:, a * 512:(a + n) * 512]
        gel = late(0, 8).rearrange("p (a f) -> p a f", a=2)
        t1 = late(8, 2).rearrange("p (a c) -> p a c", a=2)
        y1 = late(10, 1)
        q1 = late(11, 1).bitcast(BF16).rearrange("p (a c) -> p a c", a=2)
        q1T = late(12, 1).bitcast(BF16).rearrange("p (a k t) -> p a k t", a=2, k=KC)
        q2 = late(13, 2).bitcast(BF16)
        q2T = late(15, 2).bitcast(BF16).rearrange("p (g t) -> p g t", g=KG)
        fin = late(17, 2).rearrange("p (a c) -> p a c", a=2)
        HPS = bank[0:4]
        QPS = bank[4][:, :].bitcast(BF16)
        TPS = [bank[5][:, :].bitcast(BF16), bank[6][:, :].bitcast(BF16)]
        OPS = bank[7]

        def down_bank(m):
            return YPS if m > NT - TQ and m % 2 else DPS

        def ytok_bank(t):
            return XPS if t > NT - TQ and t % 2 else YPS

        def unit_tern(unit):
            u, a = unit[0:2]
            return (wtern_a if isinstance(u, int) and u < NU // 4 else wtern_b)[:, a * 512:(a + 1) * 512]

        def unit_bank(unit):
            u, a = unit[0:2]
            return (MPS if a else KPS)[:, 0:256].bitcast(BF16)

        def route_1(dve, st, v_):
            def one(ins):
                st.mark(ins)
                st.settle()
            t_e = [P, NT, E]
            f = lambda k: rt[:, k, :].rearrange("p (t e) -> p t e", e=E)
            dve.wait_ge(s_lg, B)
            v_.tensor_reduce(score[:], lg[:, :, :], AX.X, ALU.max).then_inc(s_score, 1)
            dve.wait_ge(s_score, 1)
            st.mark(v_.tensor_tensor(out=f(0), in0=lg[:, :, :], in1=score[:].unsqueeze(2).to_broadcast(t_e),
                                     op=ALU.is_equal))
            st.settle()
            one(v_.tensor_tensor(out=f(1), in0=f(0), in1=iota_e[:].unsqueeze(1).to_broadcast(t_e),
                                 op=ALU.mult))
            one(v_.tensor_reduce(rs[:, 0, 0:NT], f(1), AX.X, ALU.min))
            v_.tensor_tensor(out=f(5), in0=iota_e[:].unsqueeze(1).to_broadcast(t_e),
                             in1=rs[:, 0, 0:NT].unsqueeze(2).to_broadcast(t_e),
                             op=ALU.is_equal).then_inc(s_oh, 1)

        def route_2(dve, st, v_):
            def one(ins):
                st.mark(ins)
                st.settle()
            e_t = [P, E, NT]
            g = lambda k: rt[:, k, :].rearrange("p (e t) -> p e t", e=E)
            f = lambda k: rt[:, k, :].rearrange("p (t e) -> p t e", e=E)
            r = lambda k, n=E: rs[:, k, 0:n]
            dve.wait_ge(s_cum, 1)
            one(v_.tensor_copy(g(0), MPS[:, 256:384].rearrange("p (t e) -> p e t", e=E)))
            one(v_.tensor_tensor_scan(rt[:, 1, :], ones[:], rt[:, 0, :], 0.0, ALU.mult, ALU.add))
            one(v_.tensor_tensor(out=rt[:, 2, :], in0=rt[:, 1, :], in1=rt[:, 0, :], op=ALU.subtract))
            one(v_.tensor_reduce(r(0), g(0), AX.X, ALU.add))
            one(v_.tensor_tensor(out=g(3), in0=r(0).unsqueeze(2).to_broadcast(e_t),
                                 in1=iota_j[:].unsqueeze(1).to_broadcast(e_t), op=ALU.is_gt))
            one(v_.tensor_reduce(r(1), g(3), AX.X, ALU.add))
            one(v_.tensor_tensor_scan(r(2), ones[:, 0:E], r(1), 0.0, ALU.mult, ALU.add))
            one(v_.tensor_tensor(out=r(3), in0=r(2), in1=r(1), op=ALU.subtract))
            one(v_.scalar_tensor_tensor(out=r(4), in0=r(3), scalar=float(P), in1=g(2)[:, :, 0],
                                        op0=ALU.mult, op1=ALU.subtract))
            one(v_.tensor_tensor(out=g(4), in0=g(2), in1=r(4).unsqueeze(2).to_broadcast(e_t), op=ALU.add))
            one(v_.tensor_tensor(out=f(1), in0=rt[:, 4, :].rearrange("p (e t) -> p t e", e=E),
                                 in1=MPS[:, 128:256].rearrange("p (t e) -> p t e", e=E), op=ALU.add))
            one(v_.tensor_tensor(out=f(3), in0=f(1), in1=f(5), op=ALU.mult))
            one(v_.tensor_reduce(r(5, NT), f(3), AX.X, ALU.add))
            v_.tensor_copy(pos[:], r(5, NT)).then_inc(s_pos, 1)
            ends = rs[0:1, 2, 0:E - 1].unsqueeze(1).to_broadcast([1, 24, E - 1])
            one(v_.tensor_tensor(out=cmp3[:, 0, :, 0:E - 1],
                                 in0=iota_s[0:1, :].unsqueeze(2).to_broadcast([1, 24, E - 1]),
                                 in1=ends, op=ALU.is_ge))
            one(v_.tensor_tensor(out=cmp3[:, 1, :, 0:E - 1], in0=cmp3[:, 0, :, 0:E - 1],
                                 in1=sign_e[0:1, 0:E - 1].unsqueeze(1).to_broadcast([1, 24, E - 1]),
                                 op=ALU.mult))
            one(v_.tensor_reduce(tabf[:, 0:2, 0:24], cmp3[:, :, :, 0:E - 1], AX.X, ALU.add))
            st.mark(v_.tensor_scalar(tabi[:, 0, 0:24], tabf[:, 0, 0:24], 48.0, 48.0, ALU.mult, ALU.add))
            st.mark(v_.tensor_scalar(tabi[:, 1, 0:24], tabf[:, 1, 0:24], float(WE), None, ALU.mult))
            st.mark(v_.tensor_scalar(tabi[:, 2, 0:E], rs[0:1, 2, 0:E], 1.0, None, ALU.add))
            st.settle()
            dve.sem_inc(s_tab, 1)

        block = ctx.enter_context(nc.Block())

        @block.sync
        def _(sp):
            sp.dma_start(fk[:, 0], f_v[0, :, :, 0:P]).then_inc(s_f[0], 16)
            sp.dma_start(xk[:, 0], x_v[0, :, :, 0:P]).then_inc(s_x[0], 16)
            with nc.allow_non_contiguous_dma(reason="vectors of 512 channels"):
                for j, v in ((2, w1c), (3, u1c)):
                    sp.dma_start(par[:, j, :], v.rearrange("(k p) -> p k", p=P)).then_inc(s_par[j], 16)
                sp.dma_start(rw[:, :, :], router_w.rearrange("(k p) e -> p k e", p=P)).then_inc(s_rw, 16)
            for n in range(NCH):
                if n + 1 < NCH:
                    m = n + 1
                    b, c = m // KC, m % KC
                    if m >= 2:
                        sp.wait_ge(s_ktr, m - 1)
                        sp.wait_ge(s_xtr, m - 1)
                    sp.dma_start(fk[:, m % 2], f_v[b, :, :, c * P:(c + 1) * P]).then_inc(s_f[m % 2], 16)
                    sp.dma_start(xk[:, m % 2], x_v[b, :, :, c * P:(c + 1) * P]).then_inc(s_x[m % 2], 16)
                for j, src in enumerate((w1_v[n], w2_v[n // 4, :, (n % 4) * 512:(n % 4 + 1) * 512])):
                    if n >= 1:
                        sp.wait_ge(s_stat, 2 * (n - 1) + j + 1)
                    sp.dma_start(wstat_in[:, j], src).then_inc(s_ws[j], 16)
                if 1 <= n <= 3:
                    sp.dma_start(wsh[:, n - 1], (sh_gate, sh_up, sh_down)[n - 1].rearrange("(k p) f -> p k f", p=P)
                                 ).then_inc(s_wsh, 16)
                if n == 6:
                    for b in range(B):
                        sp.dma_start(resid[:, b * TQ * C:(b + 1) * TQ * C].rearrange("p (q c) -> p q c", q=TQ),
                                     x_v[b]).then_inc(s_resid, 16)
                if n == 4:
                    sp.wait_ge(s_const, N_CONST)
                if n >= 4:
                    for s in range(2 * (n - 4), 2 * (n - 4) + 2):
                        sp.dma_start(rows_v[s], zero).then_inc(s_zero, 16)
            for e in range(E):
                dst = wexp[:, (e % 2) * WE:(e % 2 + 1) * WE].rearrange("p (m k f) -> p m k f", m=3, k=KC)
                if e == 1:
                    for m in (NCH, NCH + 1):
                        sp.wait_ge(s_ktr, m - 1)
                        sp.wait_ge(s_kst[m % 2], 16)
                        sp.dma_start(fT[:, m % 2], side_v[m - NCH]).then_inc(s_f[m % 2], 16)
                    sp.wait_ge(s_y, NCH)
                    for u in range(8):
                        if u >= 2:
                            sp.wait_ge(s_tern, u - 1)
                        sp.dma_start(wraw[:, u % 2], w1_v[u]).then_inc(s_wr[u % 2], 16)
                    sp.wait_ge(s_down, NT)
                if e == 2:
                    sp.wait_ge(s_tab, 1)
                if e >= 2:
                    tiles = sp.value_load(tabi[0:1, 2, e - 2:e - 1], min_val=1, max_val=NS + 1)
                    sp.wait_ge(s_eo, tiles)
                for j, src in enumerate((gate_w, up_w, down_w)):
                    sp.dma_start(dst[:, j], src[e].rearrange("(k p) f -> p k f", p=P)).then_inc(s_wl, 16)
                sp.wait_ge(s_wl, 48 * (e + 1))
            with sp.Fori(0, NT // 2) as i:
                for a in range(2):
                    sp.wait_ge(s_fin, i * 2 + (a + 2))
                    sp.dma_start(out_v[bass.ds(i * 2 + a, 1)].rearrange("o p c -> (o p) c"),
                                 fin[:, a]).then_inc(s_store[a], 16)
            for a in range(2):
                sp.wait_ge(s_store[a], 16 * (NT // 2 + 1))

        @block.gpsimd
        def _(pool):
            st = Steps(pool, s_gstep)
            g = nc.gpsimd
            g.memset(ident[:], 0.0).then_inc(s_const, 1)
            g.memset(ones[:], 1.0).then_inc(s_const, 1)
            g.memset(bwd_n[:, T:T + 1], 0.0).then_inc(s_const, 1)
            g.memset(bwd_d[:, T:T + 1], 0.0).then_inc(s_const, 1)
            g.memset(zero, 0.0).then_inc(s_const, 1)
            pool.wait_ge(s_const, 5)
            g.affine_select(out=ident[:], in_=ident[:], compare_op=ALU.not_equal, fill=1.0, base=0,
                            pattern=[[-1, P]], channel_multiplier=1).then_inc(s_const, 1)
            g.affine_select(out=upper, in_=ones[:], compare_op=ALU.is_gt, fill=0.0, base=0,
                            pattern=[[1, P]], channel_multiplier=-1).then_inc(s_const, 1)
            g.iota(iota_e[:], pattern=[[1, E]], base=-E, channel_multiplier=0,
                   allow_small_or_imprecise_dtypes=True).then_inc(s_const, 1)
            g.iota(iota_j[:], pattern=[[P, NT]], base=0, channel_multiplier=0,
                   allow_small_or_imprecise_dtypes=True).then_inc(s_const, 1)
            g.iota(iota_s[:], pattern=[[1, 24]], base=0, channel_multiplier=0,
                   allow_small_or_imprecise_dtypes=True).then_inc(s_const, 1)
            g.iota(sign_e[:], pattern=[[0, E // 2], [-2, 2]], base=1, channel_multiplier=0,
                   allow_small_or_imprecise_dtypes=True).then_inc(s_const, 1)
            g.memset(magic[:], MAGIC).then_inc(s_const, 1)
            pool.wait_ge(s_const, 6)
            g.tensor_copy(identb[:], ident[:]).then_inc(s_const, 1)

            def products(n, p, stored=None):
                pool.wait_ge(s_kexp, n + 1)
                g.tensor_tensor(out=ekv[:, p], in0=kk[:, p, 0], in1=ksb[:, p], op=ALU.mult).then_inc(s_pre, 1)
                pool.wait_ge(s_pre, n + 1)
                if stored:
                    pool.wait_ge(s_kst[p], stored)
                st.mark(g.tensor_tensor(out=ksb[:, p], in0=kk[:, p, 1], in1=ksb[:, p], op=ALU.mult))

            def sums(n, p):
                pool.wait_ge(s_comb, n + 1)
                st.settle()
                g.tensor_tensor(out=den[:, p], in0=den[:, p], in1=kk[:, p, 1], op=ALU.add).then_inc(s_dd, 1)
                pool.wait_ge(s_dd, n + 1)
                g.tensor_tensor(out=num[:, p], in0=num[:, p], in1=ksb[:, p], op=ALU.add).then_inc(s_nd, 1)

            for z in range(STEPS_A):
                if z == 1:
                    products(1, 1, 16)
                if 1 <= z <= NCH:
                    sums(z - 1, (z - 1) % 2)
                if z < NCH and z != 1:
                    products(z, z % 2, 16 * (z // 2 + 1))
                if z in (19, 20):
                    pool.wait_ge(s_zero, 16 * (NS + 1))
                    pool.wait_ge(s_pos, 1)
                    for t in range((z - 19) * NT // 2, (z - 18) * NT // 2):
                        pool.wait_ge(s_scaled, t + 1)
                        g.indirect_dma_start(slot_rows[:, :],
                                             bass.IndirectOffsetOnAxis(ap=pos[:, t:t + 1], axis=0),
                                             ytok[:, t * C:(t + 1) * C], None).then_inc(s_scat, 16)
                if z >= 10:
                    m = z - 10
                    pool.wait_ge(s_dn, m + 1)
                    pool.wait_ge(s_resid, 16 * B)
                    g.tensor_tensor(out=resid[:, m * C:(m + 1) * C], in0=resid[:, m * C:(m + 1) * C],
                                    in1=dn_sb, op=ALU.add).then_inc(s_res, 1)

            for s in range(4):
                if s >= 1:
                    sums(NCH + s - 1, (s - 1) % 2)
                products(NCH + s, s % 2)
            with pool.Fori(1, 4) as i:
                st.enter(i, 4 * 1, 1)
                for c in range(KC):
                    sums(i * KC + (NCH + c - 1), (c + 1) % 2)
                    products(i * KC + (NCH + c), c % 2)
                st.leave(3)
            sums(2 * NCH - 1, 1)

            for a in range(2):
                pool.wait_ge(s_ost[a], 16 * ((NS + 1 - a) // 2 + 1))
            for t in range(NT + 4):
                if t < NT:
                    g.indirect_dma_start(resid[:, t * C:(t + 1) * C], None, slot_out[:, :],
                                         bass.IndirectOffsetOnAxis(ap=pos[:, t:t + 1], axis=0),
                                         compute_op=ALU.add).then_inc(s_mo[t % 4], 16)
                if 3 <= t < NT + 3:
                    pool.wait_ge(s_mo[(t - 3) % 4], 16 * ((t - 3) // 4 + 1))
                    pool.sem_inc(s_x1, 1)
                if t >= 4 + 2:
                    m = t - 4
                    r = r1tok[:, m * C:(m + 1) * C]
                    pool.wait_ge(s_t1, m + 1)
                    if m == 2:
                        pool.wait_ge(s_y1, 2)
                    st.mark(g.tensor_tensor(out=t1[:, m % 2], in0=t1[:, m % 2], in1=r, op=ALU.mult))
                    st.settle()
                    g.tensor_tensor(out=r, in0=r, in1=t1[:, m % 2], op=ALU.add).then_inc(s_y1, 1)

        @block.scalar
        def _(act):
            st = Steps(act, s_astep)
            a_ = nc.scalar.activation
            def k_copy(n, p):
                act.wait_ge(s_ktr, n + 1)
                if not isinstance(n, int) or n >= 2:
                    act.wait_ge(s_nd, n - 1)
                a_(ksb[:, p], KPS[:, :], ACT.Copy).then_inc(s_kcopy, 1)
                act.wait_ge(s_kcopy, n + 1)
                act.dma_start(side_v[n], ksb[:, p]).then_inc(s_kst[p], 16)

            def k_exp(n, p):
                act.wait_ge(s_ukc, n + 1)
                a_(kk[:, p], kk[:, p], ACT.Exp).then_inc(s_kexp, 1)

            def r_out(n, b, c):
                act.wait_ge(s_rtr, n - (NCH - 1))
                act.wait_ge(s_scat, 16 * NT)
                a_(r1tok[:, bass.ds(b * (TQ * C), TQ * C)].rearrange("p (q c) -> p q c", q=TQ)
                   [:, :, c * P:(c + 1) * P], YPS[:, :].rearrange("p (q c) -> p q c", q=TQ),
                   ACT.Copy).then_inc(s_rev, 1)

            def x_tanh(n):
                act.wait_ge(s_xtr, n + 1)
                if n >= 2:
                    act.wait_ge(s_y, n - 1)
                a_(tx[:, n % 2], XPS[:, :], ACT.Tanh, scale=0.5).then_inc(s_tx, 1)

            def squares(n):
                for j in range(2):
                    act.wait_ge(s_ws[j], 16 * (n + 1))
                    if n or j:
                        act.wait_ge(s_stat, 2 * n + j)
                    a_(junk, wstat_in[:, j], ACT.Square,
                       accum_out=wstat[:, j, n:n + 1]).then_inc(s_stat, 1)

            def unit_round(unit):
                u, a, loads, j = unit[0:4]
                act.wait_ge(s_rms, 1)
                act.wait_ge(s_wr[a], loads)
                a_(wraw[:, a], wraw[:, a], ACT.Identity, scale=wq[:, j, 4:5], bias=magic[:, 0:1]
                   ).then_inc(s_wrnd, 1)

            def unit_load(unit):
                u, a = unit[0:2]
                act.wait_ge(s_tern, u - 1)
                act.dma_start(wraw[:, a], unit_rows(unit)).then_inc(s_wr[a], 16)

            def xe_load(s, p):
                act.wait_ge(s_xetr, s + 1)
                act.dma_start(xe[:, p], rows_v[bass.ds(s, 1)].rearrange("o p c -> (o p) c")
                              ).then_inc(s_xe[p], 16)

            def xe_copy(s, p):
                act.wait_ge(s_xetr, s + 3)
                act.wait_ge(s_eu, s + 1)
                a_(xeT[:, p].rearrange("p k t -> p (k t)"), XPS[:, :], ACT.Copy).then_inc(s_xeT, 1)

            act.dma_start(cnd, cond.unsqueeze(0).to_broadcast([P, B, TD])).then_inc(s_cnd, 16)
            with nc.allow_non_contiguous_dma(reason="vectors of 512 channels"):
                for j, v in ((1, u0), (0, w0)):
                    act.dma_start(par[:, j, :], v.rearrange("(k p) -> p k", p=P)).then_inc(s_par[j], 16)
            k_copy(0, 0)
            act.wait_ge(s_tf, 1)
            a_(tf[:], dhalf[:], ACT.Tanh, scale=0.5).then_inc(s_tf, 1)
            for l in range(2):
                act.wait_ge(s_par[2 * l], 16)
                st.mark(a_(ew[:, l], par[:, 2 * l], ACT.Exp))
            st.settle()
            a_(ew[:, :, :], ew[:, :, :], ACT.Exp, scale=-1.0).then_inc(s_tf, 1)

            for z in range(STEPS_A):
                if 6 <= z < 22:
                    k = z - 6
                    act.wait_ge(s_g, k + 1)
                    if k:
                        act.wait_ge(s_gt, k)
                    if k % 4 == 0:
                        act.wait_ge(s_lgmm, k // 4 + 1)
                        if k:
                            act.wait_ge(s_lgtr, k // 4)
                        a_(lgT, LPS[0:E, :], ACT.Copy).then_inc(s_lgT, 1)
                    a_(gtanh, GPS[:, :], ACT.Tanh, scale=0.5).then_inc(s_tanh, 1)
                if 2 <= z < NCH:
                    k_copy(z, z % 2)
                if z == STEPS_A - 1:
                    for p in range(2):
                        xe_copy(p, p)
                for unit in units_in_a(z):
                    unit_round(unit)
                if z == STEPS_A - 2:
                    act.wait_ge(s_scat, 16 * NT)
                    for p in range(2):
                        xe_load(p, p)
                if z >= 10:
                    m = z - 10
                    act.wait_ge(s_down, m + 1)
                    if m:
                        act.wait_ge(s_res, m)
                    a_(dn_sb, down_bank(m)[:, :], ACT.Copy).then_inc(s_dn, 1)
                if 5 <= z < NCH:
                    x_tanh(z)
                for q in ytok_tiles(z) if 6 <= z < 22 else ():
                    act.wait_ge(s_ytr, q + 1)
                    a_(ytok[:, q * C:(q + 1) * C], ytok_bank(q)[:, :], ACT.Copy).then_inc(s_ytok, 1)
                if z < 5:
                    k_exp(z, z % 2)
                if z == 0:
                    k_copy(1, 1)
                if z < NCH:
                    squares(z)
                if 5 <= z < NCH:
                    k_exp(z, z % 2)
                if z < 5:
                    x_tanh(z)
                if z == 18:
                    act.wait_ge(s_oh, 1)
                    a_(score[:], score[:], ACT.Sigmoid).then_inc(s_score, 1)
                    act.wait_ge(s_score, 2)
                    act.wait_ge(s_ytok, NT)
                if z in (18, 19):
                    for t in range((z - 18) * NT // 2, (z - 17) * NT // 2):
                        a_(ytok[:, t * C:(t + 1) * C], ytok[:, t * C:(t + 1) * C], ACT.Copy,
                           scale=score[:, t:t + 1]).then_inc(s_scaled, 1)
                if z == 20:
                    act.wait_ge(s_sq, 1)
                    a_(wq[:, :, 1:2], wq[:, :, 0:1], ACT.Sqrt).then_inc(s_sq, 1)

            def e_tanh(s):
                act.wait_ge(s_eg, s + 1)
                act.wait_ge(s_gt, s + NT)
                a_(gtanh, GPS[:, :], ACT.Tanh, scale=0.5).then_inc(s_et, 1)

            def he_copy(s):
                act.wait_ge(s_ehtr, s + 2)
                act.wait_ge(s_eo, s + 1)
                a_(heT.rearrange("p k t -> p (k t)"), LPS[:, :], ACT.Copy).then_inc(s_ehT, 1)

            def o_copy(s, p, k):
                act.wait_ge(s_eo, s + 2)
                act.wait_ge(s_ost[p], k * 16 + 16)
                a_(oE[:, p], DPS[:, :], ACT.Copy).then_inc(s_oe, 1)
                act.wait_ge(s_oe, s + 2)
                act.dma_start(moe_v[bass.ds(s, 1)].rearrange("o p c -> (o p) c"), oE[:, p]
                              ).then_inc(s_ost[p], 16)

            for p in range(2):
                act.wait_ge(s_kst[p], 16 * NCH // 2)
            act.sem_inc(s_oe, 1)
            act.sem_inc(s_ehT, 1)
            for p in range(2):
                act.sem_inc(s_ost[p], 16)
            e_tanh(0)

            def e_step(s, p, k, chunk=None, ratio=None, fetch=True, last=False, units=()):
                if chunk:
                    n, b, c, count = chunk
                    if not isinstance(n, int) or n >= NCH + 2:
                        act.wait_ge(s_kcopy, n - 1)
                        act.dma_start(fT[:, p], side_v[bass.ds(b * KC + c, 1)].rearrange("o p t -> (o p) t")
                                      ).then_inc(s_f[p], 16)
                for unit in units:
                    unit_load(unit)
                if fetch:
                    xe_load(s + 2, p)
                if k is not None and not last:
                    o_copy(s - 1, 1 - p, k)
                if not last:
                    e_tanh(s + 1)
                if ratio:
                    r_out(*ratio)
                he_copy(s)
                if last:
                    o_copy(s - 1, 1 - p, k)
                if chunk:
                    act.wait_ge(s_f[p], count)
                    act.wait_ge(s_nd, n - 1)
                    a_(ksb[:, p], fT[:, p], ACT.Copy).then_inc(s_kcopy, 1)
                if fetch:
                    xe_copy(s + 2, p)
                for unit in units:
                    unit_round(unit)
                if chunk:
                    k_exp(n, p)

            for s in range(4):
                e_step(s, s % 2, (s - 1) // 2 if s else None, (NCH + s, 0, s, 16 * ((NCH + s) // 2 + 1)),
                       (NCH, 0, 0) if s == 3 else None,
                       units=[w2_unit(0, s)])
            with act.Fori(1, 4) as i:
                for c in range(KC):
                    e_step(i * KC + c, c % 2, i * 2 + ((c + 1) // 2 - 1),
                           (i * KC + (NCH + c), i, c, i * 32 + 16 * ((NCH + c) // 2 + 1)),
                           (i * KC + (NCH + c - 3), i + (c + 1) // KC - 1, (c + 1) % KC),
                           units=[w2_unit(i, c)])
            for s in range(NT, NS):
                n = NCH + s - 3
                e_step(s, s % 2, (s - 1) // 2, None, (n, B - 1, n % KC) if n < 2 * NCH else None,
                       s + 2 < NS, s == NS - 1, units_late(s))
            o_copy(NS - 1, (NS - 1) % 2, (NS - 1) // 2)

            def tanh_1(t, a):
                act.wait_ge(s_x1, t + 1)
                if not isinstance(t, int) or t >= 2:
                    act.wait_ge(s_y1, t - 1)
                a_(t1[:, a], resid[:, bass.ds(t * C, C)], ACT.Tanh, scale=0.5).then_inc(s_t1, 1)

            def q1T_copy(t, a):
                act.wait_ge(s_q1tr, t + 2)
                act.wait_ge(s_hh, t * 4 + 4)
                a_(q1T[:, a].rearrange("p k t -> p (k t)"), QPS[:, 0:512], ACT.Copy).then_inc(s_q1T, 1)

            def gelu(t, a, j):
                act.wait_ge(s_q2, t * 2 + 1)
                act.wait_ge(s_hh, t * 4 + (j + 9))
                a_(gel[:, a, j * 512:(j + 1) * 512], HPS[j][:, :], ACT.Gelu,
                   scale=sc[:, a, 4:5]).then_inc(s_gelu, 1)

            def scale_2(t, a):
                act.wait_ge(s_amax, t + 1)
                for h in range(2):
                    a_(gel[:, a, h * 1024:(h + 1) * 1024], gel[:, a, h * 1024:(h + 1) * 1024], ACT.Identity,
                       scale=sc[:, a, 6:7], bias=magic[:, 0:1]).then_inc(s_rnd, 1)

            def q2T_half(t):
                act.wait_ge(s_q2tr, t + 2)
                act.wait_ge(s_out, t + 1)
                a_(q2T[:, 0:8].rearrange("p g t -> p (g t)"), TPS[0], ACT.Copy).then_inc(s_q2Ta, 1)

            def step_1(t, a):
                at = lambda m: not isinstance(t, int) or 0 <= t + m < NT
                if at(1):
                    for j in range(4):
                        gelu(t + 1, 1 - a, j)
                if at(2):
                    q1T_copy(t + 2, a)
                if at(4):
                    tanh_1(t + 4, a)
                if at(1):
                    scale_2(t + 1, 1 - a)
                if at(0):
                    q2T_half(t)

            tanh_1(0, 0)
            tanh_1(1, 1)
            tanh_1(2, 0)
            q1T_copy(0, 0)
            step_1(-1, 1)
            step_1(0, 0)
            with act.Fori(0, 5) as i:
                for a in range(2):
                    step_1(i * 2 + (a + 1), 1 - a)
            for t in range(11, NT):
                step_1(t, t % 2)

        @block.tensor
        def _(pe):
            pe.sem_inc(s_xetr, 2)
            pe.sem_inc(s_eu, 2)
            pe.sem_inc(s_eh, 1)
            pe.sem_inc(s_ehtr, 1)
            pe.sem_inc(s_eo, 1)
            pe.wait_ge(s_const, N_CONST)
            mm, tr = nc.tensor.matmul, nc.tensor.transpose

            def four(out, src, idt, done):
                for q in range(4):
                    last = tr(out[:, q * P:(q + 1) * P], src(q), idt)
                last.then_inc(done, 1)

            def k_tr(n, p, count):
                pe.wait_ge(s_f[p], count)
                if n >= 1:
                    pe.wait_ge(s_kcopy, n)
                four(KPS, lambda q: fk[:, p, q, :], ident[:], s_ktr)

            def r_tr(n, p):
                pe.wait_ge(s_y, n + 1)
                if not isinstance(n, int) or n > NCH:
                    pe.wait_ge(s_rev, n - NCH)
                four(YPS, lambda q: num[:, p, q * P:(q + 1) * P], ident[:], s_rtr)

            def w_tr(unit):
                u = unit[0]
                pe.wait_ge(s_tern, u + 1)
                if not isinstance(u, int) or u >= 2:
                    pe.wait_ge(s_wT, u - 1)
                four(unit_bank(unit), lambda q: unit_tern(unit)[:, q * P:(q + 1) * P], identb[:], s_wtr)

            def e_in(s, p, k):
                pe.wait_ge(s_xe[p], k * 16 + 16)
                if not isinstance(s, int) or s >= 1:
                    pe.wait_ge(s_xeT, s)
                four(XPS, lambda q: xe[:, p, q * P:(q + 1) * P], ident[:], s_xetr)

            for z in range(STEPS_A):
                b, c = (z - 6) // 4, (z - 6) % 4
                shared = 6 <= z < 22
                if shared:
                    yb = y0T[:, b % 2]
                    if c == 0:
                        pe.wait_ge(s_y, 4 * (b + 1))
                        pe.wait_ge(s_rw, 16)
                        if b:
                            pe.wait_ge(s_lgT, b)
                        for k in range(KC):
                            last = mm(LPS[0:E, :], rw[:, k, :], yb[:, k, :], start=k == 0, stop=k == KC - 1)
                        last.then_inc(s_lgmm, 1)
                    pe.wait_ge(s_wsh, 48)
                    if z > 6:
                        pe.wait_ge(s_gt, z - 6)
                    for k in range(KC):
                        last = mm(GPS[:, :], wsh[:, 0, k, c * P:(c + 1) * P], yb[:, k, :],
                                  start=k == 0, stop=k == KC - 1)
                    last.then_inc(s_g, 1)
                if z < NCH:
                    k_tr(z, z % 2, 16 * (z // 2 + 1))
                for unit in units_in_a(z - 1):
                    w_tr(unit)
                if z == STEPS_A - 1:
                    e_in(0, 0, 0)
                    e_in(1, 1, 0)
                if z >= 10:
                    m = z - 10
                    pe.wait_ge(s_h, 4 * (m // 4 + 1))
                    before = m - 1 if m > NT - TQ + 1 else m
                    if before:
                        pe.wait_ge(s_dn, before)
                    for j in range(KF):
                        last = mm(down_bank(m)[:, :], shT[:, m // 4 % 2, j, m % 4 * P:(m % 4 + 1) * P],
                                  wsh[:, 2, j, :], start=j == 0, stop=j == KF - 1)
                    last.then_inc(s_down, 1)
                if z < NCH:
                    pe.wait_ge(s_x[z % 2], 16 * (z // 2 + 1))
                    if z:
                        pe.wait_ge(s_tx, z)
                    four(XPS, lambda q: xk[:, z % 2, q, :], ident[:], s_xtr)
                if shared:
                    if z > 6:
                        pe.wait_ge(s_h, z - 6)
                    for k in range(KC):
                        last = mm(UPS[:, :], wsh[:, 1, k, c * P:(c + 1) * P], yb[:, k, :],
                                  start=k == 0, stop=k == KC - 1)
                    last.then_inc(s_u, 1)
                    if c == 0:
                        pe.wait_ge(s_lgT, b + 1)
                        if b:
                            pe.wait_ge(s_lg, b)
                        for q in range(4):
                            last = tr(MPS[:, q * E:(q + 1) * E], lgT[:, q * P:(q + 1) * P], ident[0:E, 0:E])
                        last.then_inc(s_lgtr, 1)
                    for t in ytok_tiles(z):
                        before = t - 1 if t > NT - TQ else t
                        if before:
                            pe.wait_ge(s_ytok, before)
                        four(ytok_bank(t), lambda k: yb[:, k, t % 4 * P:(t % 4 + 1) * P], ident[:], s_ytr)
                if z == 18:
                    pe.wait_ge(s_oh, 1)
                    mm(MPS[:, 128:256], upper, rt[:, 5, :], start=True, stop=True)
                    mm(MPS[:, 256:384], ones[:], rt[:, 5, :], start=True, stop=True).then_inc(s_cum, 1)
                if z == 19:
                    pe.wait_ge(s_wsum, 1)
                    mm(MPS[:, 384:386], ones[:], wsum[:], start=True, stop=True).then_inc(s_wtot, 1)

            def e_weights(s):
                return pe.value_load(tabi[0:1, 1, bass.ds(s, 1)], min_val=0, max_val=WE)

            def e_product(m_, ps, done, at, p):
                for k in range(KC):
                    last = mm(ps[:, :], xeT[:, p, k, :], wexp[:, bass.ds(at + (m_ * KC + k) * F, F)],
                              start=k == 0, stop=k == KC - 1)
                last.then_inc(done, 1)

            def e_gate(s, p):
                loads = pe.value_load(tabi[0:1, 0, bass.ds(s, 1)], min_val=48, max_val=48 * E)
                at = e_weights(s)
                pe.wait_ge(s_wl, loads)
                pe.wait_ge(s_xeT, s + 1)
                pe.wait_ge(s_gt, s + NT)
                e_product(0, GPS, s_eg, at, p)

            def e_up(s, p):
                at = e_weights(s)
                pe.wait_ge(s_eh, s + 1)
                e_product(1, UPS, s_eu, at, p)

            def e_h(s, p):
                pe.wait_ge(s_eh, s + 2)
                pe.wait_ge(s_ehT, s + 1)
                four(LPS, lambda q: hE[p][:, q * P:(q + 1) * P], ident[:], s_ehtr)

            def e_down(s):
                at = e_weights(s)
                pe.wait_ge(s_ehT, s + 2)
                pe.wait_ge(s_oe, s + 1)
                for j in range(KF):
                    last = mm(DPS[:, :], heT[:, j, :], wexp[:, bass.ds(at + (2 * KC + j) * F, F)],
                              start=j == 0, stop=j == KF - 1)
                last.then_inc(s_eo, 1)

            pe.wait_ge(s_tab, 1)
            e_gate(0, 0)
            e_up(0, 0)
            for unit in units_in_a(STEPS_A - 1):
                w_tr(unit)

            def e_step(s, p, k, ratio=None, fetch=True, last=False, units=()):
                if not last:
                    e_gate(s + 1, 1 - p)
                if ratio is not None:
                    r_tr(*ratio)
                e_h(s, p)
                if fetch:
                    e_in(s + 2, p, k + 1)
                for unit in units:
                    w_tr(unit)
                if not last:
                    e_up(s + 1, 1 - p)
                e_down(s)

            for s in range(4):
                e_step(s, s % 2, s // 2, (NCH, 0) if s == 3 else None, units=[w2_unit(0, s - 1)] if s else ())
            with pe.Fori(1, 4) as i:
                for c in range(KC):
                    e_step(i * KC + c, c % 2, i * 2 + c // 2,
                           (i * KC + (NCH + c - 3), (c + 1) % 2), units=[w2_unit(i, c - 1)])
            for s in range(NT, NS):
                n = NCH + s - 3
                e_step(s, s % 2, s // 2, (n, n % 2) if n < 2 * NCH else None,
                       s + 2 < NS, s == NS - 1, [w2_unit(3, 3)] if s == NT else units_late(s - 1))

            def q1_tr(t, a):
                pe.wait_ge(s_q1, t + 1)
                pe.wait_ge(s_q1T, t + 1)
                four(QPS, lambda q: q1[:, a, q * P:(q + 1) * P], identb[:], s_q1tr)

            def hidden(t, a, j):
                pe.wait_ge(s_q1T, t + 2)
                pe.wait_ge(s_gelu, t * 4 + (j + 1))
                for k in range(KC):
                    last = mm(HPS[j][:, :], q1T[:, a, k, :], w1T[:, k, j * 512:(j + 1) * 512],
                              start=k == 0, stop=k == KC - 1)
                last.then_inc(s_hh, 1)

            def q2_tr(t):
                pe.wait_ge(s_q2, t * 2 + 6)
                pe.wait_ge(s_q2Ta, t + 1)
                pe.wait_ge(s_q2Tv, t + 1)
                for g in range(KG):
                    last = tr(TPS[g // 8][:, g % 8 * P:(g % 8 + 1) * P], q2[:, g * P:(g + 1) * P], identb[:])
                last.then_inc(s_q2tr, 1)

            def result(t):
                pe.wait_ge(s_q2Ta, t + 2)
                pe.wait_ge(s_q2Tv, t + 2)
                pe.wait_ge(s_fin, t + 1)
                for g in range(KG):
                    last = mm(OPS[:, :], q2T[:, g, :], w2T[:, g, :], start=g == 0, stop=g == KG - 1)
                last.then_inc(s_out, 1)

            pe.wait_ge(s_wT, NU)
            def step_1(t, a):
                at = lambda m: not isinstance(t, int) or 0 <= t + m < NT
                if at(1):
                    for j in range(4):
                        hidden(t + 1, 1 - a, j)
                if at(2):
                    q1_tr(t + 2, a)
                if at(-1):
                    result(t - 1)
                if at(0):
                    q2_tr(t)

            q1_tr(0, 0)
            step_1(-1, 1)
            step_1(0, 0)
            with pe.Fori(0, 5) as i:
                for a in range(2):
                    step_1(i * 2 + (a + 1), 1 - a)
            for t in range(11, NT + 1):
                step_1(t, t % 2)

        @block.vector
        def _(dve):
            st = Steps(dve, s_vstep)
            v_ = nc.vector
            for s_, k in ((s_q1tr, 1), (s_q1T, 1), (s_hh, 8), (s_gelu, 4), (s_q2, 4),
                          (s_q2tr, 1), (s_q2Ta, 1), (s_q2Tv, 1), (s_out, 1), (s_fin, 1),
                          (s_store[0], 16), (s_store[1], 16)):
                dve.sem_inc(s_, k)
            def guards(n, p, l, c):
                dve.wait_ge(s_kcopy, n + 1)
                st.mark(v_.tensor_scalar(kk[:, p, 0], ksb[:, p], 30.0, None, ALU.min))
                v_.tensor_scalar(kk[:, p, 1], ksb[:, p], par[:, 2 * l + 1, c:c + 1], 30.0,
                                 ALU.add, ALU.min).then_inc(s_ukc, 1)

            def scans(n, p, l, c, b):
                dve.wait_ge(s_pre, n + 1)
                if not isinstance(n, int) or n >= 1:
                    dve.wait_ge(s_comb, n)
                if not isinstance(n, int) or n >= 2:
                    dve.wait_ge(s_y, n - 1)
                if not isinstance(n, int) or n >= NCH + 2:
                    dve.wait_ge(s_rtr, n - (NCH + 1))
                d1 = dec[:, l, c, bass.ds(b, 1)]
                d = d1.to_broadcast([P, T])
                for sums_, bwd, src in ((den, bwd_d, kk[:, p, 0]), (num, bwd_n, ekv[:, p])):
                    st.mark(v_.tensor_tensor_scan(sums_[:, p], d, src, 0.0, ALU.mult, ALU.add))
                    st.mark(v_.tensor_tensor_scan(bwd[:, 0:T][:, ::-1], d, src[:, ::-1], 0.0,
                                                  ALU.mult, ALU.add))
                st.settle()
                st.mark(v_.scalar_tensor_tensor(out=den[:, p], in0=bwd_d[:, 1:T + 1], scalar=d1,
                                                in1=den[:, p], op0=ALU.mult, op1=ALU.add))
                st.settle()
                v_.scalar_tensor_tensor(out=num[:, p], in0=bwd_n[:, 1:T + 1], scalar=d1,
                                        in1=num[:, p], op0=ALU.mult, op1=ALU.add).then_inc(s_comb, 1)

            def ratio(n, p, l, b):
                dve.wait_ge(s_dd, n + 1)
                st.mark(v_.tensor_scalar(den[:, p], den[:, p], 1e-8, None, ALU.max))
                st.settle()
                st.mark(v_.reciprocal(den[:, p], den[:, p]))
                st.settle()
                dve.wait_ge(s_nd, n + 1)
                o = osh[:, bass.ds(b, 1)]
                ins = v_.scalar_tensor_tensor(out=num[:, p], in0=num[:, p], scalar=o, in1=den[:, p],
                                              op0=ALU.mult, op1=ALU.mult)
                if l:
                    ins.then_inc(s_y, 1)
                    return
                st.mark(ins)
                st.settle()
                dve.wait_ge(s_tx, n + 1)
                if b >= 2:
                    dve.wait_ge(s_ytr, 4 * (b - 1))
                v_.scalar_tensor_tensor(out=y0T[:, b % 2, n % KC, :], in0=tx[:, p], scalar=1.0, in1=num[:, p],
                                        op0=ALU.add, op1=ALU.mult).then_inc(s_y, 1)

            def tern(unit):
                u, a = unit[0:2]
                dve.wait_ge(s_wrnd, u + 1)
                if not isinstance(u, int) or u >= 2:
                    dve.wait_ge(s_wtr, u - 1)
                v_.tensor_scalar(unit_tern(unit), wraw[:, a], MAGIC, 1.0, ALU.subtract, ALU.min
                                 ).then_inc(s_tern, 1)

            def w_out(unit):
                u, a, loads, j, r, c = unit
                dve.wait_ge(s_wtr, u + 1)
                dst = w2T[:, c * 4:(c + 1) * 4, bass.ds(r * P, P)] if j else w1T[:, :, r * P:(r + 1) * P]
                v_.tensor_scalar(dst, unit_bank(unit).rearrange("p (k t) -> p k t", k=4), -1.0, None, ALU.max
                                 ).then_inc(s_wT, 1)

            def gate_t(count, tanh_done, h_done, before):
                dve.wait_ge(tanh_done, count)
                if not isinstance(before, int) or before > 0:
                    dve.wait_ge(h_done, before)
                v_.scalar_tensor_tensor(out=gt1, in0=gtanh, scalar=1.0, in1=GPS[:, :],
                                        op0=ALU.add, op1=ALU.mult).then_inc(s_gt, 1)

            dve.wait_ge(s_cnd, 16)
            v_.tensor_reduce(dhalf[:], cnd, AX.X, ALU.add).then_inc(s_tf, 1)
            dve.wait_ge(s_par[1], 16)
            guards(0, 0, 0, 0)
            dve.wait_ge(s_tf, 3)
            st.mark(v_.tensor_scalar(dhalf[:], tf[:], 0.25, 0.75, ALU.mult, ALU.add))
            st.mark(v_.tensor_scalar(osh[:], tf[:], 0.05, 0.45, ALU.mult, ALU.add))
            st.settle()
            for l in range(2):
                for c in range(KC):
                    st.mark(v_.tensor_scalar(dec[:, l, c, :], dhalf[:], ew[:, l, c:c + 1], None, ALU.mult))
            st.settle()
            dve.wait_ge(s_const, N_CONST)

            for z in range(STEPS_A):
                if 5 <= z < NCH + 2:
                    ratio(z - 2, z % 2, 0, (z - 2) // KC)
                if 6 <= z < 22:
                    gate_t(z - 5, s_tanh, s_h, z - 6)
                if z == 1:
                    guards(1, 1, 0, 1)
                if 1 <= z <= NCH:
                    scans(z - 1, (z - 1) % 2, 0, (z - 1) % KC, (z - 1) // KC)
                if 2 <= z < NCH:
                    guards(z, z % 2, 0, z % KC)
                if 2 <= z < 5:
                    ratio(z - 2, z % 2, 0, 0)
                if 6 <= z < 22:
                    b, c = (z - 6) // 4, (z - 6) % 4
                    dve.wait_ge(s_gt, z - 5)
                    dve.wait_ge(s_u, z - 5)
                    if b >= 2:
                        dve.wait_ge(s_down, 4 * (b - 1))
                    v_.scalar_tensor_tensor(out=shT[:, b % 2, c, :], in0=gt1, scalar=0.5, in1=UPS[:, :],
                                            op0=ALU.mult, op1=ALU.mult).then_inc(s_h, 1)
                    if c == 0:
                        dve.wait_ge(s_lgtr, b + 1)
                        v_.tensor_copy(lg[:, 4 * b:4 * b + 4, :].rearrange("p t e -> p (t e)"),
                                       MPS[:, 0:4 * E]).then_inc(s_lg, 1)
                if z == 18:
                    route_1(dve, st, v_)
                    route_2(dve, st, v_)
                if z == 18:
                    v_.tensor_reduce(wsum[:], wstat[:, :, :], AX.X, ALU.add).then_inc(s_wsum, 1)
                if z == 19:
                    dve.wait_ge(s_wtot, 1)
                    v_.tensor_scalar(wq[:, :, 0:1], MPS[:, 384:386].rearrange("p (j o) -> p j o", o=1),
                                     1.0 / (FF * C), EPS, ALU.mult, ALU.max).then_inc(s_sq, 1)
                if z == 21:
                    w = lambda k: wq[:, :, k:k + 1]
                    def one(ins):
                        st.mark(ins)
                        st.settle()
                    dve.wait_ge(s_sq, 2)
                    one(v_.reciprocal(w(2), w(1)))
                    one(v_.tensor_tensor(out=w(3), in0=w(2), in1=w(2), op=ALU.mult))
                    one(v_.tensor_tensor(out=w(3), in0=w(3), in1=w(0), op=ALU.mult))
                    one(v_.tensor_scalar(w(3), w(3), -0.5, 1.5, ALU.mult, ALU.add))
                    one(v_.tensor_tensor(out=w(4), in0=w(3), in1=w(2), op=ALU.mult))
                    one(v_.reciprocal(w(5), w(4)))
                    v_.tensor_scalar(w(6), w(5), 1.0 / 127.0, None, ALU.mult).then_inc(s_rms, 1)
                for unit in units_in_a(z - 1):
                    w_out(unit)
                for unit in units_in_a(z):
                    tern(unit)

            dve.wait_ge(s_par[3], 16)

            def e_hidden(s, p):
                dve.wait_ge(s_gt, s + (NT + 1))
                dve.wait_ge(s_eu, s + 3)
                if not isinstance(s, int) or s >= 1:
                    dve.wait_ge(s_ehtr, s)
                v_.scalar_tensor_tensor(out=hE[p], in0=gt1, scalar=0.5, in1=UPS[:, :],
                                        op0=ALU.mult, op1=ALU.mult).then_inc(s_eh, 1)

            dve.wait_ge(s_zero, 16 * (NS + 1))
            dve.wait_ge(s_res, NT)
            gate_t(1, s_et, s_eh, 1)
            e_hidden(0, 0)
            for unit in units_in_a(STEPS_A - 1):
                w_out(unit)

            def e_step(s, p, chunk=None, scan=None, done=None, last=False, units=(), before=()):
                if not last:
                    gate_t(s + 2, s_et, s_eh, s + 2)
                if scan:
                    scans(*scan)
                if chunk:
                    guards(*chunk)
                for unit in before:
                    w_out(unit)
                for unit in units:
                    tern(unit)
                if not last:
                    e_hidden(s + 1, 1 - p)
                if done:
                    ratio(*done)

            for s in range(4):
                n = NCH + s
                e_step(s, s % 2, (n, s % 2, 1, s), (n - 1, (s - 1) % 2, 1, s - 1, 0) if s >= 1 else None,
                       (n - 2, s % 2, 1, 0) if s >= 2 else None,
                       units=[w2_unit(0, s)], before=[w2_unit(0, s - 1)] if s else ())
            with dve.Fori(1, 4) as i:
                st.enter(i, 4 * (2 + 5 + 1), 1)
                for c in range(KC):
                    n = i * KC + (NCH + c)
                    e_step(i * KC + c, c % 2, (n, c % 2, 1, c),
                           (i * KC + (NCH + c - 1), (c + 1) % 2, 1, (c + 3) % KC, i + (c + 3) // KC - 1),
                           (i * KC + (NCH + c - 2), c % 2, 1, i + (c + 2) // KC - 1),
                           units=[w2_unit(i, c)], before=[w2_unit(i, c - 1)])
                st.leave(3)
            for s in range(NT, NS):
                e_step(s, s % 2, None, (2 * NCH - 1, 1, 1, KC - 1, B - 1) if s == NT else None,
                       (NCH + s - 2, s % 2, 1, B - 1) if s <= NT + 1 else None, s == NS - 1,
                       units_late(s), [w2_unit(3, 3)] if s == NT else units_late(s - 1))

            def small(ins):
                st.mark(ins)
                st.settle()

            S = lambda a, j: sc[:, a, j:j + 1]

            def round_1(t, a):
                y = r1tok[:, bass.ds(t * C, C)]
                dve.wait_ge(s_y1, t + 1)
                small(v_.tensor_reduce(S(a, 0), y, AX.X, ALU.max, apply_absolute_value=True))
                small(v_.tensor_scalar(S(a, 0), S(a, 0), EPS, 1.0 / 127.0, ALU.max, ALU.mult))
                small(v_.reciprocal(S(a, 1), S(a, 0)))
                dve.wait_ge(s_gelu, t * 4)
                st.mark(v_.tensor_scalar(S(a, 4), S(a, 0), wq[:, 0, 5:6], None, ALU.mult))
                small(v_.tensor_scalar(y1, y, S(a, 1), MAGIC, ALU.mult, ALU.add))
                if not isinstance(t, int) or t >= 2:
                    dve.wait_ge(s_q1tr, t)
                v_.tensor_scalar(q1[:, a], y1, MAGIC, 127.0, ALU.subtract, ALU.min).then_inc(s_q1, 1)

            def largest(t, a):
                for h in range(2):
                    dve.wait_ge(s_gelu, t * 4 + (2 * h + 6))
                    st.mark(v_.tensor_reduce(S(a, 8 + h), gel[:, a, h * 1024:(h + 1) * 1024], AX.X, ALU.max,
                                             apply_absolute_value=True))
                st.settle()
                small(v_.tensor_tensor(out=S(a, 5), in0=S(a, 8), in1=S(a, 9), op=ALU.max))
                small(v_.tensor_scalar(S(a, 5), S(a, 5), EPS, 1.0 / 127.0, ALU.max, ALU.mult))
                st.mark(v_.tensor_scalar(rsc[:, bass.ds(t, 1)], S(a, 5), wq[:, 1, 5:6], None, ALU.mult))
                v_.reciprocal(S(a, 6), S(a, 5)).then_inc(s_amax, 1)

            def round_2(t, a):
                for h in range(2):
                    dve.wait_ge(s_rnd, t * 2 + (h + 1))
                    dve.wait_ge(s_q2tr, t + 1)
                    v_.tensor_scalar(q2[:, h * 1024:(h + 1) * 1024], gel[:, a, h * 1024:(h + 1) * 1024],
                                     MAGIC, 127.0, ALU.subtract, ALU.min).then_inc(s_q2, 1)

            def finish(t, a, k):
                dve.wait_ge(s_out, t + 2)
                dve.wait_ge(s_store[a], k * 16 + 16)
                v_.scalar_tensor_tensor(out=fin[:, a], in0=OPS[:, :], scalar=rsc[:, bass.ds(t, 1)],
                                        in1=resid[:, bass.ds(t * C, C)], op0=ALU.mult, op1=ALU.add
                                        ).then_inc(s_fin, 1)

            def q2T_half(t):
                dve.wait_ge(s_q2tr, t + 2)
                dve.wait_ge(s_out, t + 1)
                v_.tensor_copy(q2T[:, 8:16].rearrange("p g t -> p (g t)"), TPS[1]).then_inc(s_q2Tv, 1)

            dve.wait_ge(s_eo, NS + 1)
            def step_1(t, a, k=None):
                at = lambda m: not isinstance(t, int) or 0 <= t + m < NT
                if at(1):
                    largest(t + 1, 1 - a)
                if at(3):
                    round_1(t + 3, 1 - a)
                if at(-1):
                    finish(t - 1, 1 - a, k)
                if at(0):
                    q2T_half(t)
                if at(1):
                    round_2(t + 1, 1 - a)

            for t in range(2):
                r = r1tok[:, t * C:(t + 1) * C]
                dve.wait_ge(s_t1, t + 1)
                v_.scalar_tensor_tensor(out=r, in0=t1[:, t], scalar=1.0, in1=r, op0=ALU.add, op1=ALU.mult
                                        ).then_inc(s_y1, 1)
                round_1(t, t)
            step_1(-1, 1)
            step_1(0, 0)
            with dve.Fori(0, 5) as i:
                st.enter(i, 2 * (5 + 5))
                for a in range(2):
                    step_1(i * 2 + (a + 1), 1 - a, i)
                st.leave(5)
            for t in range(11, NT + 1):
                step_1(t, t % 2, (t - 1) // 2)


_INS = ['x', 'fside_BxSxS_0', 'cond_512', 'L0_cond_w', 'L0_cond_u', 'L0_ffn_router_w', 'L0_ffn_gate_w',
        'L0_ffn_up_w', 'L0_ffn_down_w', 'L0_ffn_shared_gate_w', 'L0_ffn_shared_up_w', 'L0_ffn_shared_down_w',
        'L1_cond_w', 'L1_cond_u', 'L1_ffn_w1', 'L1_ffn_w2']


def kernel(**inputs):
    import numpy as _np
    import concourse.bacc as _bacc
    from concourse import mybir as _mybir
    from concourse.bass_utils import run_bass_kernel_spmd as _run

    nc = _bacc.Bacc("TRN2", target_bir_lowering=False, num_devices=1)
    arrays, args = {}, []
    for name in _INS:
        a = _np.ascontiguousarray(inputs[name])
        arrays[f"in_{name}_dram"] = a
        args.append(nc.dram_tensor(f"in_{name}_dram", a.shape, _mybir.dt.from_np(a.dtype), kind="ExternalInput").ap())
    f32 = _mybir.dt.float32
    args.append(nc.dram_tensor("out_0_dram", inputs["x"].shape, f32, kind="ExternalOutput").ap())
    tokens, channels = inputs["x"].shape[0] * inputs["x"].shape[1], inputs["x"].shape[2]
    slots = tokens + 128 * inputs["L0_ffn_router_w"].shape[1]
    args.append(nc.dram_tensor("slot_rows", (slots, channels), f32, kind="Internal").ap())
    args.append(nc.dram_tensor("slot_out", (slots - 128, channels), f32, kind="Internal").ap())
    args.append(nc.dram_tensor("side_rows", inputs["x"].shape, f32, kind="Internal").ap())
    build(nc, *args)
    r = _run(nc, [arrays], core_ids=[0])
    return r.results[0]["out_0_dram"]
```
